# Optimizing a Trainium2 kernel written in Bass

```python
import numpy as np
import jax
import jax.numpy as jnp

def _softmax(x, axis=-1):
    return jax.nn.softmax(x, axis=axis)

def _gelu(x):
    return jax.nn.gelu(x, approximate=True)

def _silu(x):
    return jax.nn.silu(x)

def _sigmoid(x):
    return jax.nn.sigmoid(x)

def _layernorm(x, axis=-1, eps=1e-05):
    m = jnp.mean(x, axis=axis, keepdims=True)
    v = jnp.var(x, axis=axis, keepdims=True)
    return (x - m) / jnp.sqrt(v + eps)

def _scatter_add(tgt, idx, src, axis=0):
    return tgt.at[idx].add(src)

def _segment_sum(src, seg, n):
    return jax.ops.segment_sum(src, seg, n)
kernel_name = 'mk_gnn_resnorm_d4_gnn_r64_a3d272'

def setup_inputs(seed: int=0):
    np.random.seed(seed)
    _w = jnp.asarray

    def _rec_inputs():
        import jax
        import jax.numpy as jnp
        _gk = jax.random.key(seed)
        x = -0.0003713 + 1 * jax.random.normal(jax.random.fold_in(_gk, 1), (50000, 256), jnp.float32)
        src = jax.random.randint(jax.random.fold_in(_gk, 2), (25000,), 0, 50000, jnp.int32)
        dst = jnp.minimum((50000 * jax.random.uniform(jax.random.fold_in(_gk, 3), (25000,)) ** 2.0).astype(jnp.int32), 49999)
        _o = jnp.argsort(dst, stable=True)
        src = src[_o]
        dst = dst[_o]
        return (x, src, dst)
    x, src, dst = _rec_inputs()

    def _L0_gnn_setup():
        import jax, jax.numpy as jnp
        import numpy as np
        NUM_NODES = 50000
        NUM_EDGES = 20000
        NNZ = 12500
        DIM = 256

        def _layer(x, node_idx, edge_idx, norm_n2e, norm_e2n, W_n2e, W_e2n):
            h = x @ W_n2e
            msg = norm_n2e[:, None] * h[node_idx]
            e = jax.ops.segment_sum(msg, edge_idx, num_segments=NUM_EDGES)
            e = jax.nn.relu(e)
            h2 = e @ W_e2n
            msg2 = norm_e2n[:, None] * h2[edge_idx]
            n = jax.ops.segment_sum(msg2, node_idx, num_segments=NUM_NODES)
            return (n, e)
        key = jax.random.key(seed)
        ks = jax.random.split(key, 7)
        x = jax.random.normal(ks[0], (NUM_NODES, DIM), dtype=jnp.float32)
        node_idx = jax.random.randint(ks[1], (NNZ,), 0, NUM_NODES)
        edge_idx = jax.random.randint(ks[2], (NNZ,), 0, NUM_EDGES)
        hyperedge_index = jnp.stack([node_idx, edge_idx], axis=0)
        s = 1.0 / np.sqrt(DIM)
        W0_n2e = jax.random.uniform(ks[3], (DIM, DIM), jnp.float32, -s, s)
        W0_e2n = jax.random.uniform(ks[4], (DIM, DIM), jnp.float32, -s, s)
        W1_n2e = jax.random.uniform(ks[5], (DIM, DIM), jnp.float32, -s, s)
        W1_e2n = jax.random.uniform(ks[6], (DIM, DIM), jnp.float32, -s, s)
        return {'x': x, 'hyperedge_index': hyperedge_index, 'W0_n2e': W0_n2e, 'W0_e2n': W0_e2n, 'W1_n2e': W1_n2e, 'W1_e2n': W1_e2n}
    _L0_gnn_all = _L0_gnn_setup()
    _L0_gnn_in = {k: v for k, v in _L0_gnn_all.items() if k in ('W0_n2e', 'W0_e2n', 'W1_n2e', 'W1_e2n')}
    del _L0_gnn_all

    def _L1_gnn_setup():
        import jax, jax.numpy as jnp
        import numpy as np
        N = 50000
        E = 12500
        IN_C = 256
        HID = 64
        HEADS = 4
        NEG_SLOPE = 0.2

        def _gat_conv(x, W, att_src, att_dst, b, src, dst):
            n = x.shape[0]
            h = (x @ W).reshape(n, HEADS, HID)
            a_s = jnp.einsum('nhc,hc->nh', h, att_src)
            a_d = jnp.einsum('nhc,hc->nh', h, att_dst)
            e = jax.nn.leaky_relu(a_s[src] + a_d[dst], NEG_SLOPE)
            m = jax.ops.segment_max(e, dst, num_segments=n)
            ex = jnp.exp(e - m[dst])
            denom = jax.ops.segment_sum(ex, dst, num_segments=n)
            alpha = ex / denom[dst]
            msg = h[src] * alpha[:, :, None]
            out = jax.ops.segment_sum(msg, dst, num_segments=n)
            return out.reshape(n, HEADS * HID) + b
        key = jax.random.key(seed)
        ks = jax.random.split(key, 12)
        x = jax.random.normal(ks[0], (N, IN_C), dtype=jnp.float32)
        edge_index = jax.random.randint(ks[1], (2, E), 0, N, dtype=jnp.int64)
        s1 = 1.0 / np.sqrt(IN_C)
        W1 = jax.random.normal(ks[2], (IN_C, HEADS * HID), dtype=jnp.float32) * s1
        att_src1 = jax.random.normal(ks[3], (HEADS, HID), dtype=jnp.float32) * 0.1
        att_dst1 = jax.random.normal(ks[4], (HEADS, HID), dtype=jnp.float32) * 0.1
        b1 = jnp.zeros((HEADS * HID,), dtype=jnp.float32)
        s2 = 1.0 / np.sqrt(HEADS * HID)
        W2 = jax.random.normal(ks[5], (HEADS * HID, HEADS * HID), dtype=jnp.float32) * s2
        att_src2 = jax.random.normal(ks[6], (HEADS, HID), dtype=jnp.float32) * 0.1
        att_dst2 = jax.random.normal(ks[7], (HEADS, HID), dtype=jnp.float32) * 0.1
        b2 = jnp.zeros((HEADS * HID,), dtype=jnp.float32)
        return {'x': x, 'edge_index': edge_index, 'W1': W1, 'att_src1': att_src1, 'att_dst1': att_dst1, 'b1': b1, 'W2': W2, 'att_src2': att_src2, 'att_dst2': att_dst2, 'b2': b2}
    _L1_gnn_all = _L1_gnn_setup()
    _L1_gnn_in = {k: v for k, v in _L1_gnn_all.items() if k in ('W1', 'att_src1', 'att_dst1', 'b1', 'W2', 'att_src2', 'att_dst2', 'b2')}
    del _L1_gnn_all

    def _L2_gnn_setup():
        import jax, jax.numpy as jnp
        import numpy as np
        N_NODES = 50000
        N_EDGES = 12500
        D_IN = 256
        D_OUT = 256
        BN_EPS = 1e-05
        key = jax.random.key(seed)
        k1, k2, k3, k4 = jax.random.split(key, 4)
        x = jax.random.normal(k1, (N_NODES, D_IN), dtype=jnp.float32)
        edge_index = jax.random.randint(k2, (2, N_EDGES), 0, N_NODES, dtype=jnp.int64)
        W = jax.random.normal(k3, (D_OUT, D_IN), dtype=jnp.float32) / np.sqrt(D_IN)
        b = jnp.zeros((D_OUT,), dtype=jnp.float32)
        gamma = jnp.ones((D_OUT,), dtype=jnp.float32)
        beta = jnp.zeros((D_OUT,), dtype=jnp.float32)
        return {'x': x, 'edge_index': edge_index, 'W': W, 'b': b, 'gamma': gamma, 'beta': beta}
    _L2_gnn_all = _L2_gnn_setup()
    _L2_gnn_in = {k: v for k, v in _L2_gnn_all.items() if k in ('W', 'b', 'gamma', 'beta')}
    del _L2_gnn_all

    def _L3_gnn_setup():
        import jax, jax.numpy as jnp
        import numpy as np
        N = 20000
        E = 5000
        D_IN = 256
        HID = 64
        HEADS = 4
        D_OUT = 256
        EPS = 1e-05
        SLOPE = 0.2

        def _gat(x, src, dst, W, a_src, a_dst, b, heads, ch, concat):
            n = x.shape[0]
            h = (x @ W).reshape(n, heads, ch)
            es = (h * a_src).sum(-1)
            ed = (h * a_dst).sum(-1)
            e = jax.nn.leaky_relu(es[src] + ed[dst], SLOPE)
            m = jax.ops.segment_max(e, dst, num_segments=n)
            w = jnp.exp(e - m[dst])
            den = jax.ops.segment_sum(w, dst, num_segments=n)
            alpha = w / den[dst]
            msg = h[src] * alpha[:, :, None]
            out = jax.ops.segment_sum(msg, dst, num_segments=n)
            out = out.reshape(n, heads * ch) if concat else out.mean(axis=1)
            return out + b

        def _layernorm(x, g, b):
            mu = x.mean(-1, keepdims=True)
            v = ((x - mu) ** 2).mean(-1, keepdims=True)
            return (x - mu) * jax.lax.rsqrt(v + EPS) * g + b
        key = jax.random.key(seed)
        ks = jax.random.split(key, 10)

        def glorot(k, shape):
            fan_in, fan_out = (shape[0], int(np.prod(shape[1:])))
            s = np.sqrt(2.0 / (fan_in + fan_out)).astype(np.float32)
            return jax.random.normal(k, shape, dtype=jnp.float32) * s
        x = jax.random.normal(ks[0], (N, D_IN), dtype=jnp.float32)
        edge_index = jax.random.randint(ks[1], (2, E), 0, N, dtype=jnp.int64)
        return {'x': x, 'edge_index': edge_index, 'W1': glorot(ks[2], (D_IN, HEADS * HID)), 'a1_src': glorot(ks[3], (HEADS, HID)), 'a1_dst': glorot(ks[4], (HEADS, HID)), 'b1': jnp.zeros((HEADS * HID,), jnp.float32), 'ln_g': jnp.ones((HEADS * HID,), jnp.float32), 'ln_b': jnp.zeros((HEADS * HID,), jnp.float32), 'W2': glorot(ks[5], (HEADS * HID, D_OUT)), 'a2_src': glorot(ks[6], (1, D_OUT)), 'a2_dst': glorot(ks[7], (1, D_OUT)), 'b2': jnp.zeros((D_OUT,), jnp.float32)}
    _L3_gnn_all = _L3_gnn_setup()
    _L3_gnn_in = {k: v for k, v in _L3_gnn_all.items() if k in ('W1', 'a1_src', 'a1_dst', 'b1', 'ln_g', 'ln_b', 'W2', 'a2_src', 'a2_dst', 'b2')}
    del _L3_gnn_all
    return {'x': x, 'src': src, 'dst': dst, 'L0_gnn_W0_n2e': _L0_gnn_in['W0_n2e'], 'L0_gnn_W0_e2n': _L0_gnn_in['W0_e2n'], 'L0_gnn_W1_n2e': _L0_gnn_in['W1_n2e'], 'L0_gnn_W1_e2n': _L0_gnn_in['W1_e2n'], 'L1_gnn_W1': _L1_gnn_in['W1'], 'L1_gnn_att_src1': _L1_gnn_in['att_src1'], 'L1_gnn_att_dst1': _L1_gnn_in['att_dst1'], 'L1_gnn_b1': _L1_gnn_in['b1'], 'L1_gnn_W2': _L1_gnn_in['W2'], 'L1_gnn_att_src2': _L1_gnn_in['att_src2'], 'L1_gnn_att_dst2': _L1_gnn_in['att_dst2'], 'L1_gnn_b2': _L1_gnn_in['b2'], 'L2_gnn_W': _L2_gnn_in['W'], 'L2_gnn_b': _L2_gnn_in['b'], 'L2_gnn_gamma': _L2_gnn_in['gamma'], 'L2_gnn_beta': _L2_gnn_in['beta'], 'L3_gnn_W1': _L3_gnn_in['W1'], 'L3_gnn_a1_src': _L3_gnn_in['a1_src'], 'L3_gnn_a1_dst': _L3_gnn_in['a1_dst'], 'L3_gnn_b1': _L3_gnn_in['b1'], 'L3_gnn_ln_g': _L3_gnn_in['ln_g'], 'L3_gnn_ln_b': _L3_gnn_in['ln_b'], 'L3_gnn_W2': _L3_gnn_in['W2'], 'L3_gnn_a2_src': _L3_gnn_in['a2_src'], 'L3_gnn_a2_dst': _L3_gnn_in['a2_dst'], 'L3_gnn_b2': _L3_gnn_in['b2']}

def reference(x, src, dst, L0_gnn_W0_n2e, L0_gnn_W0_e2n, L0_gnn_W1_n2e, L0_gnn_W1_e2n, L1_gnn_W1, L1_gnn_att_src1, L1_gnn_att_dst1, L1_gnn_b1, L1_gnn_W2, L1_gnn_att_src2, L1_gnn_att_dst2, L1_gnn_b2, L2_gnn_W, L2_gnn_b, L2_gnn_gamma, L2_gnn_beta, L3_gnn_W1, L3_gnn_a1_src, L3_gnn_a1_dst, L3_gnn_b1, L3_gnn_ln_g, L3_gnn_ln_b, L3_gnn_W2, L3_gnn_a2_src, L3_gnn_a2_dst, L3_gnn_b2):
    import jax
    import jax.numpy as jnp

    def _L0_gnn_ref(x, hyperedge_index, W0_n2e, W0_e2n, W1_n2e, W1_e2n):
        import jax, jax.numpy as jnp
        import numpy as np
        NUM_NODES = 50000
        NUM_EDGES = 20000
        NNZ = 12500
        DIM = 256

        def _layer(x, node_idx, edge_idx, norm_n2e, norm_e2n, W_n2e, W_e2n):
            h = x @ W_n2e
            msg = norm_n2e[:, None] * h[node_idx]
            e = jax.ops.segment_sum(msg, edge_idx, num_segments=NUM_EDGES)
            e = jax.nn.relu(e)
            h2 = e @ W_e2n
            msg2 = norm_e2n[:, None] * h2[edge_idx]
            n = jax.ops.segment_sum(msg2, node_idx, num_segments=NUM_NODES)
            return (n, e)
        node_idx, edge_idx = (hyperedge_index[0], hyperedge_index[1])
        ones = jnp.ones((node_idx.shape[0],), dtype=x.dtype)
        Dn = jax.ops.segment_sum(ones, node_idx, num_segments=NUM_NODES)
        De = jax.ops.segment_sum(ones, edge_idx, num_segments=NUM_EDGES)
        Dn_inv = jnp.where(Dn > 0, 1.0 / Dn, 0.0)
        De_inv = jnp.where(De > 0, 1.0 / De, 0.0)
        norm_n2e = De_inv[edge_idx]
        norm_e2n = Dn_inv[node_idx]
        x1, _ = _layer(x, node_idx, edge_idx, norm_n2e, norm_e2n, W0_n2e, W0_e2n)
        x1 = jax.nn.relu(x1)
        x2, _ = _layer(x1, node_idx, edge_idx, norm_n2e, norm_e2n, W1_n2e, W1_e2n)
        return x2

    def _L1_gnn_ref(x, edge_index, W1, att_src1, att_dst1, b1, W2, att_src2, att_dst2, b2):
        import jax, jax.numpy as jnp
        import numpy as np
        N = 50000
        E = 12500
        IN_C = 256
        HID = 64
        HEADS = 4
        NEG_SLOPE = 0.2

        def _gat_conv(x, W, att_src, att_dst, b, src, dst):
            n = x.shape[0]
            h = (x @ W).reshape(n, HEADS, HID)
            a_s = jnp.einsum('nhc,hc->nh', h, att_src)
            a_d = jnp.einsum('nhc,hc->nh', h, att_dst)
            e = jax.nn.leaky_relu(a_s[src] + a_d[dst], NEG_SLOPE)
            m = jax.ops.segment_max(e, dst, num_segments=n)
            ex = jnp.exp(e - m[dst])
            denom = jax.ops.segment_sum(ex, dst, num_segments=n)
            alpha = ex / denom[dst]
            msg = h[src] * alpha[:, :, None]
            out = jax.ops.segment_sum(msg, dst, num_segments=n)
            return out.reshape(n, HEADS * HID) + b
        loop = jnp.arange(N, dtype=edge_index.dtype)
        src = jnp.concatenate([edge_index[0], loop])
        dst = jnp.concatenate([edge_index[1], loop])
        h = _gat_conv(x, W1, att_src1, att_dst1, b1, src, dst)
        h = jax.nn.elu(h)
        h = _gat_conv(h, W2, att_src2, att_dst2, b2, src, dst)
        h = jax.nn.elu(h)
        return h

    def _L2_gnn_ref(x, edge_index, W, b, gamma, beta):
        import jax, jax.numpy as jnp
        import numpy as np
        N_NODES = 50000
        N_EDGES = 12500
        D_IN = 256
        D_OUT = 256
        BN_EPS = 1e-05
        n = x.shape[0]
        loop = jnp.arange(n, dtype=edge_index.dtype)
        src = jnp.concatenate([edge_index[0], loop])
        dst = jnp.concatenate([edge_index[1], loop])
        ones = jnp.ones(src.shape[0], dtype=x.dtype)
        deg = jax.ops.segment_sum(ones, dst, num_segments=n)
        dinv = jnp.where(deg > 0, jax.lax.rsqrt(deg), 0.0)
        norm = dinv[src] * dinv[dst]
        h = x @ W.T
        msgs = h[src] * norm[:, None]
        agg = jax.ops.segment_sum(msgs, dst, num_segments=n) + b
        mean = jnp.mean(agg, axis=0)
        var = jnp.var(agg, axis=0)
        y = (agg - mean) * jax.lax.rsqrt(var + BN_EPS) * gamma + beta
        return jax.nn.relu(y)

    def _L3_gnn_ref(x, edge_index, W1, a1_src, a1_dst, b1, ln_g, ln_b, W2, a2_src, a2_dst, b2):
        import jax, jax.numpy as jnp
        import numpy as np
        N = 20000
        E = 5000
        D_IN = 256
        HID = 64
        HEADS = 4
        D_OUT = 256
        EPS = 1e-05
        SLOPE = 0.2

        def _gat(x, src, dst, W, a_src, a_dst, b, heads, ch, concat):
            n = x.shape[0]
            h = (x @ W).reshape(n, heads, ch)
            es = (h * a_src).sum(-1)
            ed = (h * a_dst).sum(-1)
            e = jax.nn.leaky_relu(es[src] + ed[dst], SLOPE)
            m = jax.ops.segment_max(e, dst, num_segments=n)
            w = jnp.exp(e - m[dst])
            den = jax.ops.segment_sum(w, dst, num_segments=n)
            alpha = w / den[dst]
            msg = h[src] * alpha[:, :, None]
            out = jax.ops.segment_sum(msg, dst, num_segments=n)
            out = out.reshape(n, heads * ch) if concat else out.mean(axis=1)
            return out + b

        def _layernorm(x, g, b):
            mu = x.mean(-1, keepdims=True)
            v = ((x - mu) ** 2).mean(-1, keepdims=True)
            return (x - mu) * jax.lax.rsqrt(v + EPS) * g + b
        loops = jnp.arange(N, dtype=edge_index.dtype)
        src = jnp.concatenate([edge_index[0], loops])
        dst = jnp.concatenate([edge_index[1], loops])
        h = _gat(x, src, dst, W1, a1_src, a1_dst, b1, HEADS, HID, True)
        h = jax.nn.relu(_layernorm(h, ln_g, ln_b))
        out = _gat(h, src, dst, W2, a2_src, a2_dst, b2, 1, D_OUT, False)
        return out
    edge_index = jnp.stack([src, dst])
    x = _layernorm(x + _L0_gnn_ref(x, edge_index, L0_gnn_W0_n2e, L0_gnn_W0_e2n, L0_gnn_W1_n2e, L0_gnn_W1_e2n), axis=-1)
    x = _layernorm(x + _L1_gnn_ref(x, edge_index, L1_gnn_W1, L1_gnn_att_src1, L1_gnn_att_dst1, L1_gnn_b1, L1_gnn_W2, L1_gnn_att_src2, L1_gnn_att_dst2, L1_gnn_b2), axis=-1)
    x = _layernorm(x + _L2_gnn_ref(x, edge_index, L2_gnn_W, L2_gnn_b, L2_gnn_gamma, L2_gnn_beta), axis=-1)
    x = _layernorm(x + _L3_gnn_ref(x, edge_index, L3_gnn_W1, L3_gnn_a1_src, L3_gnn_a1_dst, L3_gnn_b1, L3_gnn_ln_g, L3_gnn_ln_b, L3_gnn_W2, L3_gnn_a2_src, L3_gnn_a2_dst, L3_gnn_b2), axis=-1)
    return x

_drawn_inputs = setup_inputs


def setup_inputs(seed=0):
    import zlib

    import numpy as np

    out = dict(_drawn_inputs(seed))
    spreads = {'L1_gnn_b1': (0.0, 0.1),
     'L1_gnn_b2': (0.0, 0.1),
     'L2_gnn_b': (0.0, 0.8),
     'L2_gnn_gamma': (1.0, 0.2),
     'L2_gnn_beta': (0.0, 0.1),
     'L3_gnn_b1': (0.0, 0.1),
     'L3_gnn_ln_g': (1.0, 0.2),
     'L3_gnn_ln_b': (0.0, 0.1),
     'L3_gnn_b2': (0.0, 0.1)}
    factors = {'L0_gnn_W0_n2e': 4.153,
     'L0_gnn_W0_e2n': 2.987,
     'L1_gnn_att_dst1': 4.24,
     'L1_gnn_att_dst2': 7.09,
     'L3_gnn_a1_dst': 3.213,
     'L3_gnn_a2_dst': 3.425}
    for name, (base, spread) in spreads.items():
        noise = np.random.default_rng([zlib.crc32(name.encode()), seed]).standard_normal(out[name].shape)
        drawn = base * np.exp(spread * noise) if base else spread * noise
        out[name] = jnp.asarray(drawn.astype(out[name].dtype))
    for name, factor in factors.items():
        out[name] = (out[name] * factor).astype(out[name].dtype)
    return out
```

```python
from contextlib import ExitStack

import concourse.bass as bass
from concourse import mybir

F32 = mybir.dt.float32
I32 = mybir.dt.int32
ALU = mybir.AluOpType
ACT = mybir.ActivationFunctionType
AX_X = mybir.AxisListType.X

P = 128
N = 50000
E = 25000
D = 256
KC = D // P
J = 4
BLK = P * J
NB = -(-N // BLK)
NB += NB % 2
NPAD = NB * BLK
TAILP = (N - (NB - 1) * BLK) // J
NHYP = 20000
HB = NHYP // BLK + 1
HB += HB % 2
C = -(-E // P)
LASTRUN = E - (P - 1) * C
BC = 14
NBAT = C // BC
RW = 264
SW = 260
NONE = 60000
BIG = 1e30
EPS = 1e-5
SLOPE = 0.2
assert C == BC * NBAT and NBAT % 2 == 0 and TAILP * J + (NB - 1) * BLK == N


class Step:

    def __init__(self, n, half=None, par=None):
        self.n = n
        self.half = n // 2 if half is None else half
        self.par = n % 2 if par is None else par
        self.fixed = half is None

    def back(self, k):
        if self.fixed:
            return Step(self.n - k)
        return Step(self.n - k, self.half - (k - self.par + 1) // 2, (self.par - k) % 2)

    def before(self, k):
        return self.fixed and self.n < k


def over_blocks(eng, step, blocks, peel=0, tail=0):
    for n in range(2 * peel):
        step(Step(n))
    with eng.Fori(peel, blocks // 2 - tail) as i:
        step(Step(i * 2, i, 0))
        step(Step(i * 2 + 1, i, 1))
    for n in range(blocks - 2 * tail, blocks):
        step(Step(n))


def hold(eng, passed, sem, value):
    eng.wait_ge(sem, value)
    if not isinstance(value, int):
        eng.sem_inc(passed, 1)


def spread(ap, k):
    return ap.unsqueeze(len(ap.shape)).to_broadcast([*ap.shape, k])


class Scope:

    def __init__(self, nc, tag):
        self.nc, self.tag, self.ctx, self.used = nc, tag, ExitStack(), []

    def __enter__(self):
        return self

    def __exit__(self, *a):
        with self.nc.Block() as block:

            @block.sync
            def _(sp):
                for sem in self.used:
                    sp.sem_clear(sem)

        self.ctx.__exit__(*a)

    def sb(self, name, shape, dt=F32):
        return self.ctx.enter_context(self.nc.sbuf_tensor(f"{self.tag}_{name}", shape, dt))

    def ps(self, name, shape, dt=F32):
        return self.ctx.enter_context(self.nc.psum_tensor(f"{self.tag}_{name}", shape, dt))

    def sem(self, name):
        self.used.append(self.ctx.enter_context(self.nc.semaphore(f"{self.tag}_{name}")))
        return self.used[-1]

    def pool_sem(self, S, name):
        return S["scope"].ctx.enter_context(self.nc.semaphore(f"{self.tag}_{name}"))

    def sems(self, name):
        return [self.sem(f"{name}{b}") for b in range(2)]

    def block(self):
        return self.nc.Block()


def setup_phase(nc, S, A, T):
    with Scope(nc, "su") as s:
        dnext32 = s.sb("dnext32", [P, C], I32)
        skey32 = s.sb("skey32", [P, C], I32)
        df = s.sb("df", [P, C])
        dnextf = s.sb("dnextf", [P, C])
        t1 = s.sb("t1", [P, C])
        head = s.sb("head", [P, C])
        cnt = s.sb("cnt", [P, C])
        ones_c = s.sb("ones_c", [P, C])
        pos = s.sb("pos", [P, C], I32)
        hpos = s.sb("hpos", [P, 1], I32)
        midx = s.sb("midx", [P, C], I32)
        meta = s.sb("meta", [P, C, 2], I32)
        empty = s.sb("empty", [P, NPAD // P, 2], I32)
        diag = s.sb("diag", [P, 2, P])
        small = s.sb("small", [P, 8])
        att = s.sb("att", [P, 6, D])
        prod = s.sb("prod", [P, D])
        wraw = s.sb("wraw", [P, KC, D])
        nodeid = s.sb("nodeid", [P, NB * J], I32)
        msb = s.sb("msb", [P, NB, J * 2], I32)
        kb = s.ps("kb", [P, 2, P])
        carry = s.ps("carry", [P, 1])
        wt = s.ps("wt", [P, KC, 2, P])
        s_fill = s.sem("filled")
        s_ld = s.sem("edges_loaded")
        s_w = s.sem("weights_loaded")
        s_iota = s.sem("iotas")
        s_id = s.sem("identity")
        s_diag = s.sem("diagonals")
        s_kb = s.sem("keys_spread")
        s_m = s.sem("join_ready")
        s_car = s.sem("count_carried")
        s_meta = s.sem("meta_ready")
        s_emp = s.sem("empty_ready")
        s_pre = s.sem("meta_prefilled")
        s_sc = s.pool_sem(S, "meta_scattered")
        s_mld = s.sem("meta_loaded")
        s_wt = s.sem("w_transposed")
        s_cn = s.sem("counts_ready")
        s_zero = s.sem("zero_rows_ready")
        s_zs = s.sem("sums_zeroed")
        s_wld = s.sem("wraw_loaded")
        zero = s.sb("zero", [P, 8, SW])
        with s.block() as block:

            @block.sync
            def _(sp):
                sp.wait_ge(s_fill, 1)
                src, dst = A["src"], A["dst"]
                full = (P - 1) * C
                for tile, ap, off in ((S["src32"], src, 0), (skey32, src, 0), (S["dst32"], dst, 0), (dnext32, dst, 1)):
                    sp.dma_start(tile[0:P - 1, :], ap[off:off + full].rearrange("(p c) -> p c", c=C)).then_inc(s_ld, 16)
                    sp.dma_start(tile[P - 1:P, 0:LASTRUN - off],
                                 ap[off + full:E].rearrange("(p c) -> p c", p=1)).then_inc(s_ld, 16)
                sp.wait_ge(s_emp, 1)
                sp.dma_start(T["META"].rearrange("(p r) c -> p (r c)", p=P), empty[:].rearrange("p r c -> p (r c)")).then_inc(s_pre, 16)
                for k, (name, ap) in enumerate(S["weights"].items()):
                    sp.dma_start(S["w_" + name][:, :, 0:D], ap.rearrange("(k p) n -> p k n", p=P)).then_inc(s_w, 16)
                sp.dma_start(wraw[:], A["L2_gnn_W"].rearrange("(k p) n -> p k n", p=P)).then_inc(s_wld, 16)
                for k, name in enumerate(ATT):
                    sp.dma_start(att[:, k, :], A[name].rearrange("h c -> (h c)").partition_broadcast(P)).then_inc(s_w, 16)
                for name in ROWS:
                    sp.dma_start(S["r_" + name][:], A[name].partition_broadcast(P)).then_inc(s_w, 16)
                for name in COLS:
                    sp.dma_start(S["c_" + name][:], A[name].rearrange("(k p) -> p k", p=P),
                                 allow_slow_non_contiguous=True).then_inc(s_w, 16)
                sp.wait_ge(s_zero, 1)
                for t in ("NS0", "NS1"):
                    rows = T[t].shape[0] // P
                    v = T[t].rearrange("(p r) c -> p r c", p=P)
                    for r in range(0, rows, 8):
                        k = min(8, rows - r)
                        sp.dma_start(v[:, r:r + k, :], zero[:, 0:k, :]).then_inc(s_zs, 16)
                sp.wait_ge(s_sc, 16 * C)
                sp.dma_start(msb[:], T["META"].rearrange("(n p j) c -> p n (j c)", p=P, j=J)).then_inc(s_mld, 16)
                sp.wait_ge(s_mld, 16)
                sp.wait_ge(s_zs, 16 * 2 * -(-(T["NS0"].shape[0] // P) // 8))

            @block.gpsimd
            def _(pool):
                pool.iota(pos[:], [[1, C]], base=0, channel_multiplier=C).then_inc(s_iota, 1)
                pool.iota(hpos[:], [[1, 1]], base=-1, channel_multiplier=C).then_inc(s_iota, 1)
                pool.iota(S["dummy32"][:], [[1, 1]], base=NPAD, channel_multiplier=1).then_inc(s_iota, 1)
                pool.iota(nodeid[:], [[BLK, NB], [1, J]], base=0, channel_multiplier=J).then_inc(s_iota, 1)
                pool.memset(S["ones"][:], 1.0)
                pool.memset(S["minus_half"][:], -0.5)
                pool.memset(zero[:], 0.0).then_inc(s_zero, 1)
                pool.drain()
                pool.affine_select(out=S["ident"][:], in_=S["ones"][:], compare_op=ALU.is_equal, fill=0.0, base=0,
                                   pattern=[[1, P]], channel_multiplier=-1)
                pool.affine_select(out=S["upper"][:], in_=S["ones"][:], compare_op=ALU.is_gt, fill=0.0, base=0,
                                   pattern=[[1, P]], channel_multiplier=-1)
                pool.affine_select(out=S["lower"][:], in_=S["ones"][:], compare_op=ALU.is_gt, fill=0.0, base=0,
                                   pattern=[[-1, P]], channel_multiplier=1).then_inc(s_id, 1)
                pool.wait_ge(s_meta, 1)
                pool.wait_ge(s_pre, 16)
                for c in range(C):
                    pool.indirect_dma_start(out=T["META"], out_offset=bass.IndirectOffsetOnAxis(ap=midx[:, c:c + 1], axis=0),
                                            in_=meta[:, c, :], in_offset=None, bounds_check=N - 1,
                                            oob_is_err=False).then_inc(s_sc, 16)
                pool.wait_ge(s_cn, 1)
                for k in range(0, NB * J, J * 14):
                    pool.tensor_tensor(S["dinv"][:, k:k + J * 14], S["deg"][:, k:k + J * 14],
                                       S["minus_half"][:, 0:J * 14], ALU.pow)

            @block.tensor
            def _(pe):
                pe.wait_ge(s_id, 1)
                pe.wait_ge(s_diag, 1)
                for k in range(2):
                    last = pe.matmul(kb[:, k, :], S["ones"][:, :], diag[:, k, :], start=True, stop=True)
                last.then_inc(s_kb, 1)
                pe.wait_ge(s_wld, 16)
                for k in range(KC):
                    for m in range(KC):
                        last = pe.transpose(wt[:, k, m, :], wraw[:, m, k * P:(k + 1) * P], S["ident"][:])
                last.then_inc(s_wt, 1)
                pe.wait_ge(s_m, 1)
                pe.matmul(carry[:], S["join"][:], cnt[:, C - 1:C], start=True, stop=True).then_inc(s_car, 1)

            @block.vector
            def _(dve):
                dve.memset(S["src32"][:], 0)
                dve.memset(skey32[:], N)
                dve.memset(S["dst32"][:], NONE)
                dve.memset(dnext32[:], NONE)
                dve.drain().then_inc(s_fill, 1)
                dve.memset(empty[:, :, 0:1], NONE)
                dve.memset(empty[:, :, 1:2], 0)
                dve.memset(ones_c[:], 1.0)
                dve.drain().then_inc(s_emp, 1)
                dve.wait_ge(s_ld, 16 * 8)
                dve.wait_ge(s_iota, 4)
                dve.tensor_copy(df[:], S["dst32"][:])
                dve.tensor_copy(dnextf[:], dnext32[:])
                dve.tensor_copy(S["skey"][:], skey32[:])
                dve.tensor_copy(S["dummy"][:], S["dummy32"][:])
                dve.memset(S["same"][:, 0:1], 0.0)
                dve.drain()
                dve.tensor_tensor(S["same"][:, 1:C], df[:, 1:C], df[:, 0:C - 1], ALU.is_equal)
                dve.tensor_scalar(head[:], df[:], df[:, 0:1], None, ALU.is_equal)
                dve.tensor_scalar(t1[:], df[:], float(NHYP - 1), None, ALU.min)
                dve.drain()
                dve.tensor_copy(S["hyp32"][:], t1[:])
                dve.tensor_scalar(S["cut"][:], S["same"][:], BIG, -BIG, ALU.mult, ALU.add)
                dve.tensor_tensor_scan(cnt[:], S["same"][:], ones_c[:], 0.0, ALU.mult, ALU.add)
                dve.tensor_reduce(small[:, 0:1], head[:], AX_X, ALU.add)
                dve.wait_ge(s_id, 1)
                dve.tensor_scalar(diag[:, 0, :], S["ident"][:], df[:, 0:1], None, ALU.mult)
                dve.tensor_scalar(diag[:, 1, :], S["ident"][:], df[:, C - 1:C], None, ALU.mult)
                dve.drain().then_inc(s_diag, 1)
                dve.wait_ge(s_kb, 1)
                dve.scalar_tensor_tensor(S["join"][:], kb[:, 0, :], df[:, C - 1:C], S["upper"][:], ALU.is_equal, ALU.mult)
                dve.scalar_tensor_tensor(S["joinT"][:], kb[:, 1, :], df[:, 0:1], S["lower"][:], ALU.is_equal, ALU.mult)
                dve.drain().then_inc(s_m, 1)
                dve.tensor_scalar(S["joincut"][:], S["joinT"][:], BIG, -BIG, ALU.mult, ALU.add)
                dve.wait_ge(s_car, 1)
                dve.tensor_copy(small[:, 1:2], carry[:])
                dve.tensor_copy(small[:, 2:3], hpos[:])
                dve.drain()
                dve.scalar_tensor_tensor(t1[:], head[:], small[:, 1:2], cnt[:], ALU.mult, ALU.add)
                dve.tensor_scalar(small[:, 3:4], small[:, 1:2], 0.0, None, ALU.is_gt)
                dve.tensor_tensor(small[:, 4:5], small[:, 0:1], small[:, 2:3], ALU.add)
                dve.tensor_copy(meta[:, :, 0:1].rearrange("p c o -> p (c o)"), pos[:])
                dve.drain()
                dve.tensor_scalar(small[:, 5:6], small[:, 4:5], float(-NONE), None, ALU.add)
                dve.tensor_copy(meta[:, :, 1:2].rearrange("p c o -> p (c o)").bitcast(F32), t1[:])
                dve.tensor_tensor(head[:], dnextf[:], df[:], ALU.not_equal)
                dve.tensor_scalar(cnt[:], df[:], float(-NONE), None, ALU.add)
                dve.drain()
                dve.tensor_tensor(small[:, 6:7], small[:, 5:6], small[:, 3:4], ALU.mult)
                dve.tensor_tensor(cnt[:], cnt[:], head[:], ALU.mult)
                dve.drain()
                dve.tensor_scalar(small[:, 7:8], small[:, 6:7], float(NONE), None, ALU.add)
                dve.tensor_scalar(cnt[:], cnt[:], float(NONE), None, ALU.add)
                dve.drain()
                dve.tensor_copy(S["repair32"][:], small[:, 7:8])
                dve.tensor_copy(midx[:], cnt[:])
                dve.drain().then_inc(s_meta, 1)
                dve.wait_ge(s_w, 16 * (len(S["weights"]) + len(ATT) + len(ROWS) + len(COLS)))
                for w, heads, a in (("L1a", 4, 0), ("L1b", 4, 2), ("L3a", 4, 4)):
                    for k in range(KC):
                        for v in range(2):
                            dve.tensor_tensor(prod[:], S["w_" + w][:, k, 0:D], att[:, a + v, :], ALU.mult)
                            dve.drain()
                            dve.tensor_reduce(S["w_" + w][:, k, D + v * heads:D + (v + 1) * heads],
                                              prod[:].rearrange("p (h c) -> p h c", h=heads), AX_X, ALU.add)
                            dve.drain()
                dve.wait_ge(s_wt, 1)
                dve.tensor_copy(S["w_L2"][:].rearrange("p k (m n) -> p k m n", m=KC), wt[:])
                dve.wait_ge(s_mld, 16)
                mv = msb[:].rearrange("p n (j c) -> p n j c", c=2)
                dve.tensor_copy(S["last32"][:].rearrange("p (n j) -> p n j", j=J), mv[:, :, :, 0])
                dve.tensor_scalar(S["deg"][:].rearrange("p (n j) -> p n j", j=J), mv[:, :, :, 1].bitcast(F32), 1.0, None, ALU.add)
                dve.tensor_scalar(S["einv"][:].rearrange("p (n j) -> p n j", j=J),
                                  mv[:, 0:HB, :, 1].bitcast(F32), 1.0, None, ALU.max)
                dve.tensor_copy(S["loop"][:], nodeid[:])
                dve.drain().then_inc(s_cn, 1)
                dve.reciprocal(S["einv"][:], S["einv"][:])
                dve.tensor_scalar(S["loop"][:], S["loop"][:], float(NHYP), None, ALU.is_lt)
                dve.drain()
                dve.tensor_scalar(S["loopcut"][:], S["loop"][:], BIG, -BIG, ALU.mult, ALU.add)


ATT = ("L1_gnn_att_src1", "L1_gnn_att_dst1", "L1_gnn_att_src2", "L1_gnn_att_dst2", "L3_gnn_a1_src", "L3_gnn_a1_dst")
ATT1 = ("L3_gnn_a2_src", "L3_gnn_a2_dst")
ROWS = ("L1_gnn_b1", "L1_gnn_b2", "L3_gnn_b1", "L3_gnn_ln_g", "L3_gnn_ln_b", "L3_gnn_b2")
COLS = ("L2_gnn_b", "L2_gnn_gamma", "L2_gnn_beta")


def last_weight_phase(nc, S, A):
    with Scope(nc, "lw") as s:
        att = s.sb("att", [P, 2, D])
        prod = s.sb("prod", [P, D])
        s_att = s.sem("att_loaded")
        with s.block() as block:

            @block.sync
            def _(sp):
                for k, name in enumerate(ATT1):
                    sp.dma_start(att[:, k, :], A[name].rearrange("h c -> (h c)").partition_broadcast(P)).then_inc(s_att, 16)

            @block.vector
            def _(dve):
                dve.wait_ge(s_att, 32)
                for k in range(KC):
                    for v in range(2):
                        dve.tensor_tensor(prod[:], S["w_L3b"][:, k, 0:D], att[:, v, :], ALU.mult)
                        dve.drain()
                        dve.tensor_reduce(S["w_L3b"][:, k, D + v:D + v + 1], prod[:], AX_X, ALU.add)
                        dve.drain()
                dve.memset(S["w_L3b"][:, :, D + 2:RW], 0.0)


def edge_phase(nc, S, tag, table, tw, acc, aw, scale=None, heads=0, ad=None):
    with Scope(nc, tag) as s:
        g = [s.sb(f"g{b}", [P, BC, tw]) for b in range(2)]
        run = [s.sb(f"run{b}", [P, BC + 1, aw]) for b in range(2)]
        st = [s.sb(f"st{b}", [P, BC], I32) for b in range(2)]
        s_st = s.sem("indices_staged")
        s_g = [s.pool_sem(S, f"rows_gathered{b}") for b in range(2)]
        s_gf = s.sem("rows_used")
        s_run = s.sem("run_ready")
        s_sv = s.sems("run_stored")
        s_ex = s.sem("exponents_ready")
        s_w = s.sem("weights_ready")
        if heads:
            std = [s.sb(f"std{b}", [P, BC], I32) for b in range(2)]
            adg = [s.sb(f"adg{b}", [P, BC, heads]) for b in range(2)]
            e = s.sb("e", [P, heads, BC])
            mx = s.sb("mx", [P, heads, BC + 1])
            ex = [s.sb(f"ex{b}", [P, 2, heads, BC]) for b in range(2)]
            wd = [s.sb(f"wd{b}", [P, 2, heads, BC]) for b in range(2)]
            s_init = s.sem("ad_cleared")
        else:
            inv = s.sb("inv", [P, BC])
        accv = acc.rearrange("(p c) w -> p c w", c=C)
        hw = D // heads if heads else D
        per = 2 if heads else 1
        with s.block() as block:

            @block.gpsimd
            def _(pool):
                if heads:
                    pool.wait_ge(s_init, 1)

                def step(t):
                    if not t.before(2):
                        hold(pool, S["passed"], s_gf, t.n - 1)
                    pool.tensor_copy(st[t.par][:], S["src32"][:, bass.ds(t.n * BC, BC)]).then_inc(s_st, 1)
                    if heads:
                        pool.tensor_copy(std[t.par][:], S["dst32"][:, bass.ds(t.n * BC, BC)]).then_inc(s_st, 1)
                    hold(pool, S["passed"], s_st, (t.n + 1) * per)
                    for k in range(BC):
                        pool.indirect_dma_start(out=g[t.par][:, k, :], out_offset=None, in_=table,
                                                in_offset=bass.IndirectOffsetOnAxis(ap=st[t.par][:, k:k + 1], axis=0),
                                                bounds_check=table.shape[0] - 1, oob_is_err=False).then_inc(s_g[t.par], 16)
                        if heads:
                            pool.indirect_dma_start(out=adg[t.par][:, k, :], out_offset=None, in_=ad,
                                                    in_offset=bass.IndirectOffsetOnAxis(ap=std[t.par][:, k:k + 1], axis=0),
                                                    bounds_check=ad.shape[0] - 1, oob_is_err=False).then_inc(s_g[t.par], 16)

                over_blocks(pool, step, NBAT, peel=1)

            @block.vector
            def _(dve):
                dve.memset(run[1][:], 0.0)
                if heads:
                    dve.memset(run[0][:], 0.0)
                    dve.memset(mx[:], -BIG)
                    for b in range(2):
                        dve.memset(adg[b][:], 0.0)
                    dve.drain().then_inc(s_init, 1)
                else:
                    dve.drain()

                def step(t):
                    gt, rt, ro = g[t.par], run[t.par], run[1 - t.par]
                    dve.wait_ge(s_g[t.par], (t.half + 1) * 16 * BC * per)
                    if not t.before(2):
                        dve.wait_ge(s_sv[t.par], t.half * 16)
                    dve.tensor_copy(rt[:, 0, :], ro[:, BC, :])
                    if heads:
                        dve.tensor_copy(mx[:, :, 0:1], mx[:, :, BC:BC + 1])
                        dve.tensor_tensor(e[:], gt[:, :, D:D + heads].rearrange("p c h -> p h c"),
                                          adg[t.par][:].rearrange("p c h -> p h c"), ALU.add)
                        dve.drain()
                        dve.scalar_tensor_tensor(e[:], e[:], SLOPE, e[:], ALU.mult, ALU.max)
                        dve.tensor_copy(wd_cut[:], S["cut"][:, bass.ds(t.n * BC, BC)])
                        dve.drain()
                        for h in range(heads):
                            dve.tensor_tensor_scan(mx[:, h, 1:BC + 1], wd_cut[:], e[:, h, :], mx[:, h, 0:1], ALU.add, ALU.max)
                        dve.drain()
                        dve.tensor_tensor(ex[t.par][:, 0], e[:], mx[:, :, 1:BC + 1], ALU.subtract)
                        dve.tensor_tensor(ex[t.par][:, 1], mx[:, :, 0:BC], mx[:, :, 1:BC + 1], ALU.subtract)
                        dve.drain()
                        for h in range(heads):
                            last = dve.tensor_tensor(ex[t.par][:, 1, h, :], ex[t.par][:, 1, h, :], wd_cut[:], ALU.add)
                        last.then_inc(s_ex, 1)
                        dve.wait_ge(s_w, t.n + 1)
                        w, decay = wd[t.par][:, 0], wd[t.par][:, 1]
                        for h in range(heads):
                            dve.tensor_tensor_scan(rt[:, 1:BC + 1, D + h], decay[:, h, :], w[:, h, :],
                                                   rt[:, 0, D + h:D + h + 1], ALU.mult, ALU.add)
                        dve.tensor_copy(rt[:, 1:BC + 1, D + heads:D + 2 * heads],
                                        mx[:, :, 1:BC + 1].rearrange("p h c -> p c h"))
                        for h in range(heads):
                            dve.tensor_tensor(gt[:, :, h * hw:(h + 1) * hw], gt[:, :, h * hw:(h + 1) * hw],
                                              spread(w[:, h, :], hw), ALU.mult)
                        dve.drain()
                        for k in range(BC):
                            for h in range(heads):
                                f = slice(h * hw, (h + 1) * hw)
                                last = dve.scalar_tensor_tensor(rt[:, k + 1, f], rt[:, k, f], decay[:, h, k:k + 1],
                                                                gt[:, k, f], ALU.mult, ALU.add)
                            last = dve.drain()
                    else:
                        dve.tensor_copy(stsame[:], S["same"][:, bass.ds(t.n * BC, BC)])
                        if scale:
                            if scale == "inverse":
                                dve.tensor_scalar(inv[:], gt[:, :, D], 1.0, None, ALU.max)
                                dve.drain()
                                dve.reciprocal(inv[:], inv[:])
                            else:
                                dve.tensor_copy(inv[:], gt[:, :, D])
                            dve.drain()
                            dve.tensor_tensor(gt[:, :, 0:D], gt[:, :, 0:D], spread(inv[:], D), ALU.mult)
                            dve.drain()
                            if scale == "inverse":
                                dve.tensor_scalar(gt[:, :, 0:D], gt[:, :, 0:D], 0.0, None, ALU.max)
                        dve.drain()
                        for k in range(BC):
                            dve.scalar_tensor_tensor(rt[:, k + 1, :], rt[:, k, :], stsame[:, k:k + 1],
                                                     gt[:, k, 0:D], ALU.mult, ALU.add)
                            last = dve.drain()
                    last.then_inc(s_run, 1)
                    dve.sem_inc(s_gf, 1)

                if heads:
                    wd_cut = s.sb("cutb", [P, BC])
                else:
                    stsame = s.sb("sameb", [P, BC])
                over_blocks(dve, step, NBAT, peel=1)
                dve.tensor_copy(S["tail"][:, 0:aw], run[(NBAT - 1) % 2][:, BC, :])

            @block.scalar
            def _(act):
                if heads:
                    def step(t):
                        act.wait_ge(s_ex, t.n + 1)
                        act.activation(wd[t.par][:], ex[t.par][:], ACT.Exp).then_inc(s_w, 1)

                    over_blocks(act, step, NBAT)

            @block.sync
            def _(sp):
                def step(t):
                    sp.wait_ge(s_run, t.n + 1)
                    sp.dma_start(accv[:, bass.ds(t.n * BC, BC), :], run[t.par][:, 1:BC + 1, :]).then_inc(s_sv[t.par], 16)

                over_blocks(sp, step, NBAT)
                for b in range(2):
                    sp.wait_ge(s_sv[b], 16 * NBAT // 2)


def repair_phase(nc, S, tag, acc, aw, heads=0):
    with Scope(nc, tag) as s:
        row = s.sb("row", [P, aw])
        car = s.sb("car", [P, D + heads])
        pc = s.ps("pc", [P, 512])
        s_r0 = s.sem("row_cleared")
        s_row = s.pool_sem(S, "row_gathered")
        s_car = s.sem("carried")
        s_fix = s.sem("row_repaired")
        s_out = s.pool_sem(S, "row_scattered")
        if heads:
            dg = s.sb("dg", [P, heads, P])
            x = s.sb("x", [P, heads, P])
            ms = s.sb("ms", [P, heads])
            mn = s.sb("mn", [P, 2, heads])
            wt = s.sb("wt", [P, 2, heads])
            xt = s.sb("xt", [P, heads, P])
            pb = s.ps("pb", [P, heads, P])
            pt = s.ps("pt", [P, heads, P])
            s_dg = s.sem("diag_ready")
            s_pb = s.sem("max_spread")
            s_x = s.sem("exponent_ready")
            s_ex = s.sem("exp_done")
            s_xm = s.sem("factors_masked")
            s_pt = s.sem("factors_turned")
            s_xt = s.sem("factors_copied")
            s_mn = s.sem("shifts_ready")
            s_wt = s.sem("shift_exp_done")
        hw = D // heads if heads else D
        with s.block() as block:

            @block.gpsimd
            def _(pool):
                pool.wait_ge(s_r0, 1)
                pool.indirect_dma_start(out=row[:, :], out_offset=None, in_=acc,
                                        in_offset=bass.IndirectOffsetOnAxis(ap=S["repair32"][:], axis=0),
                                        bounds_check=P * C - 1, oob_is_err=False).then_inc(s_row, 16)
                pool.wait_ge(s_fix, 1)
                pool.indirect_dma_start(out=acc, out_offset=bass.IndirectOffsetOnAxis(ap=S["repair32"][:], axis=0),
                                        in_=row[:, :], in_offset=None,
                                        bounds_check=P * C - 1, oob_is_err=False).then_inc(s_out, 16)
                pool.wait_ge(s_out, 16)

            @block.tensor
            def _(pe):
                if not heads:
                    pe.matmul(pc[:, 0:D], S["join"][:], S["tail"][:, 0:D], start=True, stop=True).then_inc(s_car, 1)
                    return
                pe.wait_ge(s_dg, 1)
                for h in range(heads):
                    last = pe.matmul(pb[:, h, :], S["ones"][:], dg[:, h, :], start=True, stop=True)
                last.then_inc(s_pb, 1)
                pe.wait_ge(s_xm, 1)
                for h in range(heads):
                    last = pe.transpose(pt[:, h, :], x[:, h, :], S["ident"][:])
                last.then_inc(s_pt, 1)
                pe.wait_ge(s_xt, 1)
                for h in range(heads):
                    pe.matmul(pc[:, h * hw:(h + 1) * hw], xt[:, h, :], S["tail"][:, h * hw:(h + 1) * hw], start=True, stop=True)
                    last = pe.matmul(pc[:, D + h:D + h + 1], xt[:, h, :], S["tail"][:, D + h:D + h + 1], start=True, stop=True)
                last.then_inc(s_car, 1)

            @block.vector
            def _(dve):
                dve.memset(row[:], 0.0)
                dve.drain().then_inc(s_r0, 1)
                if not heads:
                    dve.wait_ge(s_car, 1)
                    dve.wait_ge(s_row, 16)
                    dve.tensor_tensor(row[:], row[:], pc[:, 0:D], ALU.add).then_inc(s_fix, 1)
                    return
                m = S["tail"][:, D + heads:D + 2 * heads]
                for h in range(heads):
                    last = dve.tensor_scalar(dg[:, h, :], S["ident"][:], m[:, h:h + 1], None, ALU.mult)
                last.then_inc(s_dg, 1)
                dve.wait_ge(s_pb, 1)
                for h in range(heads):
                    dve.tensor_tensor(x[:, h, :], pb[:, h, :], S["joincut"][:], ALU.add)
                dve.drain()
                dve.tensor_reduce(ms[:], x[:], AX_X, ALU.max)
                dve.drain()
                dve.tensor_tensor(x[:], x[:], spread(ms[:], P), ALU.subtract).then_inc(s_x, 1)
                dve.wait_ge(s_ex, 1)
                for h in range(heads):
                    last = dve.tensor_tensor(x[:, h, :], x[:, h, :], S["joinT"][:], ALU.mult)
                last.then_inc(s_xm, 1)
                dve.wait_ge(s_pt, 1)
                dve.tensor_copy(xt[:], pt[:]).then_inc(s_xt, 1)
                dve.wait_ge(s_row, 16)
                rm = row[:, D + heads:D + 2 * heads]
                dve.tensor_tensor(car[:, D:D + heads], rm, ms[:], ALU.max)
                dve.drain()
                dve.tensor_tensor(mn[:, 0, :], rm, car[:, D:D + heads], ALU.subtract)
                dve.tensor_tensor(mn[:, 1, :], ms[:], car[:, D:D + heads], ALU.subtract).then_inc(s_mn, 1)
                dve.wait_ge(s_wt, 1)
                dve.tensor_copy(rm, car[:, D:D + heads])
                dve.wait_ge(s_car, 1)
                dve.drain()
                dve.tensor_tensor(row[:, D:D + heads], row[:, D:D + heads], wt[:, 0, :], ALU.mult)
                dve.tensor_tensor(car[:, D:D + heads], pc[:, D:D + heads], wt[:, 1, :], ALU.mult)
                for h in range(heads):
                    f = slice(h * hw, (h + 1) * hw)
                    dve.tensor_scalar(row[:, f], row[:, f], wt[:, 0, h:h + 1], None, ALU.mult)
                    dve.tensor_scalar(car[:, f], pc[:, f], wt[:, 1, h:h + 1], None, ALU.mult)
                dve.drain()
                dve.tensor_tensor(row[:, 0:D + heads], row[:, 0:D + heads], car[:, 0:D + heads], ALU.add).then_inc(s_fix, 1)

            @block.scalar
            def _(act):
                if heads:
                    act.wait_ge(s_x, 1)
                    act.activation(x[:], x[:], ACT.Exp).then_inc(s_ex, 1)
                    act.wait_ge(s_mn, 1)
                    act.activation(wt[:], mn[:], ACT.Exp).then_inc(s_wt, 1)


def hyper_phase(nc, S, tag, acc, w1, w2, out):
    with Scope(nc, tag) as s:
        g = [s.sb(f"g{b}", [P, J, D]) for b in range(2)]
        z = [s.sb(f"z{b}", [P, J, D]) for b in range(2)]
        st = [s.sb(f"st{b}", [P, J], I32) for b in range(2)]
        zt = s.sb("zt", [P, KC, J, P])
        rt = s.sb("rt", [P, KC, J * P])
        o = [s.sb(f"o{b}", [P, J, D]) for b in range(2)]
        eb = s.sb("eb", [P, J])
        pt = s.ps("pt", [P, KC, J, P])
        pr = s.ps("pr", [P, KC, J * P])
        po = s.ps("po", [P, J, 512 // 2])
        s_st = s.sem("indices_staged")
        s_clr = s.sem("rows_cleared")
        s_g = [s.pool_sem(S, f"rows_gathered{b}") for b in range(2)]
        s_z = s.sem("z_ready")
        s_t = s.sem("z_turned")
        s_zt = s.sem("zt_copied")
        s_r = s.sem("hidden_ready")
        s_rt = s.sem("hidden_relu")
        s_m = s.sem("product_ready")
        s_o = s.sem("out_copied")
        s_sv = s.sems("out_stored")
        outv = out.rearrange("(n p j) w -> n p j w", p=P, j=J)
        with s.block() as block:

            @block.gpsimd
            def _(pool):
                def step(t):
                    hold(pool, S["passed"], s_clr, t.n + 1)
                    pool.tensor_copy(st[t.par][:], S["last32"][:, bass.ds(t.n * J, J)]).then_inc(s_st, 1)
                    hold(pool, S["passed"], s_st, t.n + 1)
                    for j in range(J):
                        pool.indirect_dma_start(out=g[t.par][:, j, :], out_offset=None, in_=acc,
                                                in_offset=bass.IndirectOffsetOnAxis(ap=st[t.par][:, j:j + 1], axis=0),
                                                bounds_check=P * C - 1, oob_is_err=False).then_inc(s_g[t.par], 16)

                over_blocks(pool, step, HB)

            @block.vector
            def _(dve):
                for b in range(2):
                    dve.memset(g[b][:], 0.0).then_inc(s_clr, 1)

                def step(t):
                    dve.tensor_copy(eb[:], S["einv"][:, bass.ds(t.n * J, J)])
                    dve.drain()
                    if not t.before(2):
                        dve.wait_ge(s_t, t.n - 1)
                    dve.wait_ge(s_g[t.par], (t.half + 1) * 16 * J)
                    dve.tensor_tensor(z[t.par][:], g[t.par][:], spread(eb[:], D), ALU.mult).then_inc(s_z, 1)
                    dve.drain()
                    dve.memset(g[t.par][:], 0.0).then_inc(s_clr, 1)

                over_blocks(dve, step, HB, peel=1)

            @block.tensor
            def _(pe):
                def step(t):
                    pe.wait_ge(s_z, t.n + 1)
                    for k in range(KC):
                        for j in range(J):
                            last = pe.transpose(pt[:, k, j, :], z[t.par][:, j, k * P:(k + 1) * P], S["ident"][:])
                    last.then_inc(s_t, 1)
                    pe.wait_ge(s_zt, t.n + 1)
                    for m in range(KC):
                        for k in range(KC):
                            last = pe.matmul(pr[:, m, :], w1[:, k, m * P:(m + 1) * P],
                                             zt[:, k].rearrange("p j n -> p (j n)"), start=k == 0, stop=k == KC - 1)
                    last.then_inc(s_r, 1)
                    pe.wait_ge(s_rt, t.n + 1)
                    if not t.before(1):
                        pe.wait_ge(s_o, t.n)
                    for j in range(J):
                        for k in range(KC):
                            last = pe.matmul(po[:, j, :], rt[:, k, j * P:(j + 1) * P], w2[:, k, 0:D],
                                             start=k == 0, stop=k == KC - 1)
                    last.then_inc(s_m, 1)

                over_blocks(pe, step, HB, peel=1)

            @block.scalar
            def _(act):
                def step(t):
                    act.wait_ge(s_t, t.n + 1)
                    act.activation(zt[:], pt[:], ACT.Copy).then_inc(s_zt, 1)
                    act.wait_ge(s_r, t.n + 1)
                    act.activation(rt[:], pr[:], ACT.Relu).then_inc(s_rt, 1)
                    act.wait_ge(s_m, t.n + 1)
                    if not t.before(2):
                        act.wait_ge(s_sv[t.par], t.half * 16)
                    act.activation(o[t.par][:], po[:], ACT.Copy).then_inc(s_o, 1)

                over_blocks(act, step, HB, peel=1)

            @block.sync
            def _(sp):
                def step(t):
                    sp.wait_ge(s_o, t.n + 1)
                    sp.dma_start(outv[bass.ds(t.n, 1)].rearrange("n p j w -> (n p) j w"), o[t.par][:]).then_inc(s_sv[t.par], 16)

                over_blocks(sp, step, HB)
                for b in range(2):
                    sp.wait_ge(s_sv[b], 16 * HB // 2)


def source_sum_phase(nc, S, tag, table, sums):
    with Scope(nc, tag) as s:
        g = s.sb("g", [P, BC, SW])
        st = s.sb("st", [P, BC], I32)
        key = s.sb("key", [P, BC])
        dg = [s.sb(f"dg{b}", [P, P]) for b in range(2)]
        eq = [s.sb(f"eq{b}", [P, P]) for b in range(2)]
        junk = s.sb("junk", [P, P])
        dup = [s.sb(f"dup{b}", [P, 3]) for b in range(2)]
        idx = [s.sb(f"idx{b}", [P, 1], I32) for b in range(2)]
        tot = [s.sb(f"tot{b}", [P, SW]) for b in range(2)]
        pk = [s.ps(f"pk{b}", [P, P]) for b in range(2)]
        pt = [s.ps(f"pt{b}", [P, SW]) for b in range(2)]
        s_one = s.sem("ones_set")
        s_st = s.sem("indices_staged")
        s_key = s.sem("keys_staged")
        s_g = [s.pool_sem(S, f"row_gathered{k}") for k in range(BC)]
        s_dg = s.sem("diag_ready")
        s_pk = s.sem("keys_spread")
        s_eq = s.sem("equal_ready")
        s_tot = s.sem("total_ready")
        s_cp = s.sem("total_copied")
        s_add = s.pool_sem(S, "rows_added")
        AHEAD = 3
        with s.block() as block:

            @block.gpsimd
            def _(pool):
                pool.wait_ge(s_one, 1)

                def body(i, first):
                    if not first:
                        hold(pool, S["passed"], s_tot, i * BC)
                    pool.tensor_copy(st[:], S["hyp32"][:, bass.ds(i * BC, BC)]).then_inc(s_st, 1)
                    hold(pool, S["passed"], s_st, i + 1)

                    def gather(k):
                        pool.indirect_dma_start(out=g[:, k, 0:D], out_offset=None, in_=table,
                                                in_offset=bass.IndirectOffsetOnAxis(ap=st[:, k:k + 1], axis=0),
                                                bounds_check=table.shape[0] - 1, oob_is_err=False).then_inc(s_g[k], 16)

                    for k in range(AHEAD):
                        gather(k)
                    for k in range(BC):
                        if k + AHEAD < BC:
                            gather(k + AHEAD)
                        hold(pool, S["passed"], s_cp, i * BC + k + 1)
                        if not (first and k == 0):
                            hold(pool, S["passed"], s_add, (i * BC + k) * 16)
                        pool.indirect_dma_start(out=sums, out_offset=bass.IndirectOffsetOnAxis(ap=idx[k % 2][:, 0:1], axis=0),
                                                in_=tot[k % 2][:, :], in_offset=None, bounds_check=sums.shape[0] - 1,
                                                compute_op=ALU.add).then_inc(s_add, 16)

                body(0, True)
                with pool.Fori(1, NBAT) as i:
                    body(i, False)
                pool.wait_ge(s_add, 16 * C)

            @block.vector
            def _(dve):
                dve.memset(g[:], 1.0)
                dve.drain().then_inc(s_one, 1)

                def body(i, first):
                    if not first:
                        dve.wait_ge(s_pk, i * BC)
                    dve.tensor_copy(key[:], S["skey"][:, bass.ds(i * BC, BC)])
                    dve.drain()

                    def diagonal(k):
                        if k >= 2:
                            dve.wait_ge(s_pk, i * BC + k - 1)
                        dve.tensor_scalar(dg[k % 2][:], S["ident"][:], key[:, k:k + 1], None, ALU.mult).then_inc(s_dg, 1)

                    diagonal(0)
                    for k in range(BC):
                        if k + 1 < BC:
                            diagonal(k + 1)
                        b = k % 2
                        dve.wait_ge(s_pk, i * BC + k + 1)
                        if not (first and k < 2):
                            dve.wait_ge(s_tot, i * BC + k - 1)
                            dve.wait_ge(s_add, (i * BC + k - 1) * 16)
                        dve.tensor_scalar(eq[b][:], pk[b][:], key[:, k:k + 1], None, ALU.is_equal).then_inc(s_eq, 1)
                        dve.tensor_tensor(dup[b][:, 1:2], S["dummy"][:], key[:, k:k + 1], ALU.subtract)
                        dve.drain()
                        dve.tensor_tensor_reduce(junk[:], eq[b][:], S["lower"][:], 1.0, 0.0, ALU.mult, ALU.add, dup[b][:, 0:1])
                        dve.drain()
                        dve.tensor_scalar(dup[b][:, 0:1], dup[b][:, 0:1], 1.0, None, ALU.min)
                        dve.drain()
                        dve.scalar_tensor_tensor(dup[b][:, 2:3], dup[b][:, 1:2], dup[b][:, 0:1], key[:, k:k + 1], ALU.mult, ALU.add)
                        dve.drain()
                        dve.tensor_copy(idx[b][:], dup[b][:, 2:3]).then_inc(s_key, 1)

                body(0, True)
                with dve.Fori(1, NBAT) as i:
                    body(i, False)

            @block.tensor
            def _(pe):
                def body(i, first):
                    def keys(k):
                        pe.wait_ge(s_dg, i * BC + k + 1)
                        if not (first and k < 2):
                            pe.wait_ge(s_eq, i * BC + k - 1)
                        pe.matmul(pk[k % 2][:], S["ones"][:], dg[k % 2][:], start=True, stop=True).then_inc(s_pk, 1)

                    keys(0)
                    for k in range(BC):
                        if k + 1 < BC:
                            keys(k + 1)
                        pe.wait_ge(s_eq, i * BC + k + 1)
                        pe.wait_ge(s_g[k], (i + 1) * 16)
                        if not (first and k < 2):
                            pe.wait_ge(s_cp, i * BC + k - 1)
                        pe.matmul(pt[k % 2][:], eq[k % 2][:], g[:, k, :], start=True, stop=True).then_inc(s_tot, 1)

                body(0, True)
                with pe.Fori(1, NBAT) as i:
                    body(i, False)

            @block.scalar
            def _(act):
                def body(i, first):
                    for k in range(BC):
                        act.wait_ge(s_tot, i * BC + k + 1)
                        if not (first and k < 2):
                            act.wait_ge(s_add, (i * BC + k - 1) * 16)
                        act.wait_ge(s_key, i * BC + k + 1)
                        act.activation(tot[k % 2][:], pt[k % 2][:], ACT.Copy).then_inc(s_cp, 1)

                body(0, True)
                with act.Fori(1, NBAT) as i:
                    body(i, False)


def node_phase(nc, S, tag, rows, rw, extra=None, ew=D, gather=None, gw=0, heads=0, kind="", bias=None, elu=False,
               loops=False, norm=False, affine=None, save=None, sw=D, weight=None, oheads=0, out=None, ad=None,
               final=False):
    gcn, bn, gat = kind == "gcn", kind == "bn", kind == "gat"
    hw = D // heads if heads else D
    lag = 2 if norm else 1
    with Scope(nc, tag) as s:
        a = [s.sb(f"a{b}", [P, J, rw]) for b in range(2)]
        z = [s.sb(f"z{b}", [P, J, sw]) for b in range(2)]
        s_in = s.sems("rows_loaded")
        s_used = s.sem("inputs_used")
        s_z = s.sem("z_ready")
        s_zs = s.sems("z_stored")
        s_t = s.sem("z_turned")
        s_zt = s.sem("zt_copied")
        s_m = s.sem("product_ready")
        s_o = s.sem("out_copied")
        s_os = s.sems("out_stored")
        s_ex = s.sem("exponents_ready")
        s_wt = s.sem("weights_ready")
        s_st = s.sem("indices_staged")
        s_clr = s.sem("gathered_cleared")
        s_g = [s.pool_sem(S, f"runs_gathered{b}") for b in range(2)]
        s_var = s.sem("variance_ready")
        s_rs = s.sem("rstd_ready")
        s_y = s.sem("bn_ready")
        s_yt = s.sem("bn_turned")
        s_bs = s.sem("stats_read")
        nin = 1 + (extra is not None) + bn
        if extra is not None:
            r = [s.sb(f"r{b}", [P, J, ew]) for b in range(2)]
        if gather is not None:
            g = [s.sb(f"g{b}", [P, J, gw]) for b in range(2)]
            st = [s.sb(f"st{b}", [P, J], I32) for b in range(2)]
        if gat:
            e = s.sb("e", [P, J, heads])
            mm = s.sb("mm", [P, J, heads])
            den = s.sb("den", [P, J, heads])
            d2 = s.sb("d2", [P, J, heads])
            ex = [s.sb(f"ex{b}", [P, 2, J, heads]) for b in range(2)]
            wt = [s.sb(f"wt{b}", [P, 2, J, heads]) for b in range(2)]
            v = s.sb("v", [P, J, D])
            lp = s.sb("lp", [P, 2, J])
        u = [s.sb(f"u{b}", [P, J, D]) for b in range(2)] if norm else [s.sb("u0", [P, J, D])] * 2
        if elu:
            en = [s.sb(f"en{b}", [P, J, D]) for b in range(2)]
            ee = [s.sb(f"ee{b}", [P, J, D]) for b in range(2)]
            s_en = s.sem("negative_part_ready")
            s_ee = s.sem("negative_exp_done")
        if norm:
            bs = s.sb("bs", [P, J, 6])
            mv = [s.sb(f"mv{b}", [P, J, 2]) for b in range(2)]
            ve = [s.sb(f"ve{b}", [P, J]) for b in range(2)]
            rs = [s.sb(f"rs{b}", [P, J]) for b in range(2)]
        if kind in ("sum", "gcn") or save is not None:
            sc = s.sb("sc", [P, J])
        if weight is not None:
            zt = s.sb("zt", [P, KC, J, P])
            pt = s.ps("pt", [P, KC, J, P])
            if gcn:
                o = [s.sb(f"o{b}", [P, KC, J * P]) for b in range(2)]
                pm = s.ps("pm", [P, KC, J * P])
                stats = s.sb("stats", [P, KC, NB, 6])
                bmv = s.sb("bmv", [P, KC, 2])
                bt = s.sb("bt", [P, KC, 2])
                s_fin = s.sem("batch_variance")
                s_frs = s.sem("batch_rstd")
            else:
                o = [s.sb(f"o{b}", [P, J, RW]) for b in range(2)]
                ao = [s.sb(f"ao{b}", [P, J, oheads]) for b in range(2)]
                pm = s.ps("pm", [P, J, 512])
                wc = D + 2 * oheads
        if bn:
            yt = [s.sb(f"yt{b}", [P, KC, J * P]) for b in range(2)]
            yr = [s.sb(f"yr{b}", [P, KC, J, P]) for b in range(2)]
            py = s.ps("py", [P, J, KC, P])
        per_o = 1 if gcn else 2
        rowsv = rows.rearrange("(n p j) w -> n p j w", p=P, j=J) if rows.shape[0] == NPAD else None
        view = lambda t: t.rearrange("(n p j) w -> n p j w", p=P, j=J)
        blockof = lambda t, n: view(t)[bass.ds(n, 1)].rearrange("n p j w -> (n p) j w")
        tailrows = lambda t: t[(NB - 1) * BLK:N, :].rearrange("(p j) w -> p j w", j=J)
        headrows = lambda t, n: t[bass.ds(n * BLK, BLK), :].rearrange("(p j) w -> p j w", j=J)

        with s.block() as block:

            @block.sync
            def _(sp):
                if rowsv is None:
                    sp.wait_ge(s_clr, 1)

                def load(t):
                    if not t.before(2):
                        sp.wait_ge(s_used, t.n - 1)
                    if rowsv is None:
                        if t.fixed and t.n == NB - 1:
                            sp.dma_start(a[t.par][0:TAILP, :, :], tailrows(rows)).then_inc(s_in[t.par], 16)
                        else:
                            sp.dma_start(a[t.par][:], headrows(rows, t.n)).then_inc(s_in[t.par], 16)
                    else:
                        sp.dma_start(a[t.par][:], blockof(rows, t.n)).then_inc(s_in[t.par], 16)
                    if extra is not None:
                        sp.dma_start(r[t.par][:], headrows(extra, t.n)).then_inc(s_in[t.par], 16)
                    if bn:
                        sp.dma_start(yt[t.par][:], S["AGG"][:, :, bass.ds(t.n * BLK, BLK)]).then_inc(s_in[t.par], 16)

                def store_z(t):
                    sp.wait_ge(s_z, t.n + 1)
                    if final and t.fixed and t.n == NB - 1:
                        sp.dma_start(tailrows(save), z[t.par][0:TAILP, :, :]).then_inc(s_zs[t.par], 16)
                    else:
                        sp.dma_start(headrows(save, t.n), z[t.par][:]).then_inc(s_zs[t.par], 16)

                def store_o(t):
                    sp.wait_ge(s_o, t.n + 1)
                    if gcn:
                        sp.dma_start(S["AGG"][:, :, bass.ds(t.n * BLK, BLK)], o[t.par][:]).then_inc(s_os[t.par], 16)
                    else:
                        sp.dma_start(headrows(out, t.n), o[t.par][:]).then_inc(s_os[t.par], 16)
                        sp.dma_start(headrows(ad, t.n), ao[t.par][:]).then_inc(s_os[t.par], 16)

                def step(t):
                    load(t)
                    if save is not None and not t.before(2):
                        store_z(t.back(2))
                    if weight is not None and not t.before(3):
                        store_o(t.back(3))

                over_blocks(sp, step, NB, peel=2, tail=1)
                for n in range(NB - 3, NB):
                    if save is not None and n >= NB - 2:
                        store_z(Step(n))
                    if weight is not None:
                        store_o(Step(n))
                for b in range(2):
                    if save is not None:
                        sp.wait_ge(s_zs[b], 16 * NB // 2)
                    if weight is not None:
                        sp.wait_ge(s_os[b], 16 * per_o * NB // 2)

            @block.gpsimd
            def _(pool):
                def gathers(t):
                    hold(pool, S["passed"], s_clr, t.n + 1)
                    pool.tensor_copy(st[t.par][:], S["last32"][:, bass.ds(t.n * J, J)]).then_inc(s_st, 1)
                    hold(pool, S["passed"], s_st, t.n + 1)
                    for j in range(J):
                        pool.indirect_dma_start(out=g[t.par][:, j, :], out_offset=None, in_=gather,
                                                in_offset=bass.IndirectOffsetOnAxis(ap=st[t.par][:, j:j + 1], axis=0),
                                                bounds_check=P * C - 1, oob_is_err=False).then_inc(s_g[t.par], 16)

                def rstd(t):
                    hold(pool, S["passed"], s_var, t.n + 1)
                    pool.tensor_tensor(rs[t.par][:], ve[t.par][:], S["minus_half"][:, 0:J], ALU.pow).then_inc(s_rs, 1)

                def step(t):
                    if gather is not None:
                        gathers(t)
                    if norm and not t.before(1):
                        rstd(t.back(1))

                if gather is not None or norm:
                    over_blocks(pool, step, NB, peel=1)
                if norm:
                    rstd(Step(NB - 1))
                if gcn:
                    pool.wait_ge(s_fin, 1)
                    pool.tensor_tensor(bt[:, :, 0], bmv[:, :, 1], S["minus_half"][:, 0:KC], ALU.pow).then_inc(s_frs, 1)

            @block.tensor
            def _(pe):
                def turn_bn(t):
                    pe.wait_ge(s_y, t.n + 1)
                    if not t.before(1):
                        pe.wait_ge(s_bs, t.n)
                    for j in range(J):
                        for k in range(KC):
                            last = pe.transpose(py[:, j, k, :], yr[t.par][:, k, j, :], S["ident"][:])
                    last.then_inc(s_yt, 1)

                def product(t):
                    pe.wait_ge(s_z, t.n + 1)
                    for k in range(KC):
                        for j in range(J):
                            last = pe.transpose(pt[:, k, j, :], z[t.par][:, j, k * P:(k + 1) * P], S["ident"][:])
                    last.then_inc(s_t, 1)
                    pe.wait_ge(s_zt, t.n + 1)
                    if not t.before(1):
                        pe.wait_ge(s_o, t.n)
                    if gcn:
                        for m in range(KC):
                            for k in range(KC):
                                last = pe.matmul(pm[:, m, :], weight[:, k, m * P:(m + 1) * P],
                                                 zt[:, k].rearrange("p j n -> p (j n)"), start=k == 0, stop=k == KC - 1)
                    else:
                        for j in range(J):
                            for k in range(KC):
                                last = pe.matmul(pm[:, j, 0:wc], zt[:, k, j, :], weight[:, k, 0:wc],
                                                 start=k == 0, stop=k == KC - 1)
                    last.then_inc(s_m, 1)

                def step(t):
                    if bn:
                        turn_bn(t)
                        if not t.before(1):
                            product(t.back(1))
                    else:
                        product(t)

                if weight is not None:
                    over_blocks(pe, step, NB, peel=1)
                    if bn:
                        product(Step(NB - 1))

            @block.scalar
            def _(act):
                def front(t):
                    if gat:
                        act.wait_ge(s_ex, t.n + 1)
                        act.activation(wt[t.par][:], ex[t.par][:], ACT.Exp).then_inc(s_wt, 1)
                    if elu:
                        act.wait_ge(s_en, t.n + 1)
                        act.activation(ee[t.par][:], en[t.par][:], ACT.Exp).then_inc(s_ee, 1)
                    if bn:
                        act.wait_ge(s_in[t.par], (t.half + 1) * 16 * nin)
                        if not t.before(2):
                            act.wait_ge(s_yt, t.n - 1)
                        for k in range(KC):
                            last = act.activation(yr[t.par][:, k].rearrange("p j n -> p (j n)"), yt[t.par][:, k, :],
                                                  ACT.Relu, bias=S["bnshift"][:, k:k + 1], scale=S["bnscale"][:, k:k + 1])
                        last.then_inc(s_y, 1)

                def back(t):
                    act.wait_ge(s_t, t.n + 1)
                    act.activation(zt[:], pt[:], ACT.Copy).then_inc(s_zt, 1)
                    act.wait_ge(s_m, t.n + 1)
                    if not t.before(2):
                        act.wait_ge(s_os[t.par], t.half * 16 * per_o)
                    if gcn:
                        if not t.before(2):
                            act.wait_ge(s_bs, t.n - 1)
                        for m in range(KC):
                            last = act.activation(o[t.par][:, m, :], pm[:, m, :], ACT.Identity, bias=S["c_L2_gnn_b"][:, m:m + 1])
                    else:
                        act.activation(o[t.par][:, :, 0:wc], pm[:, :, 0:wc], ACT.Copy)
                        last = act.activation(ao[t.par][:], pm[:, :, D + oheads:D + 2 * oheads], ACT.Copy)
                    last.then_inc(s_o, 1)

                def step(t):
                    front(t)
                    if weight is not None and not t.before(lag):
                        back(t.back(lag))

                if weight is not None and not gcn and wc < RW:
                    act.wait_ge(s_clr, 2)
                over_blocks(act, step, NB, peel=2)
                if weight is not None:
                    for n in range(NB - lag, NB):
                        back(Step(n))

            @block.vector
            def _(dve):
                if weight is not None and not gcn and wc < RW:
                    for b in range(2):
                        dve.memset(o[b][:], 0.0)
                if rowsv is None:
                    for b in range(2):
                        dve.memset(a[b][:], 0.0)
                if save is not None and sw > D:
                    for b in range(2):
                        dve.memset(z[b][:], 0.0)
                dve.drain()

                def clear(b):
                    if gather is not None:
                        if gat:
                            dve.memset(g[b][:, :, 0:D + heads], 0.0)
                            dve.memset(g[b][:, :, D + heads:gw], -BIG).then_inc(s_clr, 1)
                        else:
                            dve.memset(g[b][:], 0.0).then_inc(s_clr, 1)

                if gather is None:
                    dve.sem_inc(s_clr, 2)
                clear(0)
                clear(1)

                def combine(t):
                    at, gt, ut = a[t.par], g[t.par], u[t.par]
                    if loops:
                        dve.tensor_copy(lp[:, 0, :], S["loop"][:, bass.ds(t.n * J, J)])
                        dve.tensor_copy(lp[:, 1, :], S["loopcut"][:, bass.ds(t.n * J, J)])
                    dve.tensor_tensor(e[:], at[:, :, D:D + heads], at[:, :, D + heads:D + 2 * heads], ALU.add)
                    dve.drain()
                    dve.scalar_tensor_tensor(e[:], e[:], SLOPE, e[:], ALU.mult, ALU.max)
                    dve.drain()
                    if loops:
                        dve.tensor_tensor(e[:], e[:], spread(lp[:, 0, :], heads), ALU.mult)
                        dve.drain()
                        dve.tensor_tensor(e[:], e[:], spread(lp[:, 1, :], heads), ALU.add)
                        dve.drain()
                    gm = gt[:, :, D + heads:D + 2 * heads]
                    dve.tensor_tensor(mm[:], e[:], gm, ALU.max)
                    dve.drain()
                    dve.tensor_tensor(ex[t.par][:, 0], e[:], mm[:], ALU.subtract)
                    dve.tensor_tensor(ex[t.par][:, 1], gm, mm[:], ALU.subtract).then_inc(s_ex, 1)
                    dve.wait_ge(s_wt, t.n + 1)
                    w = wt[t.par]
                    if loops:
                        dve.tensor_tensor(w[:, 0], w[:, 0], spread(lp[:, 0, :], heads), ALU.mult)
                    dve.tensor_tensor(den[:], gt[:, :, D:D + heads], w[:, 1], ALU.mult)
                    dve.drain()
                    dve.tensor_tensor(d2[:], den[:], w[:, 0], ALU.add)
                    dve.drain()
                    dve.tensor_scalar(d2[:], d2[:], 1e-30, None, ALU.max)
                    dve.drain()
                    dve.reciprocal(d2[:], d2[:])
                    dve.drain()
                    dve.tensor_tensor(w[:, 0], w[:, 0], d2[:], ALU.mult)
                    dve.tensor_tensor(w[:, 1], w[:, 1], d2[:], ALU.mult)
                    dve.drain()
                    hv = lambda x: x[:, :, 0:D].rearrange("p j (h c) -> p j h c", h=heads)
                    dve.tensor_tensor(hv(v), hv(at), spread(w[:, 0], hw), ALU.mult)
                    dve.tensor_tensor(hv(ut), hv(gt), spread(w[:, 1], hw), ALU.mult)
                    dve.drain()
                    dve.tensor_tensor(ut[:], ut[:], v[:], ALU.add)
                    dve.drain()
                    dve.tensor_tensor(ut[:], ut[:], bias[:].unsqueeze(1).to_broadcast([P, J, D]), ALU.add)
                    dve.drain()
                    if elu:
                        dve.tensor_scalar(en[t.par][:], ut[:], 0.0, None, ALU.min).then_inc(s_en, 1)

                def part1(t):
                    if bn:
                        dve.wait_ge(s_yt, t.n + 1)
                    if gather is not None:
                        dve.wait_ge(s_g[t.par], (t.half + 1) * 16 * J)
                    dve.wait_ge(s_in[t.par], (t.half + 1) * 16 * nin)
                    at, ut = a[t.par], u[t.par]
                    target = ut
                    if not norm:
                        target = z[t.par]
                        if not t.before(2):
                            dve.wait_ge(s_t, t.n - 1)
                    if gat:
                        combine(t)
                        if elu:
                            dve.tensor_scalar(ut[:], ut[:], 0.0, -1.0, ALU.max, ALU.add)
                            dve.drain()
                            dve.wait_ge(s_ee, t.n + 1)
                            dve.tensor_tensor(target[:, :, 0:D], ut[:], ee[t.par][:], ALU.add)
                            dve.drain()
                    elif kind == "sum":
                        dve.tensor_scalar(sc[:], r[t.par][:, :, D], 1.0, None, ALU.max)
                        dve.drain()
                        dve.reciprocal(sc[:], sc[:])
                        dve.drain()
                        dve.tensor_tensor(ut[:], r[t.par][:, :, 0:D], spread(sc[:], D), ALU.mult)
                        dve.drain()
                        dve.tensor_tensor(ut[:], ut[:], at[:, :, 0:D], ALU.add)
                        dve.drain()
                    elif gcn:
                        dve.tensor_copy(sc[:], S["dinv"][:, bass.ds(t.n * J, J)])
                        dve.drain()
                        dve.tensor_tensor(ut[:], at[:, :, 0:D], spread(sc[:], D), ALU.mult)
                        dve.drain()
                        dve.tensor_tensor(ut[:], ut[:], g[t.par][:], ALU.add)
                        dve.drain()
                        dve.tensor_tensor(target[:], ut[:], spread(sc[:], D), ALU.mult)
                        dve.drain()
                    elif bn:
                        dve.tensor_tensor(ut[:], at[:, :, 0:D], py[:].rearrange("p j k n -> p j (k n)"), ALU.add).then_inc(s_bs, 1)
                        dve.drain()
                    if extra is not None and kind != "sum":
                        dve.tensor_tensor(ut[:], ut[:], r[t.par][:, :, 0:D], ALU.add)
                        dve.drain()
                    dve.sem_inc(s_used, 1)
                    clear(t.par)
                    if norm:
                        for j in range(J):
                            dve.bn_stats(bs[:, j, :], ut[:, j, :])
                        dve.drain()
                        for j in range(J):
                            dve.bn_aggr(mv[t.par][:, j, :], bs[:, j, :])
                        dve.drain()
                        dve.tensor_scalar(ve[t.par][:], mv[t.par][:, :, 1], EPS, None, ALU.add).then_inc(s_var, 1)
                    else:
                        dve.sem_inc(s_z, 1)

                def part2(t):
                    ut, zz = u[t.par], z[t.par]
                    dve.wait_ge(s_rs, t.n + 1)
                    if not t.before(2):
                        if save is not None:
                            dve.wait_ge(s_zs[t.par], t.half * 16)
                        if weight is not None:
                            dve.wait_ge(s_t, t.n - 1)
                    for j in range(J):
                        last = dve.tensor_scalar(zz[:, j, 0:D], ut[:, j, :], mv[t.par][:, j, 0:1], rs[t.par][:, j:j + 1],
                                                 ALU.subtract, ALU.mult)
                    if sw > D:
                        dve.tensor_copy(zz[:, :, D], S["dinv"][:, bass.ds(t.n * J, J)])
                        last = dve.drain()
                    if affine is not None:
                        dve.drain()
                        dve.tensor_tensor(zz[:], zz[:], affine[0][:].unsqueeze(1).to_broadcast([P, J, D]), ALU.mult)
                        dve.drain()
                        dve.tensor_tensor(zz[:], zz[:], affine[1][:].unsqueeze(1).to_broadcast([P, J, D]), ALU.add)
                        dve.drain()
                        last = dve.tensor_scalar(zz[:], zz[:], 0.0, None, ALU.max)
                    last.then_inc(s_z, 1)

                def batch_stats(t):
                    dve.wait_ge(s_o, t.n + 1)
                    for m in range(KC):
                        if t.fixed and t.n == NB - 1:
                            view4 = o[t.par][:, m, :].rearrange("p (j n) -> p j n", n=P)[:, :, 0:TAILP]
                            last = dve.bn_stats(stats[:, m, t.n, :], view4)
                        else:
                            last = dve.bn_stats(stats[:, m, bass.ds(t.n, 1), :].rearrange("p n s -> p (n s)"), o[t.par][:, m, :])
                    last.then_inc(s_bs, 1)

                def step(t):
                    part1(t)
                    if norm and not t.before(1):
                        part2(t.back(1))
                    if gcn and not t.before(2):
                        batch_stats(t.back(2))

                over_blocks(dve, step, NB, peel=1)
                if norm:
                    part2(Step(NB - 1))
                if gcn:
                    batch_stats(Step(NB - 2))
                    batch_stats(Step(NB - 1))
                    dve.drain()
                    for m in range(KC):
                        dve.bn_aggr(bmv[:, m, :], stats[:, m].rearrange("p n s -> p (n s)"))
                    dve.drain()
                    dve.tensor_scalar(bmv[:, :, 1], bmv[:, :, 1], EPS, None, ALU.add).then_inc(s_fin, 1)
                    dve.wait_ge(s_frs, 1)
                    dve.tensor_tensor(S["bnscale"][:], bt[:, :, 0], S["c_L2_gnn_gamma"][:], ALU.mult)
                    dve.drain()
                    dve.tensor_tensor(bt[:, :, 1], bmv[:, :, 0], S["bnscale"][:], ALU.mult)
                    dve.drain()
                    dve.tensor_tensor(S["bnshift"][:], S["c_L2_gnn_beta"][:], bt[:, :, 1], ALU.subtract)


def gnn_kernel(nc, A, out):
    T = {
        "META": nc.dram_tensor("META", (NPAD, 2), I32).ap(),
        "NS0": nc.dram_tensor("NS0", (NPAD + P, SW), F32).ap(),
        "NS1": nc.dram_tensor("NS1", (NPAD + P, SW), F32).ap(),
        "HYP": nc.dram_tensor("HYP", (HB * BLK, D), F32).ap(),
        "SUMS": nc.dram_tensor("SUMS", (P * C, D), F32).ap(),
        "GSUMS": nc.dram_tensor("GSUMS", (P * C, RW), F32).ap(),
        "X1": nc.dram_tensor("X1", (NPAD, D), F32).ap(),
        "X2": nc.dram_tensor("X2", (NPAD, SW), F32).ap(),
        "X3": nc.dram_tensor("X3", (NPAD, D), F32).ap(),
        "HA": nc.dram_tensor("HA", (NPAD, RW), F32).ap(),
        "HBT": nc.dram_tensor("HBT", (NPAD, RW), F32).ap(),
        "AD": nc.dram_tensor("AD", (NPAD, 4), F32).ap(),
        "AD1": nc.dram_tensor("AD1", (NPAD, 1), F32).ap(),
        "AGG": nc.dram_tensor("AGG", (P, KC, NPAD), F32).ap(),
    }
    with Scope(nc, "k") as s:
        S = {"AGG": T["AGG"], "passed": s.sem("passed"),
             "scope": s}
        for name, shape, dt in (
            ("src32", [P, C], I32), ("dst32", [P, C], I32), ("hyp32", [P, C], I32), ("skey", [P, C], F32),
            ("same", [P, C], F32), ("cut", [P, C], F32), ("repair32", [P, 1], I32), ("dummy32", [P, 1], I32),
            ("dummy", [P, 1], F32), ("last32", [P, NB * J], I32), ("deg", [P, NB * J], F32), ("dinv", [P, NB * J], F32),
            ("einv", [P, HB * J], F32), ("loop", [P, NB * J], F32), ("loopcut", [P, NB * J], F32),
            ("ident", [P, P], F32), ("ones", [P, P], F32), ("upper", [P, P], F32), ("lower", [P, P], F32),
            ("join", [P, P], F32), ("joinT", [P, P], F32), ("joincut", [P, P], F32), ("minus_half", [P, 64], F32),
            ("tail", [P, RW], F32), ("bnscale", [P, KC], F32), ("bnshift", [P, KC], F32), ("w_L2", [P, KC, D], F32),
        ):
            S[name] = s.sb(name, shape, dt)
        S["weights"] = {"n2e0": A["L0_gnn_W0_n2e"], "e2n0": A["L0_gnn_W0_e2n"], "n2e1": A["L0_gnn_W1_n2e"],
                        "e2n1": A["L0_gnn_W1_e2n"], "L1a": A["L1_gnn_W1"], "L1b": A["L1_gnn_W2"],
                        "L3a": A["L3_gnn_W1"], "L3b": A["L3_gnn_W2"]}
        for name in S["weights"]:
            S["w_" + name] = s.sb("w_" + name, [P, KC, RW])
        for name in ROWS:
            S["r_" + name] = s.sb("r_" + name, [P, D])
        for name in COLS:
            S["c_" + name] = s.sb("c_" + name, [P, KC])

        setup_phase(nc, S, A, T)
        last_weight_phase(nc, S, A)
        edge_phase(nc, S, "e0", A["x"], D, T["SUMS"], D)
        repair_phase(nc, S, "f0", T["SUMS"], D)
        hyper_phase(nc, S, "h0", T["SUMS"], S["w_n2e0"], S["w_e2n0"], T["HYP"])
        source_sum_phase(nc, S, "s0", T["HYP"], T["NS0"])
        edge_phase(nc, S, "e1", T["NS0"], SW, T["SUMS"], D, scale="inverse")
        repair_phase(nc, S, "f1", T["SUMS"], D)
        hyper_phase(nc, S, "h1", T["SUMS"], S["w_n2e1"], S["w_e2n1"], T["HYP"])
        source_sum_phase(nc, S, "s1", T["HYP"], T["NS1"])
        node_phase(nc, S, "n0", A["x"], D, extra=T["NS1"], ew=SW, kind="sum", norm=True, save=T["X1"],
                   weight=S["w_L1a"], oheads=4, out=T["HA"], ad=T["AD"])
        edge_phase(nc, S, "e2", T["HA"], RW, T["GSUMS"], RW, heads=4, ad=T["AD"])
        repair_phase(nc, S, "f2", T["GSUMS"], RW, heads=4)
        node_phase(nc, S, "n1", T["HA"], RW, gather=T["GSUMS"], gw=RW, heads=4, kind="gat", bias=S["r_L1_gnn_b1"],
                   elu=True, weight=S["w_L1b"], oheads=4, out=T["HBT"], ad=T["AD"])
        edge_phase(nc, S, "e3", T["HBT"], RW, T["GSUMS"], RW, heads=4, ad=T["AD"])
        repair_phase(nc, S, "f3", T["GSUMS"], RW, heads=4)
        node_phase(nc, S, "n2", T["HBT"], RW, extra=T["X1"], gather=T["GSUMS"], gw=RW, heads=4, kind="gat",
                   bias=S["r_L1_gnn_b2"], elu=True, norm=True, save=T["X2"], sw=SW)
        edge_phase(nc, S, "e4", T["X2"], SW, T["SUMS"], D, scale="plain")
        repair_phase(nc, S, "f4", T["SUMS"], D)
        node_phase(nc, S, "n3", T["X2"], SW, gather=T["SUMS"], gw=D, kind="gcn", weight=S["w_L2"])
        node_phase(nc, S, "n4", T["X2"], SW, kind="bn", norm=True, save=T["X3"], weight=S["w_L3a"], oheads=4,
                   out=T["HA"], ad=T["AD"])
        edge_phase(nc, S, "e5", T["HA"], RW, T["GSUMS"], RW, heads=4, ad=T["AD"])
        repair_phase(nc, S, "f5", T["GSUMS"], RW, heads=4)
        node_phase(nc, S, "n5", T["HA"], RW, gather=T["GSUMS"], gw=RW, heads=4, kind="gat", bias=S["r_L3_gnn_b1"],
                   loops=True, norm=True, affine=(S["r_L3_gnn_ln_g"], S["r_L3_gnn_ln_b"]), weight=S["w_L3b"],
                   oheads=1, out=T["HBT"], ad=T["AD1"])
        edge_phase(nc, S, "e6", T["HBT"], RW, T["GSUMS"], RW, heads=1, ad=T["AD1"])
        repair_phase(nc, S, "f6", T["GSUMS"], RW, heads=1)
        node_phase(nc, S, "n6", T["HBT"], RW, extra=T["X3"], gather=T["GSUMS"], gw=RW, heads=1, kind="gat",
                   bias=S["r_L3_gnn_b2"], loops=True, norm=True, save=out, final=True)


_INS = ["x", "src", "dst", "L0_gnn_W0_n2e", "L0_gnn_W0_e2n", "L0_gnn_W1_n2e", "L0_gnn_W1_e2n", "L1_gnn_W1",
        "L1_gnn_att_src1", "L1_gnn_att_dst1", "L1_gnn_b1", "L1_gnn_W2", "L1_gnn_att_src2", "L1_gnn_att_dst2",
        "L1_gnn_b2", "L2_gnn_W", "L2_gnn_b", "L2_gnn_gamma", "L2_gnn_beta", "L3_gnn_W1", "L3_gnn_a1_src",
        "L3_gnn_a1_dst", "L3_gnn_b1", "L3_gnn_ln_g", "L3_gnn_ln_b", "L3_gnn_W2", "L3_gnn_a2_src", "L3_gnn_a2_dst",
        "L3_gnn_b2"]


def kernel(**inputs):
    import numpy as _np
    import concourse.bacc as _bacc
    from concourse import mybir as _mybir
    from concourse.bass_utils import run_bass_kernel_spmd as _run

    nc = _bacc.Bacc("TRN2", target_bir_lowering=False, num_devices=1)
    arrays, aps = {}, {}
    for name in _INS:
        a = _np.ascontiguousarray(inputs[name])
        arrays[f"in_{name}_dram"] = a
        aps[name] = nc.dram_tensor(f"in_{name}_dram", a.shape, _mybir.dt.from_np(a.dtype), kind="ExternalInput").ap()
    out = nc.dram_tensor("out_0_dram", (N, D), _mybir.dt.from_np(_np.dtype("float32")), kind="ExternalOutput").ap()
    gnn_kernel(nc, aps, out)
    r = _run(nc, [arrays], core_ids=[0])
    return r.results[0]["out_0_dram"]
```

```python
from contextlib import ExitStack

import concourse.bass as bass
from concourse import mybir

F32 = mybir.dt.float32
I32 = mybir.dt.int32
ALU = mybir.AluOpType
ACT = mybir.ActivationFunctionType
AX_X = mybir.AxisListType.X

P = 128
N = 50000
E = 25000
D = 256
KC = D // P
J = 4
BLK = P * J
U = 3
NREAL = -(-N // BLK)
NB = -(-NREAL // U) * U
NPAD = NB * BLK
TAILN = NREAL - 1
TAIL0 = TAILN * BLK
TAILP = (N - TAIL0) // J
NHYP = 20000
HB = NHYP // BLK + 1
HB += HB % 2
C = -(-E // P)
LASTRUN = E - (P - 1) * C
BC = 14
NBAT = C // BC
RW = 264
SW = 260
NONE = 60000
BIG = 1e30
EPS = 1e-5
SLOPE = 0.2
assert C == BC * NBAT and NBAT % 2 == 0 and TAILP * J + TAIL0 == N


class Step:

    def __init__(self, n, u, turn=None, slot=None):
        self.fixed = turn is None
        self.n, self.u = n, u
        self.turn = n // u if self.fixed else turn
        self.slot = n % u if self.fixed else slot

    def back(self, k):
        if self.fixed:
            return Step(self.n - k, self.u)
        return Step(self.n - k, self.u, self.turn - (k - self.slot + self.u - 1) // self.u, (self.slot - k) % self.u)

    def before(self, k):
        return self.fixed and self.n < k

    def real(self, k, blocks=None):
        return not self.fixed or 0 <= self.n - k < (blocks or NB)


def over_blocks(eng, step, blocks, lag=0, u=U, first=None, last=None):
    first = -(-(u + lag) // u) * u if first is None else first
    last = (TAILN // u) * u if last is None else last
    for n in range(first):
        step(Step(n, u))
    with eng.Fori(first // u, last // u) as i:
        for k in range(u):
            step(Step(i * u + k, u, i, k))
    for n in range(last, blocks + lag):
        step(Step(n, u))


class Chain:

    def __init__(self, eng, sem, per):
        self.eng, self.sem, self.per = eng, sem, per

    def start(self, t):
        self.base, self.k = t.n * self.per, 0

    def link(self, ins):
        ins.then_inc(self.sem, 1)
        self.k += 1

    def settle(self):
        value = self.base + self.k
        if not (isinstance(value, int) and value == 0):
            self.eng.wait_ge(self.sem, value)

    def stop(self):
        assert self.k == self.per


def hold(eng, passed, sem, value):
    eng.wait_ge(sem, value)
    if not isinstance(value, int):
        eng.sem_inc(passed, 1)


def spread(ap, k):
    return ap.unsqueeze(len(ap.shape)).to_broadcast([*ap.shape, k])


class Scope:

    def __init__(self, nc, tag):
        self.nc, self.tag, self.ctx, self.used = nc, tag, ExitStack(), []

    def __enter__(self):
        return self

    def __exit__(self, *a):
        with self.nc.Block() as block:

            @block.sync
            def _(sp):
                for sem in self.used:
                    sp.sem_clear(sem)

        self.ctx.__exit__(*a)

    def sb(self, name, shape, dt=F32):
        return self.ctx.enter_context(self.nc.sbuf_tensor(f"{self.tag}_{name}", shape, dt))

    def ps(self, name, shape, dt=F32):
        return self.ctx.enter_context(self.nc.psum_tensor(f"{self.tag}_{name}", shape, dt))

    def sem(self, name):
        self.used.append(self.ctx.enter_context(self.nc.semaphore(f"{self.tag}_{name}")))
        return self.used[-1]

    def pool_sem(self, S, name):
        return S["scope"].ctx.enter_context(self.nc.semaphore(f"{self.tag}_{name}"))

    def sems(self, name):
        return [self.sem(f"{name}{b}") for b in range(2)]

    def block(self):
        return self.nc.Block()


def setup_phase(nc, S, A, T):
    with Scope(nc, "su") as s:
        dnext32 = s.sb("dnext32", [P, C], I32)
        skey32 = s.sb("skey32", [P, C], I32)
        df = s.sb("df", [P, C])
        dnextf = s.sb("dnextf", [P, C])
        t1 = s.sb("t1", [P, C])
        head = s.sb("head", [P, C])
        cnt = s.sb("cnt", [P, C])
        ones_c = s.sb("ones_c", [P, C])
        pos = s.sb("pos", [P, C], I32)
        hpos = s.sb("hpos", [P, 1], I32)
        midx = s.sb("midx", [P, C], I32)
        meta = s.sb("meta", [P, C, 2], I32)
        empty = s.sb("empty", [P, NPAD // P, 2], I32)
        diag = s.sb("diag", [P, 2, P])
        small = s.sb("small", [P, 8])
        att = s.sb("att", [P, 6, D])
        prod = s.sb("prod", [P, D])
        wraw = s.sb("wraw", [P, KC, D])
        nodeid = s.sb("nodeid", [P, NB * J], I32)
        msb = s.sb("msb", [P, NB, J * 2], I32)
        kb = s.ps("kb", [P, 2, P])
        carry = s.ps("carry", [P, 1])
        wt = s.ps("wt", [P, KC, 2, P])
        s_fill = s.sem("filled")
        s_ld = s.sem("edges_loaded")
        s_w = s.sem("weights_loaded")
        s_iota = s.sem("iotas")
        s_id = s.sem("identity")
        s_diag = s.sem("diagonals")
        s_kb = s.sem("keys_spread")
        s_m = s.sem("join_ready")
        s_car = s.sem("count_carried")
        s_meta = s.sem("meta_ready")
        s_emp = s.sem("empty_ready")
        s_pre = s.sem("meta_prefilled")
        s_sc = s.pool_sem(S, "meta_scattered")
        s_mld = s.sem("meta_loaded")
        s_wt = s.sem("w_transposed")
        s_cn = s.sem("counts_ready")
        s_zero = s.sem("zero_rows_ready")
        s_zs = s.sem("sums_zeroed")
        s_wld = s.sem("wraw_loaded")
        zero = s.sb("zero", [P, 8, SW])
        with s.block() as block:

            @block.sync
            def _(sp):
                sp.wait_ge(s_fill, 1)
                src, dst = A["src"], A["dst"]
                full = (P - 1) * C
                for tile, ap, off in ((S["src32"], src, 0), (skey32, src, 0), (S["dst32"], dst, 0), (dnext32, dst, 1)):
                    sp.dma_start(tile[0:P - 1, :], ap[off:off + full].rearrange("(p c) -> p c", c=C)).then_inc(s_ld, 16)
                    sp.dma_start(tile[P - 1:P, 0:LASTRUN - off],
                                 ap[off + full:E].rearrange("(p c) -> p c", p=1)).then_inc(s_ld, 16)
                sp.wait_ge(s_emp, 1)
                sp.dma_start(T["META"].rearrange("(p r) c -> p (r c)", p=P), empty[:].rearrange("p r c -> p (r c)")).then_inc(s_pre, 16)
                for k, (name, ap) in enumerate(S["weights"].items()):
                    sp.dma_start(S["w_" + name][:, :, 0:D], ap.rearrange("(k p) n -> p k n", p=P)).then_inc(s_w, 16)
                sp.dma_start(wraw[:], A["L2_gnn_W"].rearrange("(k p) n -> p k n", p=P)).then_inc(s_wld, 16)
                for k, name in enumerate(ATT):
                    sp.dma_start(att[:, k, :], A[name].rearrange("h c -> (h c)").partition_broadcast(P)).then_inc(s_w, 16)
                for name in ROWS:
                    sp.dma_start(S["r_" + name][:], A[name].partition_broadcast(P)).then_inc(s_w, 16)
                for name in COLS:
                    sp.dma_start(S["c_" + name][:], A[name].rearrange("(k p) -> p k", p=P),
                                 allow_slow_non_contiguous=True).then_inc(s_w, 16)
                sp.wait_ge(s_zero, 1)
                for t in ("NS0", "NS1"):
                    rows = T[t].shape[0] // P
                    v = T[t].rearrange("(p r) c -> p r c", p=P)
                    for r in range(0, rows, 8):
                        k = min(8, rows - r)
                        sp.dma_start(v[:, r:r + k, :], zero[:, 0:k, :]).then_inc(s_zs, 16)
                sp.wait_ge(s_sc, 16 * C)
                sp.dma_start(msb[:], T["META"].rearrange("(n p j) c -> p n (j c)", p=P, j=J)).then_inc(s_mld, 16)
                sp.wait_ge(s_mld, 16)
                sp.wait_ge(s_zs, 16 * 2 * -(-(T["NS0"].shape[0] // P) // 8))

            @block.gpsimd
            def _(pool):
                pool.iota(pos[:], [[1, C]], base=0, channel_multiplier=C).then_inc(s_iota, 1)
                pool.iota(hpos[:], [[1, 1]], base=-1, channel_multiplier=C).then_inc(s_iota, 1)
                pool.iota(S["dummy32"][:], [[1, 1]], base=NPAD, channel_multiplier=1).then_inc(s_iota, 1)
                pool.iota(nodeid[:], [[BLK, NB], [1, J]], base=0, channel_multiplier=J).then_inc(s_iota, 1)
                pool.memset(S["ones"][:], 1.0)
                pool.memset(S["minus_half"][:], -0.5)
                pool.memset(zero[:], 0.0).then_inc(s_zero, 1)
                pool.drain()
                pool.affine_select(out=S["ident"][:], in_=S["ones"][:], compare_op=ALU.is_equal, fill=0.0, base=0,
                                   pattern=[[1, P]], channel_multiplier=-1)
                pool.affine_select(out=S["upper"][:], in_=S["ones"][:], compare_op=ALU.is_gt, fill=0.0, base=0,
                                   pattern=[[1, P]], channel_multiplier=-1)
                pool.affine_select(out=S["lower"][:], in_=S["ones"][:], compare_op=ALU.is_gt, fill=0.0, base=0,
                                   pattern=[[-1, P]], channel_multiplier=1).then_inc(s_id, 1)
                pool.wait_ge(s_meta, 1)
                pool.wait_ge(s_pre, 16)
                for c in range(C):
                    pool.indirect_dma_start(out=T["META"], out_offset=bass.IndirectOffsetOnAxis(ap=midx[:, c:c + 1], axis=0),
                                            in_=meta[:, c, :], in_offset=None, bounds_check=N - 1,
                                            oob_is_err=False).then_inc(s_sc, 16)
                pool.wait_ge(s_cn, 1)
                for k in range(0, NB * J, J * 14):
                    w = min(J * 14, NB * J - k)
                    pool.tensor_tensor(S["dinv"][:, k:k + w], S["deg"][:, k:k + w], S["minus_half"][:, 0:w], ALU.pow)

            @block.tensor
            def _(pe):
                pe.wait_ge(s_id, 1)
                pe.wait_ge(s_diag, 1)
                for k in range(2):
                    last = pe.matmul(kb[:, k, :], S["ones"][:, :], diag[:, k, :], start=True, stop=True)
                last.then_inc(s_kb, 1)
                pe.wait_ge(s_wld, 16)
                for k in range(KC):
                    for m in range(KC):
                        last = pe.transpose(wt[:, k, m, :], wraw[:, m, k * P:(k + 1) * P], S["ident"][:])
                last.then_inc(s_wt, 1)
                pe.wait_ge(s_m, 1)
                pe.matmul(carry[:], S["join"][:], cnt[:, C - 1:C], start=True, stop=True).then_inc(s_car, 1)

            @block.vector
            def _(dve):
                dve.memset(S["src32"][:], 0)
                dve.memset(skey32[:], N)
                dve.memset(S["dst32"][:], NONE)
                dve.memset(dnext32[:], NONE)
                dve.drain().then_inc(s_fill, 1)
                dve.memset(empty[:, :, 0:1], NONE)
                dve.memset(empty[:, :, 1:2], 0)
                dve.memset(ones_c[:], 1.0)
                dve.drain().then_inc(s_emp, 1)
                dve.wait_ge(s_ld, 16 * 8)
                dve.wait_ge(s_iota, 4)
                dve.tensor_copy(df[:], S["dst32"][:])
                dve.tensor_copy(dnextf[:], dnext32[:])
                dve.tensor_copy(S["skey"][:], skey32[:])
                dve.tensor_copy(S["dummy"][:], S["dummy32"][:])
                dve.memset(S["same"][:, 0:1], 0.0)
                dve.drain()
                dve.tensor_tensor(S["same"][:, 1:C], df[:, 1:C], df[:, 0:C - 1], ALU.is_equal)
                dve.tensor_scalar(head[:], df[:], df[:, 0:1], None, ALU.is_equal)
                dve.tensor_scalar(t1[:], df[:], float(NHYP - 1), None, ALU.min)
                dve.drain()
                dve.tensor_copy(S["hyp32"][:], t1[:])
                dve.tensor_scalar(S["cut"][:], S["same"][:], BIG, -BIG, ALU.mult, ALU.add)
                dve.tensor_tensor_scan(cnt[:], S["same"][:], ones_c[:], 0.0, ALU.mult, ALU.add)
                dve.tensor_reduce(small[:, 0:1], head[:], AX_X, ALU.add)
                dve.wait_ge(s_id, 1)
                dve.tensor_scalar(diag[:, 0, :], S["ident"][:], df[:, 0:1], None, ALU.mult)
                dve.tensor_scalar(diag[:, 1, :], S["ident"][:], df[:, C - 1:C], None, ALU.mult)
                dve.drain().then_inc(s_diag, 1)
                dve.wait_ge(s_kb, 1)
                dve.scalar_tensor_tensor(S["join"][:], kb[:, 0, :], df[:, C - 1:C], S["upper"][:], ALU.is_equal, ALU.mult)
                dve.scalar_tensor_tensor(S["joinT"][:], kb[:, 1, :], df[:, 0:1], S["lower"][:], ALU.is_equal, ALU.mult)
                dve.drain().then_inc(s_m, 1)
                dve.tensor_scalar(S["joincut"][:], S["joinT"][:], BIG, -BIG, ALU.mult, ALU.add)
                dve.wait_ge(s_car, 1)
                dve.tensor_copy(small[:, 1:2], carry[:])
                dve.tensor_copy(small[:, 2:3], hpos[:])
                dve.drain()
                dve.scalar_tensor_tensor(t1[:], head[:], small[:, 1:2], cnt[:], ALU.mult, ALU.add)
                dve.tensor_scalar(small[:, 3:4], small[:, 1:2], 0.0, None, ALU.is_gt)
                dve.tensor_tensor(small[:, 4:5], small[:, 0:1], small[:, 2:3], ALU.add)
                dve.tensor_copy(meta[:, :, 0:1].rearrange("p c o -> p (c o)"), pos[:])
                dve.drain()
                dve.tensor_scalar(small[:, 5:6], small[:, 4:5], float(-NONE), None, ALU.add)
                dve.tensor_copy(meta[:, :, 1:2].rearrange("p c o -> p (c o)").bitcast(F32), t1[:])
                dve.tensor_tensor(head[:], dnextf[:], df[:], ALU.not_equal)
                dve.tensor_scalar(cnt[:], df[:], float(-NONE), None, ALU.add)
                dve.drain()
                dve.tensor_tensor(small[:, 6:7], small[:, 5:6], small[:, 3:4], ALU.mult)
                dve.tensor_tensor(cnt[:], cnt[:], head[:], ALU.mult)
                dve.drain()
                dve.tensor_scalar(small[:, 7:8], small[:, 6:7], float(NONE), None, ALU.add)
                dve.tensor_scalar(cnt[:], cnt[:], float(NONE), None, ALU.add)
                dve.drain()
                dve.tensor_copy(S["repair32"][:], small[:, 7:8])
                dve.tensor_copy(midx[:], cnt[:])
                dve.drain().then_inc(s_meta, 1)
                dve.wait_ge(s_w, 16 * (len(S["weights"]) + len(ATT) + len(ROWS) + len(COLS)))
                for w, heads, a in (("L1a", 4, 0), ("L1b", 4, 2), ("L3a", 4, 4)):
                    for k in range(KC):
                        for v in range(2):
                            dve.tensor_tensor(prod[:], S["w_" + w][:, k, 0:D], att[:, a + v, :], ALU.mult)
                            dve.drain()
                            dve.tensor_reduce(S["w_" + w][:, k, D + v * heads:D + (v + 1) * heads],
                                              prod[:].rearrange("p (h c) -> p h c", h=heads), AX_X, ALU.add)
                            dve.drain()
                dve.wait_ge(s_wt, 1)
                dve.tensor_copy(S["w_L2"][:].rearrange("p k (m n) -> p k m n", m=KC), wt[:])
                dve.wait_ge(s_mld, 16)
                mv = msb[:].rearrange("p n (j c) -> p n j c", c=2)
                dve.tensor_copy(S["last32"][:].rearrange("p (n j) -> p n j", j=J), mv[:, :, :, 0])
                dve.tensor_scalar(S["deg"][:].rearrange("p (n j) -> p n j", j=J), mv[:, :, :, 1].bitcast(F32), 1.0, None, ALU.add)
                dve.tensor_scalar(S["einv"][:].rearrange("p (n j) -> p n j", j=J),
                                  mv[:, 0:HB, :, 1].bitcast(F32), 1.0, None, ALU.max)
                dve.tensor_scalar(S["has"][:].rearrange("p (n j) -> p n j", j=J), mv[:, :, :, 1].bitcast(F32), 1.0, None, ALU.min)
                dve.tensor_copy(S["loop"][:], nodeid[:])
                dve.drain().then_inc(s_cn, 1)
                dve.reciprocal(S["einv"][:], S["einv"][:])
                dve.memset(S["minus_one"][:], -1.0)
                dve.tensor_scalar(S["r1_L1_gnn_b2"][:], S["r_L1_gnn_b2"][:], 1.0, None, ALU.add)
                dve.tensor_scalar(S["loop"][:], S["loop"][:], float(NHYP), None, ALU.is_lt)
                dve.drain()
                dve.tensor_scalar(S["loopcut"][:], S["loop"][:], BIG, -BIG, ALU.mult, ALU.add)
                dve.tensor_tensor(S["einv"][:], S["einv"][:], S["has"][:, 0:HB * J], ALU.mult)


ATT = ("L1_gnn_att_src1", "L1_gnn_att_dst1", "L1_gnn_att_src2", "L1_gnn_att_dst2", "L3_gnn_a1_src", "L3_gnn_a1_dst")
ATT1 = ("L3_gnn_a2_src", "L3_gnn_a2_dst")
ROWS = ("L1_gnn_b2", "L3_gnn_b1", "L3_gnn_b2")
COLS = ("L1_gnn_b1", "L2_gnn_b", "L2_gnn_gamma", "L2_gnn_beta", "L3_gnn_ln_g", "L3_gnn_ln_b")


def last_weight_phase(nc, S, A):
    with Scope(nc, "lw") as s:
        att = s.sb("att", [P, 2, D])
        prod = s.sb("prod", [P, D])
        s_att = s.sem("att_loaded")
        with s.block() as block:

            @block.sync
            def _(sp):
                for k, name in enumerate(ATT1):
                    sp.dma_start(att[:, k, :], A[name].rearrange("h c -> (h c)").partition_broadcast(P)).then_inc(s_att, 16)

            @block.vector
            def _(dve):
                dve.wait_ge(s_att, 32)
                for k in range(KC):
                    for v in range(2):
                        dve.tensor_tensor(prod[:], S["w_L3b"][:, k, 0:D], att[:, v, :], ALU.mult)
                        dve.drain()
                        dve.tensor_reduce(S["w_L3b"][:, k, D + v:D + v + 1], prod[:], AX_X, ALU.add)
                        dve.drain()
                dve.memset(S["w_L3b"][:, :, D + 2:RW], 0.0)


def edge_phase(nc, S, tag, table, tw, acc, aw, scale=None, heads=0, ad=None):
    with Scope(nc, tag) as s:
        g = [s.sb(f"g{b}", [P, BC, tw]) for b in range(2)]
        run = [s.sb(f"run{b}", [P, BC + 1, aw]) for b in range(2)]
        st = [s.sb(f"st{b}", [P, BC], I32) for b in range(2)]
        s_st = s.sem("indices_staged")
        s_g = [s.pool_sem(S, f"rows_gathered{b}") for b in range(2)]
        s_gf = s.sem("rows_used")
        s_run = s.sem("run_ready")
        s_sv = s.sems("run_stored")
        s_ex = s.sem("exponents_ready")
        s_w = s.sem("weights_ready")
        if heads:
            std = [s.sb(f"std{b}", [P, BC], I32) for b in range(2)]
            adg = [s.sb(f"adg{b}", [P, BC, heads]) for b in range(2)]
            e = s.sb("e", [P, heads, BC])
            mx = s.sb("mx", [P, heads, BC + 1])
            ex = [s.sb(f"ex{b}", [P, 2, heads, BC]) for b in range(2)]
            wd = [s.sb(f"wd{b}", [P, 2, heads, BC]) for b in range(2)]
            s_init = s.sem("ad_cleared")
        else:
            inv = s.sb("inv", [P, BC])
        accv = acc.rearrange("(p c) w -> p c w", c=C)
        hw = D // heads if heads else D
        per = 2 if heads else 1
        with s.block() as block:

            @block.gpsimd
            def _(pool):
                if heads:
                    pool.wait_ge(s_init, 1)

                def step(t):
                    if not t.before(2):
                        hold(pool, S["passed"], s_gf, t.n - 1)
                    pool.tensor_copy(st[t.slot][:], S["src32"][:, bass.ds(t.n * BC, BC)]).then_inc(s_st, 1)
                    if heads:
                        pool.tensor_copy(std[t.slot][:], S["dst32"][:, bass.ds(t.n * BC, BC)]).then_inc(s_st, 1)
                    hold(pool, S["passed"], s_st, (t.n + 1) * per)
                    for k in range(BC):
                        pool.indirect_dma_start(out=g[t.slot][:, k, :], out_offset=None, in_=table,
                                                in_offset=bass.IndirectOffsetOnAxis(ap=st[t.slot][:, k:k + 1], axis=0),
                                                bounds_check=table.shape[0] - 1, oob_is_err=False).then_inc(s_g[t.slot], 16)
                        if heads:
                            pool.indirect_dma_start(out=adg[t.slot][:, k, :], out_offset=None, in_=ad,
                                                    in_offset=bass.IndirectOffsetOnAxis(ap=std[t.slot][:, k:k + 1], axis=0),
                                                    bounds_check=ad.shape[0] - 1, oob_is_err=False).then_inc(s_g[t.slot], 16)

                over_blocks(pool, step, NBAT, u=2, first=2, last=NBAT)

            @block.vector
            def _(dve):
                dve.memset(run[1][:], 0.0)
                if heads:
                    dve.memset(run[0][:], 0.0)
                    dve.memset(mx[:], -BIG)
                    for b in range(2):
                        dve.memset(adg[b][:], 0.0)
                    dve.drain().then_inc(s_init, 1)
                else:
                    dve.drain()

                def step(t):
                    gt, rt, ro = g[t.slot], run[t.slot], run[1 - t.slot]
                    dve.wait_ge(s_g[t.slot], (t.turn + 1) * 16 * BC * per)
                    if not t.before(2):
                        dve.wait_ge(s_sv[t.slot], t.turn * 16)
                    dve.tensor_copy(rt[:, 0, :], ro[:, BC, :])
                    if heads:
                        dve.tensor_copy(mx[:, :, 0:1], mx[:, :, BC:BC + 1])
                        dve.tensor_tensor(e[:], gt[:, :, D:D + heads].rearrange("p c h -> p h c"),
                                          adg[t.slot][:].rearrange("p c h -> p h c"), ALU.add)
                        dve.drain()
                        dve.scalar_tensor_tensor(e[:], e[:], SLOPE, e[:], ALU.mult, ALU.max)
                        dve.tensor_copy(wd_cut[:], S["cut"][:, bass.ds(t.n * BC, BC)])
                        dve.drain()
                        for h in range(heads):
                            dve.tensor_tensor_scan(mx[:, h, 1:BC + 1], wd_cut[:], e[:, h, :], mx[:, h, 0:1], ALU.add, ALU.max)
                        dve.drain()
                        dve.tensor_tensor(ex[t.slot][:, 0], e[:], mx[:, :, 1:BC + 1], ALU.subtract)
                        dve.tensor_tensor(ex[t.slot][:, 1], mx[:, :, 0:BC], mx[:, :, 1:BC + 1], ALU.subtract)
                        dve.drain()
                        for h in range(heads):
                            last = dve.tensor_tensor(ex[t.slot][:, 1, h, :], ex[t.slot][:, 1, h, :], wd_cut[:], ALU.add)
                        last.then_inc(s_ex, 1)
                        dve.wait_ge(s_w, t.n + 1)
                        w, decay = wd[t.slot][:, 0], wd[t.slot][:, 1]
                        for h in range(heads):
                            dve.tensor_tensor_scan(rt[:, 1:BC + 1, D + h], decay[:, h, :], w[:, h, :],
                                                   rt[:, 0, D + h:D + h + 1], ALU.mult, ALU.add)
                        dve.tensor_copy(rt[:, 1:BC + 1, D + heads:D + 2 * heads],
                                        mx[:, :, 1:BC + 1].rearrange("p h c -> p c h"))
                        for h in range(heads):
                            dve.tensor_tensor(gt[:, :, h * hw:(h + 1) * hw], gt[:, :, h * hw:(h + 1) * hw],
                                              spread(w[:, h, :], hw), ALU.mult)
                        dve.drain()
                        for k in range(BC):
                            for h in range(heads):
                                f = slice(h * hw, (h + 1) * hw)
                                last = dve.scalar_tensor_tensor(rt[:, k + 1, f], rt[:, k, f], decay[:, h, k:k + 1],
                                                                gt[:, k, f], ALU.mult, ALU.add)
                            last = dve.drain()
                    else:
                        dve.tensor_copy(stsame[:], S["same"][:, bass.ds(t.n * BC, BC)])
                        if scale:
                            if scale == "inverse":
                                dve.tensor_scalar(inv[:], gt[:, :, D], 1.0, None, ALU.max)
                                dve.drain()
                                dve.reciprocal(inv[:], inv[:])
                            else:
                                dve.tensor_copy(inv[:], gt[:, :, D])
                            dve.drain()
                            dve.tensor_tensor(gt[:, :, 0:D], gt[:, :, 0:D], spread(inv[:], D), ALU.mult)
                            dve.drain()
                            if scale == "inverse":
                                dve.tensor_scalar(gt[:, :, 0:D], gt[:, :, 0:D], 0.0, None, ALU.max)
                        dve.drain()
                        for k in range(BC):
                            dve.scalar_tensor_tensor(rt[:, k + 1, :], rt[:, k, :], stsame[:, k:k + 1],
                                                     gt[:, k, 0:D], ALU.mult, ALU.add)
                            last = dve.drain()
                    last.then_inc(s_run, 1)
                    dve.sem_inc(s_gf, 1)

                if heads:
                    wd_cut = s.sb("cutb", [P, BC])
                else:
                    stsame = s.sb("sameb", [P, BC])
                over_blocks(dve, step, NBAT, u=2, first=2, last=NBAT)
                dve.tensor_copy(S["tail"][:, 0:aw], run[(NBAT - 1) % 2][:, BC, :])

            @block.scalar
            def _(act):
                if heads:
                    def step(t):
                        act.wait_ge(s_ex, t.n + 1)
                        act.activation(wd[t.slot][:], ex[t.slot][:], ACT.Exp).then_inc(s_w, 1)

                    over_blocks(act, step, NBAT, u=2, first=0, last=NBAT)

            @block.sync
            def _(sp):
                def step(t):
                    sp.wait_ge(s_run, t.n + 1)
                    sp.dma_start(accv[:, bass.ds(t.n * BC, BC), :], run[t.slot][:, 1:BC + 1, :]).then_inc(s_sv[t.slot], 16)

                over_blocks(sp, step, NBAT, u=2, first=0, last=NBAT)
                for b in range(2):
                    sp.wait_ge(s_sv[b], 16 * NBAT // 2)


def repair_phase(nc, S, tag, acc, aw, heads=0):
    with Scope(nc, tag) as s:
        row = s.sb("row", [P, aw])
        car = s.sb("car", [P, D + heads])
        pc = s.ps("pc", [P, 512])
        s_r0 = s.sem("row_cleared")
        s_row = s.pool_sem(S, "row_gathered")
        s_car = s.sem("carried")
        s_fix = s.sem("row_repaired")
        s_out = s.pool_sem(S, "row_scattered")
        if heads:
            dg = s.sb("dg", [P, heads, P])
            x = s.sb("x", [P, heads, P])
            ms = s.sb("ms", [P, heads])
            mn = s.sb("mn", [P, 2, heads])
            wt = s.sb("wt", [P, 2, heads])
            xt = s.sb("xt", [P, heads, P])
            pb = s.ps("pb", [P, heads, P])
            pt = s.ps("pt", [P, heads, P])
            s_dg = s.sem("diag_ready")
            s_pb = s.sem("max_spread")
            s_x = s.sem("exponent_ready")
            s_ex = s.sem("exp_done")
            s_xm = s.sem("factors_masked")
            s_pt = s.sem("factors_turned")
            s_xt = s.sem("factors_copied")
            s_mn = s.sem("shifts_ready")
            s_wt = s.sem("shift_exp_done")
        hw = D // heads if heads else D
        with s.block() as block:

            @block.gpsimd
            def _(pool):
                pool.wait_ge(s_r0, 1)
                pool.indirect_dma_start(out=row[:, :], out_offset=None, in_=acc,
                                        in_offset=bass.IndirectOffsetOnAxis(ap=S["repair32"][:], axis=0),
                                        bounds_check=P * C - 1, oob_is_err=False).then_inc(s_row, 16)
                pool.wait_ge(s_fix, 1)
                pool.indirect_dma_start(out=acc, out_offset=bass.IndirectOffsetOnAxis(ap=S["repair32"][:], axis=0),
                                        in_=row[:, :], in_offset=None,
                                        bounds_check=P * C - 1, oob_is_err=False).then_inc(s_out, 16)
                pool.wait_ge(s_out, 16)

            @block.tensor
            def _(pe):
                if not heads:
                    pe.matmul(pc[:, 0:D], S["join"][:], S["tail"][:, 0:D], start=True, stop=True).then_inc(s_car, 1)
                    return
                pe.wait_ge(s_dg, 1)
                for h in range(heads):
                    last = pe.matmul(pb[:, h, :], S["ones"][:], dg[:, h, :], start=True, stop=True)
                last.then_inc(s_pb, 1)
                pe.wait_ge(s_xm, 1)
                for h in range(heads):
                    last = pe.transpose(pt[:, h, :], x[:, h, :], S["ident"][:])
                last.then_inc(s_pt, 1)
                pe.wait_ge(s_xt, 1)
                for h in range(heads):
                    pe.matmul(pc[:, h * hw:(h + 1) * hw], xt[:, h, :], S["tail"][:, h * hw:(h + 1) * hw], start=True, stop=True)
                    last = pe.matmul(pc[:, D + h:D + h + 1], xt[:, h, :], S["tail"][:, D + h:D + h + 1], start=True, stop=True)
                last.then_inc(s_car, 1)

            @block.vector
            def _(dve):
                dve.memset(row[:], 0.0)
                dve.drain().then_inc(s_r0, 1)
                if not heads:
                    dve.wait_ge(s_car, 1)
                    dve.wait_ge(s_row, 16)
                    dve.tensor_tensor(row[:], row[:], pc[:, 0:D], ALU.add).then_inc(s_fix, 1)
                    return
                m = S["tail"][:, D + heads:D + 2 * heads]
                for h in range(heads):
                    last = dve.tensor_scalar(dg[:, h, :], S["ident"][:], m[:, h:h + 1], None, ALU.mult)
                last.then_inc(s_dg, 1)
                dve.wait_ge(s_pb, 1)
                for h in range(heads):
                    dve.tensor_tensor(x[:, h, :], pb[:, h, :], S["joincut"][:], ALU.add)
                dve.drain()
                dve.tensor_reduce(ms[:], x[:], AX_X, ALU.max)
                dve.drain()
                dve.tensor_tensor(x[:], x[:], spread(ms[:], P), ALU.subtract).then_inc(s_x, 1)
                dve.wait_ge(s_ex, 1)
                for h in range(heads):
                    last = dve.tensor_tensor(x[:, h, :], x[:, h, :], S["joinT"][:], ALU.mult)
                last.then_inc(s_xm, 1)
                dve.wait_ge(s_pt, 1)
                dve.tensor_copy(xt[:], pt[:]).then_inc(s_xt, 1)
                dve.wait_ge(s_row, 16)
                rm = row[:, D + heads:D + 2 * heads]
                dve.tensor_tensor(car[:, D:D + heads], rm, ms[:], ALU.max)
                dve.drain()
                dve.tensor_tensor(mn[:, 0, :], rm, car[:, D:D + heads], ALU.subtract)
                dve.tensor_tensor(mn[:, 1, :], ms[:], car[:, D:D + heads], ALU.subtract).then_inc(s_mn, 1)
                dve.wait_ge(s_wt, 1)
                dve.tensor_copy(rm, car[:, D:D + heads])
                dve.wait_ge(s_car, 1)
                dve.drain()
                dve.tensor_tensor(row[:, D:D + heads], row[:, D:D + heads], wt[:, 0, :], ALU.mult)
                dve.tensor_tensor(car[:, D:D + heads], pc[:, D:D + heads], wt[:, 1, :], ALU.mult)
                for h in range(heads):
                    f = slice(h * hw, (h + 1) * hw)
                    dve.tensor_scalar(row[:, f], row[:, f], wt[:, 0, h:h + 1], None, ALU.mult)
                    dve.tensor_scalar(car[:, f], pc[:, f], wt[:, 1, h:h + 1], None, ALU.mult)
                dve.drain()
                dve.tensor_tensor(row[:, 0:D + heads], row[:, 0:D + heads], car[:, 0:D + heads], ALU.add).then_inc(s_fix, 1)

            @block.scalar
            def _(act):
                if heads:
                    act.wait_ge(s_x, 1)
                    act.activation(x[:], x[:], ACT.Exp).then_inc(s_ex, 1)
                    act.wait_ge(s_mn, 1)
                    act.activation(wt[:], mn[:], ACT.Exp).then_inc(s_wt, 1)


def hyper_phase(nc, S, tag, acc, w1, w2, out):
    with Scope(nc, tag) as s:
        g = [s.sb(f"g{b}", [P, J, D]) for b in range(2)]
        z = [s.sb(f"z{b}", [P, J, D]) for b in range(2)]
        st = [s.sb(f"st{b}", [P, J], I32) for b in range(2)]
        zt = s.sb("zt", [P, KC, J, P])
        rt = s.sb("rt", [P, KC, J * P])
        o = [s.sb(f"o{b}", [P, J, D]) for b in range(2)]
        eb = s.sb("eb", [P, J])
        pt = s.ps("pt", [P, KC, J, P])
        pr = s.ps("pr", [P, KC, J * P])
        po = s.ps("po", [P, J, 512 // 2])
        s_st = s.sem("indices_staged")
        s_clr = s.sem("rows_cleared")
        s_g = [s.pool_sem(S, f"rows_gathered{b}") for b in range(2)]
        s_z = s.sem("z_ready")
        s_t = s.sem("z_turned")
        s_zt = s.sem("zt_copied")
        s_r = s.sem("hidden_ready")
        s_rt = s.sem("hidden_relu")
        s_m = s.sem("product_ready")
        s_o = s.sem("out_copied")
        s_sv = s.sems("out_stored")
        outv = out.rearrange("(n p j) w -> n p j w", p=P, j=J)
        with s.block() as block:

            @block.gpsimd
            def _(pool):
                def step(t):
                    hold(pool, S["passed"], s_clr, t.n + 1)
                    pool.tensor_copy(st[t.slot][:], S["last32"][:, bass.ds(t.n * J, J)]).then_inc(s_st, 1)
                    hold(pool, S["passed"], s_st, t.n + 1)
                    for j in range(J):
                        pool.indirect_dma_start(out=g[t.slot][:, j, :], out_offset=None, in_=acc,
                                                in_offset=bass.IndirectOffsetOnAxis(ap=st[t.slot][:, j:j + 1], axis=0),
                                                bounds_check=P * C - 1, oob_is_err=False).then_inc(s_g[t.slot], 16)

                over_blocks(pool, step, HB, u=2, first=0, last=HB)

            @block.vector
            def _(dve):
                for b in range(2):
                    dve.memset(g[b][:], 0.0).then_inc(s_clr, 1)

                def step(t):
                    dve.tensor_copy(eb[:], S["einv"][:, bass.ds(t.n * J, J)])
                    dve.drain()
                    if not t.before(2):
                        dve.wait_ge(s_t, t.n - 1)
                    dve.wait_ge(s_g[t.slot], (t.turn + 1) * 16 * J)
                    dve.tensor_tensor(z[t.slot][:], g[t.slot][:], spread(eb[:], D), ALU.mult).then_inc(s_z, 1)
                    dve.wait_ge(s_z, t.n + 1)
                    dve.sem_inc(s_clr, 1)

                over_blocks(dve, step, HB, u=2, first=2, last=HB)

            @block.tensor
            def _(pe):
                def step(t):
                    pe.wait_ge(s_z, t.n + 1)
                    for k in range(KC):
                        for j in range(J):
                            last = pe.transpose(pt[:, k, j, :], z[t.slot][:, j, k * P:(k + 1) * P], S["ident"][:])
                    last.then_inc(s_t, 1)
                    pe.wait_ge(s_zt, t.n + 1)
                    for m in range(KC):
                        for k in range(KC):
                            last = pe.matmul(pr[:, m, :], w1[:, k, m * P:(m + 1) * P],
                                             zt[:, k].rearrange("p j n -> p (j n)"), start=k == 0, stop=k == KC - 1)
                    last.then_inc(s_r, 1)
                    pe.wait_ge(s_rt, t.n + 1)
                    if not t.before(1):
                        pe.wait_ge(s_o, t.n)
                    for j in range(J):
                        for k in range(KC):
                            last = pe.matmul(po[:, j, :], rt[:, k, j * P:(j + 1) * P], w2[:, k, 0:D],
                                             start=k == 0, stop=k == KC - 1)
                    last.then_inc(s_m, 1)

                over_blocks(pe, step, HB, u=2, first=2, last=HB)

            @block.scalar
            def _(act):
                def step(t):
                    act.wait_ge(s_t, t.n + 1)
                    act.activation(zt[:], pt[:], ACT.Copy).then_inc(s_zt, 1)
                    act.wait_ge(s_r, t.n + 1)
                    act.activation(rt[:], pr[:], ACT.Relu).then_inc(s_rt, 1)
                    act.wait_ge(s_m, t.n + 1)
                    if not t.before(2):
                        act.wait_ge(s_sv[t.slot], t.turn * 16)
                    act.activation(o[t.slot][:], po[:], ACT.Copy).then_inc(s_o, 1)

                over_blocks(act, step, HB, u=2, first=2, last=HB)

            @block.sync
            def _(sp):
                def step(t):
                    sp.wait_ge(s_o, t.n + 1)
                    sp.dma_start(outv[bass.ds(t.n, 1)].rearrange("n p j w -> (n p) j w"), o[t.slot][:]).then_inc(s_sv[t.slot], 16)

                over_blocks(sp, step, HB, u=2, first=0, last=HB)
                for b in range(2):
                    sp.wait_ge(s_sv[b], 16 * HB // 2)


def source_sum_phase(nc, S, tag, table, sums):
    with Scope(nc, tag) as s:
        g = s.sb("g", [P, BC, SW])
        st = s.sb("st", [P, BC], I32)
        key = s.sb("key", [P, BC])
        dg = [s.sb(f"dg{b}", [P, P]) for b in range(2)]
        eq = [s.sb(f"eq{b}", [P, P]) for b in range(2)]
        junk = s.sb("junk", [P, P])
        dup = [s.sb(f"dup{b}", [P, 3]) for b in range(2)]
        idx = [s.sb(f"idx{b}", [P, 1], I32) for b in range(2)]
        tot = [s.sb(f"tot{b}", [P, SW]) for b in range(2)]
        pk = [s.ps(f"pk{b}", [P, P]) for b in range(2)]
        pt = [s.ps(f"pt{b}", [P, SW]) for b in range(2)]
        s_one = s.sem("ones_set")
        s_st = s.sem("indices_staged")
        s_key = s.sem("keys_staged")
        s_g = [s.pool_sem(S, f"row_gathered{k}") for k in range(BC)]
        s_dg = s.sem("diag_ready")
        s_pk = s.sem("keys_spread")
        s_eq = s.sem("equal_ready")
        s_tot = s.sem("total_ready")
        s_cp = s.sem("total_copied")
        s_add = s.pool_sem(S, "rows_added")
        AHEAD = 3
        with s.block() as block:

            @block.gpsimd
            def _(pool):
                pool.wait_ge(s_one, 1)

                def body(i, first):
                    if not first:
                        hold(pool, S["passed"], s_tot, i * BC)
                    pool.tensor_copy(st[:], S["hyp32"][:, bass.ds(i * BC, BC)]).then_inc(s_st, 1)
                    hold(pool, S["passed"], s_st, i + 1)

                    def gather(k):
                        pool.indirect_dma_start(out=g[:, k, 0:D], out_offset=None, in_=table,
                                                in_offset=bass.IndirectOffsetOnAxis(ap=st[:, k:k + 1], axis=0),
                                                bounds_check=table.shape[0] - 1, oob_is_err=False).then_inc(s_g[k], 16)

                    for k in range(AHEAD):
                        gather(k)
                    for k in range(BC):
                        if k + AHEAD < BC:
                            gather(k + AHEAD)
                        hold(pool, S["passed"], s_cp, i * BC + k + 1)
                        if not (first and k == 0):
                            hold(pool, S["passed"], s_add, (i * BC + k) * 16)
                        pool.indirect_dma_start(out=sums, out_offset=bass.IndirectOffsetOnAxis(ap=idx[k % 2][:, 0:1], axis=0),
                                                in_=tot[k % 2][:, :], in_offset=None, bounds_check=sums.shape[0] - 1,
                                                compute_op=ALU.add).then_inc(s_add, 16)

                body(0, True)
                with pool.Fori(1, NBAT) as i:
                    body(i, False)
                pool.wait_ge(s_add, 16 * C)

            @block.vector
            def _(dve):
                dve.memset(g[:], 1.0)
                dve.drain().then_inc(s_one, 1)

                def body(i, first):
                    if not first:
                        dve.wait_ge(s_pk, i * BC)
                    dve.tensor_copy(key[:], S["skey"][:, bass.ds(i * BC, BC)])
                    dve.drain()

                    def diagonal(k):
                        if k >= 2:
                            dve.wait_ge(s_pk, i * BC + k - 1)
                        dve.tensor_scalar(dg[k % 2][:], S["ident"][:], key[:, k:k + 1], None, ALU.mult).then_inc(s_dg, 1)

                    diagonal(0)
                    for k in range(BC):
                        if k + 1 < BC:
                            diagonal(k + 1)
                        b = k % 2
                        dve.wait_ge(s_pk, i * BC + k + 1)
                        if not (first and k < 2):
                            dve.wait_ge(s_tot, i * BC + k - 1)
                            dve.wait_ge(s_add, (i * BC + k - 1) * 16)
                        dve.tensor_scalar(eq[b][:], pk[b][:], key[:, k:k + 1], None, ALU.is_equal).then_inc(s_eq, 1)
                        dve.tensor_tensor(dup[b][:, 1:2], S["dummy"][:], key[:, k:k + 1], ALU.subtract)
                        dve.drain()
                        dve.tensor_tensor_reduce(junk[:], eq[b][:], S["lower"][:], 1.0, 0.0, ALU.mult, ALU.add, dup[b][:, 0:1])
                        dve.drain()
                        dve.tensor_scalar(dup[b][:, 0:1], dup[b][:, 0:1], 1.0, None, ALU.min)
                        dve.drain()
                        dve.scalar_tensor_tensor(dup[b][:, 2:3], dup[b][:, 1:2], dup[b][:, 0:1], key[:, k:k + 1], ALU.mult, ALU.add)
                        dve.drain()
                        dve.tensor_copy(idx[b][:], dup[b][:, 2:3]).then_inc(s_key, 1)

                body(0, True)
                with dve.Fori(1, NBAT) as i:
                    body(i, False)

            @block.tensor
            def _(pe):
                def body(i, first):
                    def keys(k):
                        pe.wait_ge(s_dg, i * BC + k + 1)
                        if not (first and k < 2):
                            pe.wait_ge(s_eq, i * BC + k - 1)
                        pe.matmul(pk[k % 2][:], S["ones"][:], dg[k % 2][:], start=True, stop=True).then_inc(s_pk, 1)

                    keys(0)
                    for k in range(BC):
                        if k + 1 < BC:
                            keys(k + 1)
                        pe.wait_ge(s_eq, i * BC + k + 1)
                        pe.wait_ge(s_g[k], (i + 1) * 16)
                        if not (first and k < 2):
                            pe.wait_ge(s_cp, i * BC + k - 1)
                        pe.matmul(pt[k % 2][:], eq[k % 2][:], g[:, k, :], start=True, stop=True).then_inc(s_tot, 1)

                body(0, True)
                with pe.Fori(1, NBAT) as i:
                    body(i, False)

            @block.scalar
            def _(act):
                def body(i, first):
                    for k in range(BC):
                        act.wait_ge(s_tot, i * BC + k + 1)
                        if not (first and k < 2):
                            act.wait_ge(s_add, (i * BC + k - 1) * 16)
                        act.wait_ge(s_key, i * BC + k + 1)
                        act.activation(tot[k % 2][:], pt[k % 2][:], ACT.Copy).then_inc(s_cp, 1)

                body(0, True)
                with act.Fori(1, NBAT) as i:
                    body(i, False)


def node_phase(nc, S, tag, kind, rows, rw, extra=None, ew=D, gather=None, gw=0, heads=0, bias=None, elu="",
               loops=False, norm=False, relu=None, save=None, sw=D, weight=None, oheads=0, out=None, ad=None,
               final=False):
    gcn, bn, gat, total = kind == "gcn", kind == "bn", kind == "gat", kind == "sum"
    turned = elu == "turned"
    hw = D // heads if heads else D
    b_lag = 1 if gat else 0
    c_lag = {"gat": 2, "bn": 1}.get(kind, 0)
    z_lag = c_lag + 1 if norm else b_lag
    m_lag = z_lag + 1
    o_lag = m_lag + 1 if turned else m_lag
    r_lag = max(c_lag - 1, 0)
    with Scope(nc, tag) as s:
        bufs = lambda name, shape, dt=F32: [s.sb(f"{name}{b}", shape, dt) for b in range(U)]
        sems = lambda name: [s.sem(f"{name}{b}") for b in range(U)]
        a = bufs("a", [P, J, rw])
        s_in = sems("rows_loaded")
        s_used = s.sem("rows_used")
        s_rin = sems("residual_loaded")
        s_rused = s.sem("residual_used")
        s_z = s.sem("z_ready")
        s_zs = sems("z_stored")
        s_t = s.sem("z_turned")
        s_zt = s.sem("zt_ready")
        s_m = s.sem("product_ready")
        s_o = s.sem("out_copied")
        s_os = sems("out_stored")
        s_ex = s.sem("exponents_ready")
        s_wt = s.sem("weights_ready")
        s_nw = s.sem("weights_normalized")
        s_v = s.sem("self_part_ready")
        s_st = s.sem("indices_staged")
        s_clr = s.sem("gathered_cleared")
        s_g = [s.pool_sem(S, f"runs_gathered{b}") for b in range(U)]
        s_var = s.sem("variance_ready")
        s_rs = s.sem("rstd_ready")
        s_y = s.sem("bn_ready")
        s_yt = s.sem("bn_turned")
        s_bs = s.sem("turned_read")
        s_en = s.sem("elu_input_ready")
        s_ee = s.sem("elu_exp_done")
        s_a, s_n, s_b, s_c = s.sem("logit_steps"), s.sem("weight_steps"), s.sem("sum_steps"), s.sem("c_steps")
        nin = 2 if bn else 1
        if extra is not None:
            r = bufs("r", [P, J, ew])
        if gather is not None:
            g = bufs("g", [P, J, gw])
            st = bufs("st", [P, J], I32)
        if gat:
            e = s.sb("e", [P, J, heads])
            mm = s.sb("mm", [P, J, heads])
            den = s.sb("den", [P, J, heads])
            ex = bufs("ex", [P, 2, J, heads])
            wt = bufs("wt", [P, 2, J, heads])
            v = bufs("v", [P, J, D])
            lp = bufs("lp", [P, J])
        u = bufs("u", [P, J, D]) if norm or elu else None
        if elu:
            ee = bufs("ee", [P, J * D])
        if norm:
            bs = s.sb("bs", [P, J, 6])
            mv = bufs("mv", [P, J, 2])
            ve = bufs("ve", [P, J])
            rs = bufs("rs", [P, J])
        if norm or gcn:
            z = bufs("z", [P, J, sw])
        else:
            z = u
        if total or gcn:
            scs = bufs("sc", [P, 2, J])
        if weight is not None:
            zt = s.sb("zt", [P, KC, J, P])
            pt = s.ps("pt", [P, KC, J, P])
            if gcn:
                o = bufs("o", [P, KC, J * P])
                pm = s.ps("pm", [P, KC, J * P])
                stats = s.sb("stats", [P, KC, NB, 6])
                bmv = s.sb("bmv", [P, KC, 2])
                bt = s.sb("bt", [P, KC, 2])
                s_fin = s.sem("batch_variance")
                s_frs = s.sem("batch_rstd")
            else:
                o = bufs("o", [P, J, RW])
                ao = bufs("ao", [P, J, oheads])
                pm = s.ps("pm", [P, J, 512])
                wc = D + 2 * oheads
        if bn:
            yt = bufs("yt", [P, KC, J * P])
            yr = bufs("yr", [P, KC, J, P])
            py = s.ps("py", [P, J, KC, P])
        per_o = 1 if gcn else 2
        padded = rows.shape[0] == NPAD
        tailrows = lambda t: t[TAIL0:N, :].rearrange("(p j) w -> p j w", j=J)
        blockof = lambda t, n: t[bass.ds(n * BLK, BLK), :].rearrange("(p j) w -> p j w", j=J)
        by_head = lambda x: x[:, :, 0:D].rearrange("p j (h c) -> p j h c", h=heads)
        is_tail = lambda t: t.fixed and t.n == TAILN
        is_padding = lambda t: t.fixed and t.n > TAILN

        with s.block() as block:

            @block.sync
            def _(sp):
                sp.wait_ge(s_clr, 1)

                def load(t):
                    if not t.before(U):
                        hold(sp, S["passed"], s_used, t.n - U + 1)
                    if is_tail(t) and not padded:
                        sp.dma_start(a[t.slot][0:TAILP, :, :], tailrows(rows)).then_inc(s_in[t.slot], 16)
                    elif is_padding(t) and not padded:
                        sp.dma_start(a[t.slot][0:TAILP, :, :], tailrows(rows)).then_inc(s_in[t.slot], 16)
                    else:
                        sp.dma_start(a[t.slot][:], blockof(rows, t.n)).then_inc(s_in[t.slot], 16)
                    if bn:
                        sp.dma_start(yt[t.slot][:], S["AGG"][:, :, bass.ds(t.n * BLK, BLK)]).then_inc(s_in[t.slot], 16)

                def load_residual(t):
                    if not t.before(U):
                        hold(sp, S["passed"], s_rused, t.n - U + 1)
                    sp.dma_start(r[t.slot][:], blockof(extra, t.n)).then_inc(s_rin[t.slot], 16)

                def store_z(t):
                    hold(sp, S["passed"], s_z, t.n + 1)
                    if final and is_tail(t):
                        sp.dma_start(tailrows(save), z[t.slot][0:TAILP, :, :]).then_inc(s_zs[t.slot], 16)
                    elif not (final and is_padding(t)):
                        sp.dma_start(blockof(save, t.n), z[t.slot][:]).then_inc(s_zs[t.slot], 16)

                def store_out(t):
                    hold(sp, S["passed"], s_o, t.n + 1)
                    if gcn:
                        sp.dma_start(S["AGG"][:, :, bass.ds(t.n * BLK, BLK)], o[t.slot][:]).then_inc(s_os[t.slot], 16)
                    else:
                        sp.dma_start(blockof(out, t.n), o[t.slot][:]).then_inc(s_os[t.slot], 16)
                        sp.dma_start(blockof(ad, t.n), ao[t.slot][:]).then_inc(s_os[t.slot], 16)

                def step(t):
                    if t.real(0):
                        load(t)
                    if extra is not None and t.real(r_lag):
                        load_residual(t.back(r_lag))
                    if save is not None and t.real(z_lag + 1):
                        store_z(t.back(z_lag + 1))
                    if weight is not None and t.real(o_lag + 1):
                        store_out(t.back(o_lag + 1))

                over_blocks(sp, step, NB, (o_lag if weight is not None else z_lag) + 1)
                for b in range(U):
                    if save is not None:
                        sp.wait_ge(s_zs[b], 16 * len(range(b, NREAL if final else NB, U)))
                    if weight is not None:
                        sp.wait_ge(s_os[b], 16 * per_o * (NB // U))

            @block.gpsimd
            def _(pool):
                def gathers(t):
                    hold(pool, S["passed"], s_clr, t.n + 1)
                    pool.tensor_copy(st[t.slot][:], S["last32"][:, bass.ds(t.n * J, J)]).then_inc(s_st, 1)
                    hold(pool, S["passed"], s_st, t.n + 1)
                    for j in range(J):
                        pool.indirect_dma_start(out=g[t.slot][:, j, :], out_offset=None, in_=gather,
                                                in_offset=bass.IndirectOffsetOnAxis(ap=st[t.slot][:, j:j + 1], axis=0),
                                                bounds_check=P * C - 1, oob_is_err=False).then_inc(s_g[t.slot], 16)

                def rstd(t):
                    hold(pool, S["passed"], s_var, t.n + 1)
                    pool.tensor_tensor(rs[t.slot][:], ve[t.slot][:], S["minus_half"][:, 0:J], ALU.pow).then_inc(s_rs, 1)

                def step(t):
                    if gather is not None and t.real(0):
                        gathers(t)
                    if norm and t.real(z_lag):
                        rstd(t.back(z_lag))

                if gather is not None or norm:
                    over_blocks(pool, step, NB, z_lag)
                if gcn:
                    pool.wait_ge(s_fin, 1)
                    pool.tensor_tensor(bt[:, :, 0], bmv[:, :, 1], S["minus_half"][:, 0:KC], ALU.pow).then_inc(s_frs, 1)

            @block.tensor
            def _(pe):
                def turn_bn(t):
                    pe.wait_ge(s_y, t.n + 1)
                    if not t.before(1):
                        pe.wait_ge(s_bs, t.n)
                    for j in range(J):
                        for k in range(KC):
                            last = pe.transpose(py[:, j, k, :], yr[t.slot][:, k, j, :], S["ident"][:])
                    last.then_inc(s_yt, 1)

                def turn(t):
                    pe.wait_ge(s_z, t.n + 1)
                    if not t.before(1):
                        pe.wait_ge(s_zt, t.n)
                    for k in range(KC):
                        for j in range(J):
                            last = pe.transpose(pt[:, k, j, :], z[t.slot][:, j, k * P:(k + 1) * P], S["ident"][:])
                    last.then_inc(s_t, 1)

                def product(t):
                    pe.wait_ge(s_zt, t.n + 1)
                    if not t.before(1):
                        pe.wait_ge(s_o, t.n)
                    if gcn:
                        for m in range(KC):
                            for k in range(KC):
                                last = pe.matmul(pm[:, m, :], weight[:, k, m * P:(m + 1) * P],
                                                 zt[:, k].rearrange("p j n -> p (j n)"), start=k == 0, stop=k == KC - 1)
                    else:
                        for j in range(J):
                            for k in range(KC):
                                last = pe.matmul(pm[:, j, 0:wc], zt[:, k, j, :], weight[:, k, 0:wc],
                                                 start=k == 0, stop=k == KC - 1)
                    last.then_inc(s_m, 1)

                def step(t):
                    if bn and t.real(0):
                        turn_bn(t)
                    if t.real(m_lag):
                        product(t.back(m_lag))
                    if t.real(z_lag):
                        turn(t.back(z_lag))

                if weight is not None:
                    over_blocks(pe, step, NB, m_lag)

            @block.scalar
            def _(act):
                def normalize_bn(t):
                    act.wait_ge(s_in[t.slot], (t.turn + 1) * 16 * nin)
                    if not t.before(U):
                        act.wait_ge(s_yt, t.n - U + 1)
                    for k in range(KC):
                        last = act.activation(yr[t.slot][:, k].rearrange("p j n -> p (j n)"), yt[t.slot][:, k, :],
                                              ACT.Relu, bias=S["bnshift"][:, k:k + 1], scale=S["bnscale"][:, k:k + 1])
                    last.then_inc(s_y, 1)

                def exp_weights(t):
                    act.wait_ge(s_ex, t.n + 1)
                    act.activation(wt[t.slot][:], ex[t.slot][:], ACT.Exp).then_inc(s_wt, 1)

                def self_part(t):
                    act.wait_ge(s_nw, t.n + 1)
                    for j in range(J):
                        for h in range(heads):
                            f = slice(h * hw, (h + 1) * hw)
                            last = act.activation(v[t.slot][:, j, f], a[t.slot][:, j, f], ACT.Copy,
                                                  scale=wt[t.slot][:, 0, j, h:h + 1])
                    last.then_inc(s_v, 1)

                def exp_elu(t):
                    if turned:
                        act.wait_ge(s_t, t.n + 1)
                        for k in range(KC):
                            last = act.activation(ee[t.slot][:, k * J * P:(k + 1) * J * P],
                                                  pt[:, k].rearrange("p j n -> p (j n)"), ACT.Exp, bias=bias[:, k:k + 1])
                    else:
                        act.wait_ge(s_en, t.n + 1)
                        last = act.activation(ee[t.slot][:], u[t.slot][:].rearrange("p j d -> p (j d)"), ACT.Exp,
                                              bias=S["minus_one"][:])
                    last.then_inc(s_ee, 1)

                def copy_turned(t):
                    act.wait_ge(s_t, t.n + 1)
                    if not t.before(1):
                        act.wait_ge(s_m, t.n)
                    if relu is None:
                        last = act.activation(zt[:], pt[:], ACT.Copy)
                    else:
                        for k in range(KC):
                            last = act.activation(zt[:, k], pt[:, k], ACT.Relu, bias=relu[1][:, k:k + 1],
                                                  scale=relu[0][:, k:k + 1])
                    last.then_inc(s_zt, 1)

                def copy_out(t):
                    act.wait_ge(s_m, t.n + 1)
                    if not t.before(U):
                        act.wait_ge(s_os[t.slot], t.turn * 16 * per_o)
                    if gcn:
                        if not t.before(U):
                            act.wait_ge(s_bs, t.n - U + 1)
                        for m in range(KC):
                            last = act.activation(o[t.slot][:, m, :], pm[:, m, :], ACT.Identity, bias=S["c_L2_gnn_b"][:, m:m + 1])
                    else:
                        act.activation(o[t.slot][:, :, 0:wc], pm[:, :, 0:wc], ACT.Copy)
                        last = act.activation(ao[t.slot][:], pm[:, :, D + oheads:D + 2 * oheads], ACT.Copy)
                    last.then_inc(s_o, 1)

                def step(t):
                    if weight is not None and not turned and t.real(m_lag):
                        copy_turned(t.back(m_lag))
                    if bn and t.real(0):
                        normalize_bn(t)
                    if elu and t.real(2):
                        exp_elu(t.back(2))
                    if gat and t.real(1):
                        self_part(t.back(1))
                    if gat and t.real(0):
                        exp_weights(t)
                    if weight is not None and t.real(o_lag):
                        copy_out(t.back(o_lag))

                act.wait_ge(s_clr, 1)
                over_blocks(act, step, NB, o_lag if weight is not None else max(c_lag, b_lag))

            @block.vector
            def _(dve):
                for b in range(U):
                    if weight is not None and not gcn and wc < RW:
                        dve.memset(o[b][:], 0.0)
                    if not padded:
                        dve.memset(a[b][:], 0.0)
                    if sw > D:
                        dve.memset(z[b][:], 0.0)
                    if gather is not None:
                        dve.memset(g[b][:], 0.0)
                dve.drain()

                def clear(b):
                    if gat:
                        dve.memset(g[b][:, :, D + heads:D + 2 * heads], -BIG).then_inc(s_clr, 1)
                    else:
                        dve.sem_inc(s_clr, 1)

                for b in range(U):
                    clear(b)
                logit = Chain(dve, s_a, 5 if loops else 3)
                share = Chain(dve, s_n, 3)
                summed = Chain(dve, s_b, {"sum": 3, "gcn": 2 + J}.get(kind, 1 if turned else 2))
                third = Chain(dve, s_c, 1 if turned else 2 * J + (2 if elu else 1 if bn or (gat and extra is not None) else 0))

                def logits(t, k):
                    at, gt = a[t.slot], g[t.slot]
                    gm = gt[:, :, D + heads:D + 2 * heads]
                    if k == 0:
                        dve.wait_ge(s_in[t.slot], (t.turn + 1) * 16 * nin)
                        logit.start(t)
                        if loops:
                            logit.link(dve.tensor_copy(lp[t.slot][:], S["loopcut"][:, bass.ds(t.n * J, J)]))
                        logit.link(dve.tensor_tensor(e[:], at[:, :, D:D + heads], at[:, :, D + heads:D + 2 * heads], ALU.add))
                    if k == 1:
                        logit.settle()
                        logit.link(dve.scalar_tensor_tensor(e[:], e[:], SLOPE, e[:], ALU.mult, ALU.max))
                    if k == 2:
                        logit.settle()
                        if loops:
                            logit.link(dve.tensor_tensor(e[:], e[:], spread(lp[t.slot][:], heads), ALU.add))
                            logit.settle()
                        dve.wait_ge(s_g[t.slot], (t.turn + 1) * 16 * J)
                        logit.link(dve.scalar_tensor_tensor(mm[:], e[:], -BIG / 2, gm, ALU.max, ALU.max))
                    if k == 3:
                        logit.settle()
                        dve.tensor_tensor(ex[t.slot][:, 0], e[:], mm[:], ALU.subtract)
                        dve.tensor_tensor(ex[t.slot][:, 1], gm, mm[:], ALU.subtract).then_inc(s_ex, 1)
                        logit.stop()

                def shares(t, k):
                    w = wt[t.slot]
                    if k == 0:
                        dve.wait_ge(s_wt, t.n + 1)
                        share.start(t)
                        share.link(dve.tensor_tensor(den[:], g[t.slot][:, :, D:D + heads], w[:, 1], ALU.mult))
                    if k == 1:
                        share.settle()
                        share.link(dve.scalar_tensor_tensor(den[:], den[:], 1e-30, w[:, 0], ALU.max, ALU.add))
                    if k == 2:
                        share.settle()
                        share.link(dve.reciprocal(den[:], den[:]))
                    if k == 3:
                        share.settle()
                        dve.tensor_tensor(w[:, 0], w[:, 0], den[:], ALU.mult)
                        dve.tensor_tensor(w[:, 1], w[:, 1], den[:], ALU.mult).then_inc(s_nw, 1)
                        share.stop()

                def sum_up(t):
                    at = a[t.slot]
                    if not gat:
                        dve.wait_ge(s_in[t.slot], (t.turn + 1) * 16 * nin)
                    summed.start(t)
                    if gat:
                        ut, gt = u[t.slot], g[t.slot]
                        if turned and not t.before(U):
                            dve.wait_ge(s_t, t.n - U + 1)
                        dve.wait_ge(s_nw, t.n + 1)
                        summed.link(dve.tensor_tensor(by_head(ut), by_head(gt), spread(wt[t.slot][:, 1], hw), ALU.mult))
                        dve.wait_ge(s_v, t.n + 1)
                        summed.settle()
                        if turned:
                            dve.tensor_tensor(ut[:], ut[:], v[t.slot][:], ALU.add).then_inc(s_z, 1)
                        else:
                            summed.link(dve.tensor_tensor(ut[:], ut[:], v[t.slot][:], ALU.add))
                            summed.settle()
                            dve.tensor_tensor(ut[:], ut[:], bias[:].unsqueeze(1).to_broadcast([P, J, D]), ALU.add).then_inc(s_en, 1)
                        dve.memset(gt[:, :, D + heads:D + 2 * heads], -BIG).then_inc(s_clr, 1)
                        dve.wait_ge(s_clr, t.n + U + 1)
                        dve.sem_inc(s_used, 1)
                    elif total:
                        rt, ut, sc = r[t.slot], u[t.slot], scs[t.slot]
                        dve.wait_ge(s_rin[t.slot], (t.turn + 1) * 16)
                        summed.link(dve.tensor_scalar(sc[:, 0, :], rt[:, :, D], 1.0, None, ALU.max))
                        summed.settle()
                        summed.link(dve.reciprocal(sc[:, 0, :], sc[:, 0, :]))
                        summed.settle()
                        summed.link(dve.tensor_tensor(ut[:], rt[:, :, 0:D], spread(sc[:, 0, :], D), ALU.mult))
                        summed.settle()
                        dve.tensor_tensor(ut[:], ut[:], at[:, :, 0:D], ALU.add).then_inc(s_en, 1)
                        dve.wait_ge(s_en, t.n + 1)
                        dve.sem_inc(s_used, 1)
                        dve.sem_inc(s_rused, 1)
                    elif gcn:
                        zz, sc = z[t.slot], scs[t.slot]
                        dve.wait_ge(s_g[t.slot], (t.turn + 1) * 16 * J)
                        if not t.before(U):
                            dve.wait_ge(s_t, t.n - U + 1)
                        dve.tensor_copy(sc[:, 0, :], S["dinv"][:, bass.ds(t.n * J, J)])
                        summed.link(dve.tensor_copy(sc[:, 1, :], S["has"][:, bass.ds(t.n * J, J)]))
                        summed.settle()
                        summed.link(dve.tensor_tensor(zz[:], at[:, :, 0:D], spread(sc[:, 0, :], D), ALU.mult))
                        summed.settle()
                        for j in range(J):
                            summed.link(dve.scalar_tensor_tensor(zz[:, j, :], g[t.slot][:, j, :], sc[:, 1, j:j + 1],
                                                                 zz[:, j, :], ALU.mult, ALU.add))
                        summed.settle()
                        dve.tensor_tensor(zz[:], zz[:], spread(sc[:, 0, :], D), ALU.mult).then_inc(s_z, 1)
                        dve.sem_inc(s_used, 1)
                        dve.sem_inc(s_clr, 1)
                    summed.stop()

                def stage_c(t):
                    third.start(t)
                    if turned:
                        dve.wait_ge(s_ee, t.n + 1)
                        if not t.before(1):
                            dve.wait_ge(s_m, t.n)
                        third.link(dve.tensor_scalar(ee[t.slot][:], ee[t.slot][:], 1.0, -1.0, ALU.min, ALU.add))
                        third.settle()
                        for k in range(KC):
                            last = dve.scalar_tensor_tensor(zt[:, k].rearrange("p j n -> p (j n)"),
                                                            pt[:, k].rearrange("p j n -> p (j n)"), bias[:, k:k + 1],
                                                            ee[t.slot][:, k * J * P:(k + 1) * J * P], ALU.add, ALU.max)
                        last.then_inc(s_zt, 1)
                        third.stop()
                        return
                    ut = u[t.slot]
                    if elu:
                        dve.wait_ge(s_ee, t.n + 1)
                        third.link(dve.scalar_tensor_tensor(ut[:].rearrange("p j d -> p (j d)"), ee[t.slot][:], 1.0,
                                                            ut[:].rearrange("p j d -> p (j d)"), ALU.min, ALU.max))
                        third.settle()
                        dve.wait_ge(s_rin[t.slot], (t.turn + 1) * 16)
                        third.link(dve.scalar_tensor_tensor(ut[:], ut[:], -1.0, r[t.slot][:], ALU.add, ALU.add))
                    elif bn:
                        dve.wait_ge(s_yt, t.n + 1)
                        third.link(dve.tensor_tensor(ut[:], a[t.slot][:, :, 0:D], py[:].rearrange("p j k n -> p j (k n)"), ALU.add))
                        third.settle()
                        dve.sem_inc(s_bs, 1)
                        dve.sem_inc(s_used, 1)
                    elif gat and extra is not None:
                        dve.wait_ge(s_rin[t.slot], (t.turn + 1) * 16)
                        dve.wait_ge(s_en, t.n + 1)
                        third.link(dve.tensor_tensor(ut[:], ut[:], r[t.slot][:], ALU.add))
                    else:
                        dve.wait_ge(s_en, t.n + 1)
                    third.settle()
                    if extra is not None and gat:
                        dve.sem_inc(s_rused, 1)
                    for j in range(J):
                        third.link(dve.bn_stats(bs[:, j, :], ut[:, j, :]))
                    third.settle()
                    dve.sem_inc(S["passed"], 1)
                    for j in range(J):
                        third.link(dve.bn_aggr(mv[t.slot][:, j, :], bs[:, j, :]))
                    third.settle()
                    last = dve.tensor_scalar(ve[t.slot][:], mv[t.slot][:, :, 1], EPS, None, ALU.add)
                    last.then_inc(s_var, 1)
                    third.stop()

                def normalize(t):
                    ut, zz = u[t.slot], z[t.slot]
                    dve.wait_ge(s_rs, t.n + 1)
                    if not t.before(U):
                        if save is not None:
                            dve.wait_ge(s_zs[t.slot], t.turn * 16)
                        if weight is not None:
                            dve.wait_ge(s_t, t.n - U + 1)
                    if sw > D:
                        dve.tensor_copy(zz[:, :, D], S["dinv"][:, bass.ds(t.n * J, J)])
                    for j in range(J):
                        last = dve.tensor_scalar(zz[:, j, 0:D], ut[:, j, :], mv[t.slot][:, j, 0:1], rs[t.slot][:, j:j + 1],
                                                 ALU.subtract, ALU.mult)
                    last.then_inc(s_z, 1)

                def batch_stats(t):
                    dve.wait_ge(s_o, t.n + 1)
                    for m in range(KC):
                        if is_padding(t):
                            continue
                        if is_tail(t):
                            last = dve.bn_stats(stats[:, m, t.n, :], o[t.slot][:, m, :].rearrange("p (j n) -> p j n", n=P)[:, :, 0:TAILP])
                        else:
                            last = dve.bn_stats(stats[:, m, bass.ds(t.n, 1), :].rearrange("p n s -> p (n s)"), o[t.slot][:, m, :])
                    last = dve.drain() if is_padding(t) else last
                    last.then_inc(s_bs, 1)

                def step(t):
                    for k in range(4):
                        if gat and t.real(1):
                            shares(t.back(1), k)
                        if gat and t.real(0):
                            logits(t, k)
                    if (gat or bn) and t.real(c_lag):
                        stage_c(t.back(c_lag))
                    if total and t.real(c_lag):
                        sum_up(t)
                        stage_c(t)
                    if norm and t.real(z_lag):
                        normalize(t.back(z_lag))
                    if (gat or gcn) and t.real(b_lag):
                        sum_up(t.back(b_lag))
                    if gcn and t.real(m_lag + 1):
                        batch_stats(t.back(m_lag + 1))

                over_blocks(dve, step, NB, max(z_lag, c_lag, m_lag + 1 if gcn else 0))
                if gcn:
                    dve.drain()
                    for m in range(KC):
                        dve.bn_aggr(bmv[:, m, :], stats[:, m, 0:NREAL].rearrange("p n s -> p (n s)"))
                    dve.drain()
                    dve.tensor_scalar(bmv[:, :, 1], bmv[:, :, 1], EPS, None, ALU.add).then_inc(s_fin, 1)
                    dve.wait_ge(s_frs, 1)
                    dve.tensor_tensor(S["bnscale"][:], bt[:, :, 0], S["c_L2_gnn_gamma"][:], ALU.mult)
                    dve.drain()
                    dve.tensor_tensor(bt[:, :, 1], bmv[:, :, 0], S["bnscale"][:], ALU.mult)
                    dve.drain()
                    dve.tensor_tensor(S["bnshift"][:], S["c_L2_gnn_beta"][:], bt[:, :, 1], ALU.subtract)


def gnn_kernel(nc, A, out):
    T = {
        "META": nc.dram_tensor("META", (NPAD, 2), I32).ap(),
        "NS0": nc.dram_tensor("NS0", (NPAD + P, SW), F32).ap(),
        "NS1": nc.dram_tensor("NS1", (NPAD + P, SW), F32).ap(),
        "HYP": nc.dram_tensor("HYP", (HB * BLK, D), F32).ap(),
        "SUMS": nc.dram_tensor("SUMS", (P * C, D), F32).ap(),
        "GSUMS": nc.dram_tensor("GSUMS", (P * C, RW), F32).ap(),
        "X1": nc.dram_tensor("X1", (NPAD, D), F32).ap(),
        "X2": nc.dram_tensor("X2", (NPAD, SW), F32).ap(),
        "X3": nc.dram_tensor("X3", (NPAD, D), F32).ap(),
        "HA": nc.dram_tensor("HA", (NPAD, RW), F32).ap(),
        "HBT": nc.dram_tensor("HBT", (NPAD, RW), F32).ap(),
        "AD": nc.dram_tensor("AD", (NPAD, 4), F32).ap(),
        "AD1": nc.dram_tensor("AD1", (NPAD, 1), F32).ap(),
        "AGG": nc.dram_tensor("AGG", (P, KC, NPAD), F32).ap(),
    }
    with Scope(nc, "k") as s:
        S = {"AGG": T["AGG"], "passed": s.sem("passed"),
             "scope": s}
        for name, shape, dt in (
            ("src32", [P, C], I32), ("dst32", [P, C], I32), ("hyp32", [P, C], I32), ("skey", [P, C], F32),
            ("same", [P, C], F32), ("cut", [P, C], F32), ("repair32", [P, 1], I32), ("dummy32", [P, 1], I32),
            ("dummy", [P, 1], F32), ("last32", [P, NB * J], I32), ("deg", [P, NB * J], F32), ("dinv", [P, NB * J], F32),
            ("einv", [P, HB * J], F32), ("has", [P, NB * J], F32), ("minus_one", [P, 1], F32), ("r1_L1_gnn_b2", [P, D], F32), ("loop", [P, NB * J], F32), ("loopcut", [P, NB * J], F32),
            ("ident", [P, P], F32), ("ones", [P, P], F32), ("upper", [P, P], F32), ("lower", [P, P], F32),
            ("join", [P, P], F32), ("joinT", [P, P], F32), ("joincut", [P, P], F32), ("minus_half", [P, 64], F32),
            ("tail", [P, RW], F32), ("bnscale", [P, KC], F32), ("bnshift", [P, KC], F32), ("w_L2", [P, KC, D], F32),
        ):
            S[name] = s.sb(name, shape, dt)
        S["weights"] = {"n2e0": A["L0_gnn_W0_n2e"], "e2n0": A["L0_gnn_W0_e2n"], "n2e1": A["L0_gnn_W1_n2e"],
                        "e2n1": A["L0_gnn_W1_e2n"], "L1a": A["L1_gnn_W1"], "L1b": A["L1_gnn_W2"],
                        "L3a": A["L3_gnn_W1"], "L3b": A["L3_gnn_W2"]}
        for name in S["weights"]:
            S["w_" + name] = s.sb("w_" + name, [P, KC, RW])
        for name in ROWS:
            S["r_" + name] = s.sb("r_" + name, [P, D])
        for name in COLS:
            S["c_" + name] = s.sb("c_" + name, [P, KC])

        setup_phase(nc, S, A, T)
        last_weight_phase(nc, S, A)
        edge_phase(nc, S, "e0", A["x"], D, T["SUMS"], D)
        repair_phase(nc, S, "f0", T["SUMS"], D)
        hyper_phase(nc, S, "h0", T["SUMS"], S["w_n2e0"], S["w_e2n0"], T["HYP"])
        source_sum_phase(nc, S, "s0", T["HYP"], T["NS0"])
        edge_phase(nc, S, "e1", T["NS0"], SW, T["SUMS"], D, scale="inverse")
        repair_phase(nc, S, "f1", T["SUMS"], D)
        hyper_phase(nc, S, "h1", T["SUMS"], S["w_n2e1"], S["w_e2n1"], T["HYP"])
        source_sum_phase(nc, S, "s1", T["HYP"], T["NS1"])
        node_phase(nc, S, "n0", "sum", A["x"], D, extra=T["NS1"], ew=SW, norm=True, save=T["X1"],
                   weight=S["w_L1a"], oheads=4, out=T["HA"], ad=T["AD"])
        edge_phase(nc, S, "e2", T["HA"], RW, T["GSUMS"], RW, heads=4, ad=T["AD"])
        repair_phase(nc, S, "f2", T["GSUMS"], RW, heads=4)
        node_phase(nc, S, "n1", "gat", T["HA"], RW, gather=T["GSUMS"], gw=RW, heads=4, bias=S["c_L1_gnn_b1"],
                   elu="turned", weight=S["w_L1b"], oheads=4, out=T["HBT"], ad=T["AD"])
        edge_phase(nc, S, "e3", T["HBT"], RW, T["GSUMS"], RW, heads=4, ad=T["AD"])
        repair_phase(nc, S, "f3", T["GSUMS"], RW, heads=4)
        node_phase(nc, S, "n2", "gat", T["HBT"], RW, extra=T["X1"], gather=T["GSUMS"], gw=RW, heads=4,
                   bias=S["r1_L1_gnn_b2"], elu="rows", norm=True, save=T["X2"], sw=SW)
        edge_phase(nc, S, "e4", T["X2"], SW, T["SUMS"], D, scale="plain")
        repair_phase(nc, S, "f4", T["SUMS"], D)
        node_phase(nc, S, "n3", "gcn", T["X2"], SW, gather=T["SUMS"], gw=D, weight=S["w_L2"])
        node_phase(nc, S, "n4", "bn", T["X2"], SW, norm=True, save=T["X3"], weight=S["w_L3a"], oheads=4,
                   out=T["HA"], ad=T["AD"])
        edge_phase(nc, S, "e5", T["HA"], RW, T["GSUMS"], RW, heads=4, ad=T["AD"])
        repair_phase(nc, S, "f5", T["GSUMS"], RW, heads=4)
        node_phase(nc, S, "n5", "gat", T["HA"], RW, gather=T["GSUMS"], gw=RW, heads=4, bias=S["r_L3_gnn_b1"],
                   loops=True, norm=True, relu=(S["c_L3_gnn_ln_g"], S["c_L3_gnn_ln_b"]), weight=S["w_L3b"],
                   oheads=1, out=T["HBT"], ad=T["AD1"])
        edge_phase(nc, S, "e6", T["HBT"], RW, T["GSUMS"], RW, heads=1, ad=T["AD1"])
        repair_phase(nc, S, "f6", T["GSUMS"], RW, heads=1)
        node_phase(nc, S, "n6", "gat", T["HBT"], RW, extra=T["X3"], gather=T["GSUMS"], gw=RW, heads=1,
                   bias=S["r_L3_gnn_b2"], loops=True, norm=True, save=out, final=True)


_INS = ["x", "src", "dst", "L0_gnn_W0_n2e", "L0_gnn_W0_e2n", "L0_gnn_W1_n2e", "L0_gnn_W1_e2n", "L1_gnn_W1",
        "L1_gnn_att_src1", "L1_gnn_att_dst1", "L1_gnn_b1", "L1_gnn_W2", "L1_gnn_att_src2", "L1_gnn_att_dst2",
        "L1_gnn_b2", "L2_gnn_W", "L2_gnn_b", "L2_gnn_gamma", "L2_gnn_beta", "L3_gnn_W1", "L3_gnn_a1_src",
        "L3_gnn_a1_dst", "L3_gnn_b1", "L3_gnn_ln_g", "L3_gnn_ln_b", "L3_gnn_W2", "L3_gnn_a2_src", "L3_gnn_a2_dst",
        "L3_gnn_b2"]


def kernel(**inputs):
    import numpy as _np
    import concourse.bacc as _bacc
    from concourse import mybir as _mybir
    from concourse.bass_utils import run_bass_kernel_spmd as _run

    nc = _bacc.Bacc("TRN2", target_bir_lowering=False, num_devices=1)
    arrays, aps = {}, {}
    for name in _INS:
        a = _np.ascontiguousarray(inputs[name])
        arrays[f"in_{name}_dram"] = a
        aps[name] = nc.dram_tensor(f"in_{name}_dram", a.shape, _mybir.dt.from_np(a.dtype), kind="ExternalInput").ap()
    out = nc.dram_tensor("out_0_dram", (N, D), _mybir.dt.from_np(_np.dtype("float32")), kind="ExternalOutput").ap()
    gnn_kernel(nc, aps, out)
    r = _run(nc, [arrays], core_ids=[0])
    return r.results[0]["out_0_dram"]
```

```python
from contextlib import ExitStack

import concourse.bass as bass
from concourse import mybir

F32 = mybir.dt.float32
I32 = mybir.dt.int32
ALU = mybir.AluOpType
ACT = mybir.ActivationFunctionType
AX_X = mybir.AxisListType.X

P = 128
N = 50000
E = 25000
D = 256
KC = D // P
J = 4
BLK = P * J
NREAL = -(-N // BLK)
NB = -(-NREAL // J) * J
NPAD = NB * BLK
TAILN = NREAL - 1
TAIL0 = TAILN * BLK
TAILP = (N - TAIL0) // J
NHYP = 20000
HB = NHYP // BLK + 1
HB += HB % 2
C = -(-E // P)
LASTRUN = E - (P - 1) * C
BC = 14
NBAT = C // BC
RW = 264
SW = 260
NONE = 60000
BIG = 1e30
EPS = 1e-5
SLOPE = 0.2
assert NPAD - N >= 2 * P and C == BC * NBAT and NBAT % 2 == 0 and TAILP * J + TAIL0 == N


class Step:

    def __init__(self, n, u, turn=None, slot=None):
        self.fixed = turn is None
        self.n, self.u = n, u
        self.turn = n // u if self.fixed else turn
        self.slot = n % u if self.fixed else slot

    def back(self, k):
        if self.fixed:
            return Step(self.n - k, self.u)
        return Step(self.n - k, self.u, self.turn - (k - self.slot + self.u - 1) // self.u, (self.slot - k) % self.u)

    def before(self, k):
        return self.fixed and self.n < k

    def real(self, k, blocks=None):
        return not self.fixed or 0 <= self.n - k < (blocks or NB)


def over_blocks(eng, step, blocks, lag=0, u=2, first=None, last=None):
    first = -(-(u + lag) // u) * u if first is None else first
    last = (TAILN // u) * u if last is None else last
    for n in range(first):
        step(Step(n, u))
    with eng.Fori(first // u, last // u) as i:
        for k in range(u):
            step(Step(i * u + k, u, i, k))
    for n in range(last, blocks + lag):
        step(Step(n, u))


class Chain:

    def __init__(self, eng, sem, per):
        self.eng, self.sem, self.per = eng, sem, per

    def start(self, t):
        self.base, self.k = t.n * self.per, 0

    def link(self, ins):
        ins.then_inc(self.sem, 1)
        self.k += 1

    def settle(self):
        value = self.base + self.k
        if not (isinstance(value, int) and value == 0):
            self.eng.wait_ge(self.sem, value)

    def stop(self):
        assert self.k == self.per


def take_turns(*stages):
    done = object()
    while stages:
        stages = [stage for stage in stages if next(stage, done) is not done]


def hold(eng, passed, sem, value):
    eng.wait_ge(sem, value)
    if not isinstance(value, int):
        eng.sem_inc(passed, 1)


def spread(ap, k):
    return ap.unsqueeze(len(ap.shape)).to_broadcast([*ap.shape, k])


class Scope:

    def __init__(self, nc, tag):
        self.nc, self.tag, self.ctx, self.used = nc, tag, ExitStack(), []

    def __enter__(self):
        return self

    def __exit__(self, *a):
        with self.nc.Block() as block:

            @block.sync
            def _(sp):
                for sem in self.used:
                    sp.sem_clear(sem)

        self.ctx.__exit__(*a)

    def sb(self, name, shape, dt=F32):
        return self.ctx.enter_context(self.nc.sbuf_tensor(f"{self.tag}_{name}", shape, dt))

    def ps(self, name, shape, dt=F32):
        return self.ctx.enter_context(self.nc.psum_tensor(f"{self.tag}_{name}", shape, dt))

    def sem(self, name):
        self.used.append(self.ctx.enter_context(self.nc.semaphore(f"{self.tag}_{name}")))
        return self.used[-1]

    def pool_sem(self, S, name):
        return S["scope"].ctx.enter_context(self.nc.semaphore(f"{self.tag}_{name}"))

    def sems(self, name):
        return [self.sem(f"{name}{b}") for b in range(2)]

    def block(self):
        return self.nc.Block()


def clear_rows(eng, table, zero, sem):
    rows, k = table.shape[0] // P, zero.shape[1]
    v = table.rearrange("(p r) c -> p r c", p=P)
    for r in range(0, rows, k):
        w = min(k, rows - r)
        eng.dma_start(v[:, r:r + w, :], zero[:, 0:w, :]).then_inc(sem, 16)
    return -(-rows // k)


def setup_phase(nc, S, A, T):
    with Scope(nc, "su") as s:
        dnext32 = s.sb("dnext32", [P, C], I32)
        skey32 = s.sb("skey32", [P, C], I32)
        df = s.sb("df", [P, C])
        dnextf = s.sb("dnextf", [P, C])
        t1 = s.sb("t1", [P, C])
        head = s.sb("head", [P, C])
        cnt = s.sb("cnt", [P, C])
        ones_c = s.sb("ones_c", [P, C])
        pos = s.sb("pos", [P, C], I32)
        hpos = s.sb("hpos", [P, 1], I32)
        midx = s.sb("midx", [P, C], I32)
        meta = s.sb("meta", [P, C, 2], I32)
        empty = s.sb("empty", [P, NPAD // P, 2], I32)
        diag = s.sb("diag", [P, 2, P])
        small = s.sb("small", [P, 8])
        att = s.sb("att", [P, 6, D])
        prod = s.sb("prod", [P, D])
        wraw = s.sb("wraw", [P, KC, D])
        nodeid = s.sb("nodeid", [P, NB * J], I32)
        msb = s.sb("msb", [P, NB, J * 2], I32)
        kb = s.ps("kb", [P, 2, P])
        carry = s.ps("carry", [P, 1])
        wt = s.ps("wt", [P, KC, 2, P])
        s_fill = s.sem("filled")
        s_ld = s.sem("edges_loaded")
        s_w = s.sem("weights_loaded")
        s_iota = s.sem("iotas")
        s_id = s.sem("identity")
        s_diag = s.sem("diagonals")
        s_kb = s.sem("keys_spread")
        s_m = s.sem("join_ready")
        s_car = s.sem("count_carried")
        s_meta = s.sem("meta_ready")
        s_emp = s.sem("empty_ready")
        s_pre = s.sem("meta_prefilled")
        s_sc = s.pool_sem(S, "meta_scattered")
        s_mld = s.sem("meta_loaded")
        s_wt = s.sem("w_transposed")
        s_cn = s.sem("counts_ready")
        s_zero = s.sem("zero_rows_ready")
        s_zs = s.sem("sums_zeroed")
        s_wld = s.sem("wraw_loaded")
        zero = s.sb("zero", [P, 8, SW])
        with s.block() as block:

            @block.sync
            def _(sp):
                sp.wait_ge(s_fill, 1)
                src, dst = A["src"], A["dst"]
                full = (P - 1) * C
                for tile, ap, off in ((S["src32"], src, 0), (skey32, src, 0), (S["dst32"], dst, 0), (dnext32, dst, 1)):
                    sp.dma_start(tile[0:P - 1, :], ap[off:off + full].rearrange("(p c) -> p c", c=C)).then_inc(s_ld, 16)
                    sp.dma_start(tile[P - 1:P, 0:LASTRUN - off],
                                 ap[off + full:E].rearrange("(p c) -> p c", p=1)).then_inc(s_ld, 16)
                sp.wait_ge(s_emp, 1)
                sp.dma_start(T["META"].rearrange("(p r) c -> p (r c)", p=P), empty[:].rearrange("p r c -> p (r c)")).then_inc(s_pre, 16)
                for k, (name, ap) in enumerate(S["weights"].items()):
                    sp.dma_start(S["w_" + name][:, :, 0:D], ap.rearrange("(k p) n -> p k n", p=P)).then_inc(s_w, 16)
                sp.dma_start(wraw[:], A["L2_gnn_W"].rearrange("(k p) n -> p k n", p=P)).then_inc(s_wld, 16)
                for k, name in enumerate(ATT):
                    sp.dma_start(att[:, k, :], A[name].rearrange("h c -> (h c)").partition_broadcast(P)).then_inc(s_w, 16)
                for name in ROWS:
                    sp.dma_start(S["r_" + name][:], A[name].partition_broadcast(P)).then_inc(s_w, 16)
                for name in COLS:
                    sp.dma_start(S["c_" + name][:], A[name].rearrange("(k p) -> p k", p=P),
                                 allow_slow_non_contiguous=True).then_inc(s_w, 16)
                sp.wait_ge(s_zero, 1)
                chunks = clear_rows(sp, T["NS0"], zero, s_zs)
                sp.wait_ge(s_sc, 16 * C)
                sp.dma_start(msb[:], T["META"].rearrange("(n p j) c -> p n (j c)", p=P, j=J)).then_inc(s_mld, 16)
                sp.wait_ge(s_mld, 16)
                sp.wait_ge(s_zs, 16 * chunks)

            @block.gpsimd
            def _(pool):
                pool.iota(pos[:], [[1, C]], base=0, channel_multiplier=C).then_inc(s_iota, 1)
                pool.iota(hpos[:], [[1, 1]], base=-1, channel_multiplier=C).then_inc(s_iota, 1)
                pool.iota(S["dummy32"][:], [[P, 2]], base=NPAD - 2 * P, channel_multiplier=1).then_inc(s_iota, 1)
                pool.iota(nodeid[:], [[BLK, NB], [1, J]], base=0, channel_multiplier=J).then_inc(s_iota, 1)
                pool.memset(S["ones"][:], 1.0)
                pool.memset(S["minus_half"][:], -0.5)
                pool.memset(zero[:], 0.0).then_inc(s_zero, 1)
                pool.drain()
                pool.affine_select(out=S["ident"][:], in_=S["ones"][:], compare_op=ALU.is_equal, fill=0.0, base=0,
                                   pattern=[[1, P]], channel_multiplier=-1)
                pool.affine_select(out=S["upper"][:], in_=S["ones"][:], compare_op=ALU.is_gt, fill=0.0, base=0,
                                   pattern=[[1, P]], channel_multiplier=-1)
                pool.affine_select(out=S["lower"][:], in_=S["ones"][:], compare_op=ALU.is_gt, fill=0.0, base=0,
                                   pattern=[[-1, P]], channel_multiplier=1).then_inc(s_id, 1)
                pool.wait_ge(s_meta, 1)
                pool.wait_ge(s_pre, 16)
                for c in range(C):
                    pool.indirect_dma_start(out=T["META"], out_offset=bass.IndirectOffsetOnAxis(ap=midx[:, c:c + 1], axis=0),
                                            in_=meta[:, c, :], in_offset=None, bounds_check=N - 1,
                                            oob_is_err=False).then_inc(s_sc, 16)
                pool.wait_ge(s_cn, 1)
                for k in range(0, NB * J, J * 14):
                    w = min(J * 14, NB * J - k)
                    pool.tensor_tensor(S["dinv"][:, k:k + w], S["deg"][:, k:k + w], S["minus_half"][:, 0:w], ALU.pow)

            @block.tensor
            def _(pe):
                pe.wait_ge(s_id, 1)
                pe.wait_ge(s_diag, 1)
                for k in range(2):
                    last = pe.matmul(kb[:, k, :], S["ones"][:, :], diag[:, k, :], start=True, stop=True)
                last.then_inc(s_kb, 1)
                pe.wait_ge(s_wld, 16)
                for k in range(KC):
                    for m in range(KC):
                        last = pe.transpose(wt[:, k, m, :], wraw[:, m, k * P:(k + 1) * P], S["ident"][:])
                last.then_inc(s_wt, 1)
                pe.wait_ge(s_m, 1)
                pe.matmul(carry[:], S["join"][:], cnt[:, C - 1:C], start=True, stop=True).then_inc(s_car, 1)

            @block.vector
            def _(dve):
                dve.memset(S["src32"][:], 0)
                dve.memset(skey32[:], N)
                dve.memset(S["dst32"][:], NONE)
                dve.memset(dnext32[:], NONE)
                dve.drain().then_inc(s_fill, 1)
                dve.memset(empty[:, :, 0:1], NONE)
                dve.memset(empty[:, :, 1:2], 0)
                dve.memset(ones_c[:], 1.0)
                dve.drain().then_inc(s_emp, 1)
                dve.wait_ge(s_ld, 16 * 8)
                dve.wait_ge(s_iota, 4)
                dve.tensor_copy(df[:], S["dst32"][:])
                dve.tensor_copy(dnextf[:], dnext32[:])
                dve.tensor_copy(S["skey"][:], skey32[:])
                dve.tensor_copy(S["dummy"][:], S["dummy32"][:])
                dve.memset(S["same"][:, 0:1], 0.0)
                dve.drain()
                dve.tensor_tensor(S["same"][:, 1:C], df[:, 1:C], df[:, 0:C - 1], ALU.is_equal)
                dve.tensor_scalar(head[:], df[:], df[:, 0:1], None, ALU.is_equal)
                dve.tensor_scalar(t1[:], df[:], float(NHYP - 1), None, ALU.min)
                dve.drain()
                dve.tensor_copy(S["hyp32"][:], t1[:])
                dve.tensor_scalar(S["cut"][:], S["same"][:], BIG, -BIG, ALU.mult, ALU.add)
                dve.tensor_tensor_scan(cnt[:], S["same"][:], ones_c[:], 0.0, ALU.mult, ALU.add)
                dve.tensor_reduce(small[:, 0:1], head[:], AX_X, ALU.add)
                dve.wait_ge(s_id, 1)
                dve.tensor_scalar(diag[:, 0, :], S["ident"][:], df[:, 0:1], None, ALU.mult)
                dve.tensor_scalar(diag[:, 1, :], S["ident"][:], df[:, C - 1:C], None, ALU.mult)
                dve.drain().then_inc(s_diag, 1)
                dve.wait_ge(s_kb, 1)
                dve.scalar_tensor_tensor(S["join"][:], kb[:, 0, :], df[:, C - 1:C], S["upper"][:], ALU.is_equal, ALU.mult)
                dve.scalar_tensor_tensor(S["joinT"][:], kb[:, 1, :], df[:, 0:1], S["lower"][:], ALU.is_equal, ALU.mult)
                dve.drain().then_inc(s_m, 1)
                dve.tensor_scalar(S["joincut"][:], S["joinT"][:], BIG, -BIG, ALU.mult, ALU.add)
                dve.wait_ge(s_car, 1)
                dve.tensor_copy(small[:, 1:2], carry[:])
                dve.tensor_copy(small[:, 2:3], hpos[:])
                dve.drain()
                dve.scalar_tensor_tensor(t1[:], head[:], small[:, 1:2], cnt[:], ALU.mult, ALU.add)
                dve.tensor_scalar(small[:, 3:4], small[:, 1:2], 0.0, None, ALU.is_gt)
                dve.tensor_tensor(small[:, 4:5], small[:, 0:1], small[:, 2:3], ALU.add)
                dve.tensor_copy(meta[:, :, 0:1].rearrange("p c o -> p (c o)"), pos[:])
                dve.drain()
                dve.tensor_scalar(small[:, 5:6], small[:, 4:5], float(-NONE), None, ALU.add)
                dve.tensor_copy(meta[:, :, 1:2].rearrange("p c o -> p (c o)").bitcast(F32), t1[:])
                dve.tensor_tensor(head[:], dnextf[:], df[:], ALU.not_equal)
                dve.tensor_scalar(cnt[:], df[:], float(-NONE), None, ALU.add)
                dve.drain()
                dve.tensor_tensor(small[:, 6:7], small[:, 5:6], small[:, 3:4], ALU.mult)
                dve.tensor_tensor(cnt[:], cnt[:], head[:], ALU.mult)
                dve.drain()
                dve.tensor_scalar(small[:, 7:8], small[:, 6:7], float(NONE), None, ALU.add)
                dve.tensor_scalar(cnt[:], cnt[:], float(NONE), None, ALU.add)
                dve.drain()
                dve.tensor_copy(S["repair32"][:], small[:, 7:8])
                dve.tensor_copy(midx[:], cnt[:])
                dve.drain().then_inc(s_meta, 1)
                dve.wait_ge(s_w, 16 * (len(S["weights"]) + len(ATT) + len(ROWS) + len(COLS)))
                for w, heads, a in (("L1a", 4, 0), ("L1b", 4, 2), ("L3a", 4, 4)):
                    for k in range(KC):
                        for v in range(2):
                            dve.tensor_tensor(prod[:], S["w_" + w][:, k, 0:D], att[:, a + v, :], ALU.mult)
                            dve.drain()
                            dve.tensor_reduce(S["w_" + w][:, k, D + v * heads:D + (v + 1) * heads],
                                              prod[:].rearrange("p (h c) -> p h c", h=heads), AX_X, ALU.add)
                            dve.drain()
                dve.wait_ge(s_wt, 1)
                dve.tensor_copy(S["w_L2"][:].rearrange("p k (m n) -> p k m n", m=KC), wt[:])
                dve.wait_ge(s_mld, 16)
                mv = msb[:].rearrange("p n (j c) -> p n j c", c=2)
                dve.tensor_copy(S["last32"][:].rearrange("p (n j) -> p n j", j=J), mv[:, :, :, 0])
                dve.tensor_scalar(S["deg"][:].rearrange("p (n j) -> p n j", j=J), mv[:, :, :, 1].bitcast(F32), 1.0, None, ALU.add)
                dve.tensor_scalar(S["einv"][:].rearrange("p (n j) -> p n j", j=J),
                                  mv[:, 0:HB, :, 1].bitcast(F32), 1.0, None, ALU.max)
                dve.tensor_scalar(S["has"][:].rearrange("p (n j) -> p n j", j=J), mv[:, :, :, 1].bitcast(F32), 1.0, None, ALU.min)
                dve.tensor_copy(S["loop"][:], nodeid[:])
                dve.drain().then_inc(s_cn, 1)
                dve.reciprocal(S["einv"][:], S["einv"][:])
                dve.memset(S["minus_one"][:], -1.0)
                dve.tensor_scalar(S["r1_L1_gnn_b2"][:], S["r_L1_gnn_b2"][:], 1.0, None, ALU.add)
                dve.tensor_scalar(S["loop"][:], S["loop"][:], float(NHYP), None, ALU.is_lt)
                dve.drain()
                dve.tensor_scalar(S["loopcut"][:], S["loop"][:], BIG, -BIG, ALU.mult, ALU.add)
                dve.tensor_tensor(S["einv"][:], S["einv"][:], S["has"][:, 0:HB * J], ALU.mult)


ATT = ("L1_gnn_att_src1", "L1_gnn_att_dst1", "L1_gnn_att_src2", "L1_gnn_att_dst2", "L3_gnn_a1_src", "L3_gnn_a1_dst")
ATT1 = ("L3_gnn_a2_src", "L3_gnn_a2_dst")
ROWS = ("L1_gnn_b2", "L3_gnn_b1", "L3_gnn_b2")
COLS = ("L1_gnn_b1", "L2_gnn_b", "L2_gnn_gamma", "L2_gnn_beta", "L3_gnn_ln_g", "L3_gnn_ln_b")


def last_weight_phase(nc, S, A):
    with Scope(nc, "lw") as s:
        att = s.sb("att", [P, 2, D])
        prod = s.sb("prod", [P, D])
        s_att = s.sem("att_loaded")
        with s.block() as block:

            @block.sync
            def _(sp):
                for k, name in enumerate(ATT1):
                    sp.dma_start(att[:, k, :], A[name].rearrange("h c -> (h c)").partition_broadcast(P)).then_inc(s_att, 16)

            @block.vector
            def _(dve):
                dve.wait_ge(s_att, 32)
                for k in range(KC):
                    for v in range(2):
                        dve.tensor_tensor(prod[:], S["w_L3b"][:, k, 0:D], att[:, v, :], ALU.mult)
                        dve.drain()
                        dve.tensor_reduce(S["w_L3b"][:, k, D + v:D + v + 1], prod[:], AX_X, ALU.add)
                        dve.drain()
                dve.memset(S["w_L3b"][:, :, D + 2:RW], 0.0)


def edge_phase(nc, S, tag, table, tw, acc, aw, scale=None, heads=0, ad=None):
    with Scope(nc, tag) as s:
        g = [s.sb(f"g{b}", [P, BC, tw]) for b in range(2)]
        run = [s.sb(f"run{b}", [P, BC + 1, aw]) for b in range(2)]
        st = [s.sb(f"st{b}", [P, BC], I32) for b in range(2)]
        s_st = s.sem("indices_staged")
        s_g = [s.pool_sem(S, f"rows_gathered{b}") for b in range(2)]
        s_gf = s.sem("rows_used")
        s_run = s.sem("run_ready")
        s_sv = s.sems("run_stored")
        s_ex = s.sem("exponents_ready")
        s_w = s.sem("weights_ready")
        if heads:
            std = [s.sb(f"std{b}", [P, BC], I32) for b in range(2)]
            adg = [s.sb(f"adg{b}", [P, BC, heads]) for b in range(2)]
            e = s.sb("e", [P, heads, BC])
            mx = s.sb("mx", [P, heads, BC + 1])
            ex = [s.sb(f"ex{b}", [P, 2, heads, BC]) for b in range(2)]
            wd = [s.sb(f"wd{b}", [P, 2, heads, BC]) for b in range(2)]
            s_init = s.sem("ad_cleared")
        else:
            inv = s.sb("inv", [P, BC])
        accv = acc.rearrange("(p c) w -> p c w", c=C)
        hw = D // heads if heads else D
        per = 2 if heads else 1
        with s.block() as block:

            @block.gpsimd
            def _(pool):
                if heads:
                    pool.wait_ge(s_init, 1)

                def step(t):
                    if not t.before(2):
                        hold(pool, S["passed"], s_gf, t.n - 1)
                    pool.tensor_copy(st[t.slot][:], S["src32"][:, bass.ds(t.n * BC, BC)]).then_inc(s_st, 1)
                    if heads:
                        pool.tensor_copy(std[t.slot][:], S["dst32"][:, bass.ds(t.n * BC, BC)]).then_inc(s_st, 1)
                    hold(pool, S["passed"], s_st, (t.n + 1) * per)
                    for k in range(BC):
                        pool.indirect_dma_start(out=g[t.slot][:, k, :], out_offset=None, in_=table,
                                                in_offset=bass.IndirectOffsetOnAxis(ap=st[t.slot][:, k:k + 1], axis=0),
                                                bounds_check=table.shape[0] - 1, oob_is_err=False).then_inc(s_g[t.slot], 16)
                        if heads:
                            pool.indirect_dma_start(out=adg[t.slot][:, k, :], out_offset=None, in_=ad,
                                                    in_offset=bass.IndirectOffsetOnAxis(ap=std[t.slot][:, k:k + 1], axis=0),
                                                    bounds_check=ad.shape[0] - 1, oob_is_err=False).then_inc(s_g[t.slot], 16)

                over_blocks(pool, step, NBAT, u=2, first=2, last=NBAT)

            @block.vector
            def _(dve):
                dve.memset(run[1][:], 0.0)
                if heads:
                    dve.memset(run[0][:], 0.0)
                    dve.memset(mx[:], -BIG)
                    for b in range(2):
                        dve.memset(adg[b][:], 0.0)
                    dve.drain().then_inc(s_init, 1)
                else:
                    dve.drain()

                def step(t):
                    gt, rt, ro = g[t.slot], run[t.slot], run[1 - t.slot]
                    dve.wait_ge(s_g[t.slot], (t.turn + 1) * 16 * BC * per)
                    if not t.before(2):
                        dve.wait_ge(s_sv[t.slot], t.turn * 16)
                    dve.tensor_copy(rt[:, 0, :], ro[:, BC, :])
                    if heads:
                        dve.tensor_copy(mx[:, :, 0:1], mx[:, :, BC:BC + 1])
                        dve.tensor_tensor(e[:], gt[:, :, D:D + heads].rearrange("p c h -> p h c"),
                                          adg[t.slot][:].rearrange("p c h -> p h c"), ALU.add)
                        dve.drain()
                        dve.scalar_tensor_tensor(e[:], e[:], SLOPE, e[:], ALU.mult, ALU.max)
                        dve.tensor_copy(wd_cut[:], S["cut"][:, bass.ds(t.n * BC, BC)])
                        dve.drain()
                        for h in range(heads):
                            dve.tensor_tensor_scan(mx[:, h, 1:BC + 1], wd_cut[:], e[:, h, :], mx[:, h, 0:1], ALU.add, ALU.max)
                        dve.drain()
                        dve.tensor_tensor(ex[t.slot][:, 0], e[:], mx[:, :, 1:BC + 1], ALU.subtract)
                        dve.tensor_tensor(ex[t.slot][:, 1], mx[:, :, 0:BC], mx[:, :, 1:BC + 1], ALU.subtract)
                        dve.drain()
                        for h in range(heads):
                            last = dve.tensor_tensor(ex[t.slot][:, 1, h, :], ex[t.slot][:, 1, h, :], wd_cut[:], ALU.add)
                        last.then_inc(s_ex, 1)
                        dve.wait_ge(s_w, t.n + 1)
                        w, decay = wd[t.slot][:, 0], wd[t.slot][:, 1]
                        for h in range(heads):
                            dve.tensor_tensor_scan(rt[:, 1:BC + 1, D + h], decay[:, h, :], w[:, h, :],
                                                   rt[:, 0, D + h:D + h + 1], ALU.mult, ALU.add)
                        dve.tensor_copy(rt[:, 1:BC + 1, D + heads:D + 2 * heads],
                                        mx[:, :, 1:BC + 1].rearrange("p h c -> p c h"))
                        for h in range(heads):
                            dve.tensor_tensor(gt[:, :, h * hw:(h + 1) * hw], gt[:, :, h * hw:(h + 1) * hw],
                                              spread(w[:, h, :], hw), ALU.mult)
                        dve.drain()
                        for k in range(BC):
                            for h in range(heads):
                                f = slice(h * hw, (h + 1) * hw)
                                last = dve.scalar_tensor_tensor(rt[:, k + 1, f], rt[:, k, f], decay[:, h, k:k + 1],
                                                                gt[:, k, f], ALU.mult, ALU.add)
                            last = dve.drain()
                    else:
                        dve.tensor_copy(stsame[:], S["same"][:, bass.ds(t.n * BC, BC)])
                        if scale:
                            if scale == "inverse":
                                dve.tensor_scalar(inv[:], gt[:, :, D], 1.0, None, ALU.max)
                                dve.drain()
                                dve.reciprocal(inv[:], inv[:])
                            else:
                                dve.tensor_copy(inv[:], gt[:, :, D])
                            dve.drain()
                            dve.tensor_tensor(gt[:, :, 0:D], gt[:, :, 0:D], spread(inv[:], D), ALU.mult)
                            dve.drain()
                            if scale == "inverse":
                                dve.tensor_scalar(gt[:, :, 0:D], gt[:, :, 0:D], 0.0, None, ALU.max)
                        dve.drain()
                        for k in range(BC):
                            dve.scalar_tensor_tensor(rt[:, k + 1, :], rt[:, k, :], stsame[:, k:k + 1],
                                                     gt[:, k, 0:D], ALU.mult, ALU.add)
                            last = dve.drain()
                    last.then_inc(s_run, 1)
                    dve.sem_inc(s_gf, 1)

                if heads:
                    wd_cut = s.sb("cutb", [P, BC])
                else:
                    stsame = s.sb("sameb", [P, BC])
                over_blocks(dve, step, NBAT, u=2, first=2, last=NBAT)
                dve.tensor_copy(S["tail"][:, 0:aw], run[(NBAT - 1) % 2][:, BC, :])

            @block.scalar
            def _(act):
                if heads:
                    def step(t):
                        act.wait_ge(s_ex, t.n + 1)
                        act.activation(wd[t.slot][:], ex[t.slot][:], ACT.Exp).then_inc(s_w, 1)

                    over_blocks(act, step, NBAT, u=2, first=0, last=NBAT)

            @block.sync
            def _(sp):
                def step(t):
                    sp.wait_ge(s_run, t.n + 1)
                    sp.dma_start(accv[:, bass.ds(t.n * BC, BC), :], run[t.slot][:, 1:BC + 1, :]).then_inc(s_sv[t.slot], 16)

                over_blocks(sp, step, NBAT, u=2, first=0, last=NBAT)
                for b in range(2):
                    sp.wait_ge(s_sv[b], 16 * NBAT // 2)


def repair_phase(nc, S, tag, acc, aw, heads=0):
    with Scope(nc, tag) as s:
        row = s.sb("row", [P, aw])
        car = s.sb("car", [P, D + heads])
        pc = s.ps("pc", [P, 512])
        s_r0 = s.sem("row_cleared")
        s_row = s.pool_sem(S, "row_gathered")
        s_car = s.sem("carried")
        s_fix = s.sem("row_repaired")
        s_out = s.pool_sem(S, "row_scattered")
        if heads:
            dg = s.sb("dg", [P, heads, P])
            x = s.sb("x", [P, heads, P])
            ms = s.sb("ms", [P, heads])
            mn = s.sb("mn", [P, 2, heads])
            wt = s.sb("wt", [P, 2, heads])
            xt = s.sb("xt", [P, heads, P])
            pb = s.ps("pb", [P, heads, P])
            pt = s.ps("pt", [P, heads, P])
            s_dg = s.sem("diag_ready")
            s_pb = s.sem("max_spread")
            s_x = s.sem("exponent_ready")
            s_ex = s.sem("exp_done")
            s_xm = s.sem("factors_masked")
            s_pt = s.sem("factors_turned")
            s_xt = s.sem("factors_copied")
            s_mn = s.sem("shifts_ready")
            s_wt = s.sem("shift_exp_done")
        hw = D // heads if heads else D
        with s.block() as block:

            @block.gpsimd
            def _(pool):
                pool.wait_ge(s_r0, 1)
                pool.indirect_dma_start(out=row[:, :], out_offset=None, in_=acc,
                                        in_offset=bass.IndirectOffsetOnAxis(ap=S["repair32"][:], axis=0),
                                        bounds_check=P * C - 1, oob_is_err=False).then_inc(s_row, 16)
                pool.wait_ge(s_fix, 1)
                pool.indirect_dma_start(out=acc, out_offset=bass.IndirectOffsetOnAxis(ap=S["repair32"][:], axis=0),
                                        in_=row[:, :], in_offset=None,
                                        bounds_check=P * C - 1, oob_is_err=False).then_inc(s_out, 16)
                pool.wait_ge(s_out, 16)

            @block.tensor
            def _(pe):
                if not heads:
                    pe.matmul(pc[:, 0:D], S["join"][:], S["tail"][:, 0:D], start=True, stop=True).then_inc(s_car, 1)
                    return
                pe.wait_ge(s_dg, 1)
                for h in range(heads):
                    last = pe.matmul(pb[:, h, :], S["ones"][:], dg[:, h, :], start=True, stop=True)
                last.then_inc(s_pb, 1)
                pe.wait_ge(s_xm, 1)
                for h in range(heads):
                    last = pe.transpose(pt[:, h, :], x[:, h, :], S["ident"][:])
                last.then_inc(s_pt, 1)
                pe.wait_ge(s_xt, 1)
                for h in range(heads):
                    pe.matmul(pc[:, h * hw:(h + 1) * hw], xt[:, h, :], S["tail"][:, h * hw:(h + 1) * hw], start=True, stop=True)
                    last = pe.matmul(pc[:, D + h:D + h + 1], xt[:, h, :], S["tail"][:, D + h:D + h + 1], start=True, stop=True)
                last.then_inc(s_car, 1)

            @block.vector
            def _(dve):
                dve.memset(row[:], 0.0)
                dve.drain().then_inc(s_r0, 1)
                if not heads:
                    dve.wait_ge(s_car, 1)
                    dve.wait_ge(s_row, 16)
                    dve.tensor_tensor(row[:], row[:], pc[:, 0:D], ALU.add).then_inc(s_fix, 1)
                    return
                m = S["tail"][:, D + heads:D + 2 * heads]
                for h in range(heads):
                    last = dve.tensor_scalar(dg[:, h, :], S["ident"][:], m[:, h:h + 1], None, ALU.mult)
                last.then_inc(s_dg, 1)
                dve.wait_ge(s_pb, 1)
                for h in range(heads):
                    dve.tensor_tensor(x[:, h, :], pb[:, h, :], S["joincut"][:], ALU.add)
                dve.drain()
                dve.tensor_reduce(ms[:], x[:], AX_X, ALU.max)
                dve.drain()
                dve.tensor_tensor(x[:], x[:], spread(ms[:], P), ALU.subtract).then_inc(s_x, 1)
                dve.wait_ge(s_ex, 1)
                for h in range(heads):
                    last = dve.tensor_tensor(x[:, h, :], x[:, h, :], S["joinT"][:], ALU.mult)
                last.then_inc(s_xm, 1)
                dve.wait_ge(s_pt, 1)
                dve.tensor_copy(xt[:], pt[:]).then_inc(s_xt, 1)
                dve.wait_ge(s_row, 16)
                rm = row[:, D + heads:D + 2 * heads]
                dve.tensor_tensor(car[:, D:D + heads], rm, ms[:], ALU.max)
                dve.drain()
                dve.tensor_tensor(mn[:, 0, :], rm, car[:, D:D + heads], ALU.subtract)
                dve.tensor_tensor(mn[:, 1, :], ms[:], car[:, D:D + heads], ALU.subtract).then_inc(s_mn, 1)
                dve.wait_ge(s_wt, 1)
                dve.tensor_copy(rm, car[:, D:D + heads])
                dve.wait_ge(s_car, 1)
                dve.drain()
                dve.tensor_tensor(row[:, D:D + heads], row[:, D:D + heads], wt[:, 0, :], ALU.mult)
                dve.tensor_tensor(car[:, D:D + heads], pc[:, D:D + heads], wt[:, 1, :], ALU.mult)
                for h in range(heads):
                    f = slice(h * hw, (h + 1) * hw)
                    dve.tensor_scalar(row[:, f], row[:, f], wt[:, 0, h:h + 1], None, ALU.mult)
                    dve.tensor_scalar(car[:, f], pc[:, f], wt[:, 1, h:h + 1], None, ALU.mult)
                dve.drain()
                dve.tensor_tensor(row[:, 0:D + heads], row[:, 0:D + heads], car[:, 0:D + heads], ALU.add).then_inc(s_fix, 1)

            @block.scalar
            def _(act):
                if heads:
                    act.wait_ge(s_x, 1)
                    act.activation(x[:], x[:], ACT.Exp).then_inc(s_ex, 1)
                    act.wait_ge(s_mn, 1)
                    act.activation(wt[:], mn[:], ACT.Exp).then_inc(s_wt, 1)


def hyper_phase(nc, S, tag, acc, w1, w2, out, clear=None):
    with Scope(nc, tag) as s:
        g = [s.sb(f"g{b}", [P, J, D]) for b in range(2)]
        z = [s.sb(f"z{b}", [P, J, D]) for b in range(2)]
        st = [s.sb(f"st{b}", [P, J], I32) for b in range(2)]
        zt = s.sb("zt", [P, KC, J, P])
        rt = s.sb("rt", [P, KC, J * P])
        o = [s.sb(f"o{b}", [P, J, D]) for b in range(2)]
        eb = s.sb("eb", [P, J])
        pt = s.ps("pt", [P, KC, J, P])
        pr = s.ps("pr", [P, KC, J * P])
        po = s.ps("po", [P, J, 512 // 2])
        s_st = s.sem("indices_staged")
        s_clr = s.sem("rows_cleared")
        s_g = [s.pool_sem(S, f"rows_gathered{b}") for b in range(2)]
        s_z = s.sem("z_ready")
        s_t = s.sem("z_turned")
        s_zt = s.sem("zt_copied")
        s_r = s.sem("hidden_ready")
        s_rt = s.sem("hidden_relu")
        s_m = s.sem("product_ready")
        s_o = s.sem("out_copied")
        s_sv = s.sems("out_stored")
        if clear is not None:
            zrows = clear.shape[0] // (P * HB)
            assert clear.shape[0] == P * HB * zrows
            zero = s.sb("zero", [P, zrows, SW])
            s_zero = s.sem("zero_rows_ready")
            s_zs = s.sem("rows_cleared_in_dram")
        outv = out.rearrange("(n p j) w -> n p j w", p=P, j=J)
        with s.block() as block:

            @block.gpsimd
            def _(pool):
                def step(t):
                    hold(pool, S["passed"], s_clr, t.n + 1)
                    pool.tensor_copy(st[t.slot][:], S["last32"][:, bass.ds(t.n * J, J)]).then_inc(s_st, 1)
                    hold(pool, S["passed"], s_st, t.n + 1)
                    for j in range(J):
                        pool.indirect_dma_start(out=g[t.slot][:, j, :], out_offset=None, in_=acc,
                                                in_offset=bass.IndirectOffsetOnAxis(ap=st[t.slot][:, j:j + 1], axis=0),
                                                bounds_check=P * C - 1, oob_is_err=False).then_inc(s_g[t.slot], 16)

                over_blocks(pool, step, HB, u=2, first=0, last=HB)

            @block.vector
            def _(dve):
                for b in range(2):
                    dve.memset(g[b][:], 0.0).then_inc(s_clr, 1)
                if clear is not None:
                    dve.memset(zero[:], 0.0).then_inc(s_zero, 1)

                def step(t):
                    dve.tensor_copy(eb[:], S["einv"][:, bass.ds(t.n * J, J)])
                    dve.drain()
                    if not t.before(2):
                        dve.wait_ge(s_t, t.n - 1)
                    dve.wait_ge(s_g[t.slot], (t.turn + 1) * 16 * J)
                    dve.tensor_tensor(z[t.slot][:], g[t.slot][:], spread(eb[:], D), ALU.mult).then_inc(s_z, 1)
                    dve.wait_ge(s_z, t.n + 1)
                    dve.sem_inc(s_clr, 1)

                over_blocks(dve, step, HB, u=2, first=2, last=HB)

            @block.tensor
            def _(pe):
                def turn(t):
                    pe.wait_ge(s_z, t.n + 1)
                    if not t.before(1):
                        pe.wait_ge(s_zt, t.n)
                    for k in range(KC):
                        for j in range(J):
                            last = pe.transpose(pt[:, k, j, :], z[t.slot][:, j, k * P:(k + 1) * P], S["ident"][:])
                    last.then_inc(s_t, 1)

                def hidden(t):
                    pe.wait_ge(s_zt, t.n + 1)
                    if not t.before(1):
                        pe.wait_ge(s_rt, t.n)
                    for m in range(KC):
                        for k in range(KC):
                            last = pe.matmul(pr[:, m, :], w1[:, k, m * P:(m + 1) * P],
                                             zt[:, k].rearrange("p j n -> p (j n)"), start=k == 0, stop=k == KC - 1)
                    last.then_inc(s_r, 1)

                def output(t):
                    pe.wait_ge(s_rt, t.n + 1)
                    if not t.before(1):
                        pe.wait_ge(s_o, t.n)
                    for j in range(J):
                        for k in range(KC):
                            last = pe.matmul(po[:, j, :], rt[:, k, j * P:(j + 1) * P], w2[:, k, 0:D],
                                             start=k == 0, stop=k == KC - 1)
                    last.then_inc(s_m, 1)

                def step(t):
                    if t.real(2, HB):
                        output(t.back(2))
                    if t.real(1, HB):
                        hidden(t.back(1))
                    if t.real(0, HB):
                        turn(t)

                over_blocks(pe, step, HB, 2, u=2, first=4, last=HB)

            @block.scalar
            def _(act):
                def copy_turned(t):
                    act.wait_ge(s_t, t.n + 1)
                    if not t.before(1):
                        act.wait_ge(s_r, t.n)
                    act.activation(zt[:], pt[:], ACT.Copy).then_inc(s_zt, 1)

                def relu_hidden(t):
                    act.wait_ge(s_r, t.n + 1)
                    if not t.before(1):
                        act.wait_ge(s_m, t.n)
                    act.activation(rt[:], pr[:], ACT.Relu).then_inc(s_rt, 1)

                def copy_out(t):
                    act.wait_ge(s_m, t.n + 1)
                    if not t.before(2):
                        act.wait_ge(s_sv[t.slot], t.turn * 16)
                    act.activation(o[t.slot][:], po[:], ACT.Copy).then_inc(s_o, 1)

                def step(t):
                    if t.real(2, HB):
                        copy_out(t.back(2))
                    if t.real(1, HB):
                        relu_hidden(t.back(1))
                    if t.real(0, HB):
                        copy_turned(t)

                over_blocks(act, step, HB, 2, u=2, first=4, last=HB)

            @block.sync
            def _(sp):
                if clear is not None:
                    sp.wait_ge(s_zero, 1)

                def step(t):
                    if clear is not None:
                        sp.dma_start(clear.rearrange("(p r) c -> p r c", p=P)[:, bass.ds(t.n * zrows, zrows), :],
                                     zero[:]).then_inc(s_zs, 16)
                    sp.wait_ge(s_o, t.n + 1)
                    sp.dma_start(outv[bass.ds(t.n, 1)].rearrange("n p j w -> (n p) j w"), o[t.slot][:]).then_inc(s_sv[t.slot], 16)

                over_blocks(sp, step, HB, u=2, first=0, last=HB)
                for b in range(2):
                    sp.wait_ge(s_sv[b], 16 * HB // 2)
                if clear is not None:
                    sp.wait_ge(s_zs, 16 * HB)


def source_sum_phase(nc, S, tag, table, sums):
    SB = 2 * BC
    H = SB // 2
    AHEAD = 2
    bodies = C // SB
    assert C == SB * bodies
    with Scope(nc, tag) as s:
        g = s.sb("g", [P, SB, SW])
        st = s.sb("st", [P, SB], I32)
        key = s.sb("key", [P, SB])
        dg = [s.sb(f"dg{b}", [P, 2, P]) for b in range(2)]
        eq = [s.sb(f"eq{b}", [P, 3, P]) for b in range(2)]
        junk = s.sb("junk", [P, 3, P])
        cnt = [s.sb(f"cnt{b}", [P, 3]) for b in range(2)]
        dist = [s.sb(f"dist{b}", [P, 2]) for b in range(2)]
        idx = [s.sb(f"idx{b}", [P, 2], I32) for b in range(2)]
        tot = [s.sb(f"tot{b}", [P, 2, SW]) for b in range(2)]
        pk = [s.ps(f"pk{b}", [P, 2, P]) for b in range(2)]
        pt = [s.ps(f"pt{b}", [P, 2, 512]) for b in range(2)]
        s_one = s.sem("ones_set")
        s_st = s.sem("indices_staged")
        s_key = s.sem("targets_ready")
        s_g = [s.pool_sem(S, f"pair_gathered{h}") for h in range(H)]
        s_dg = s.sem("diag_ready")
        s_pk = s.sem("keys_spread")
        s_eq = s.sem("equal_ready")
        s_tot = s.sem("total_ready")
        s_cp = s.sem("total_copied")
        s_add = s.pool_sem(S, "rows_added")
        with s.block() as block:

            @block.gpsimd
            def _(pool):
                pool.wait_ge(s_one, 1)

                def body(i, first):
                    if not first:
                        hold(pool, S["passed"], s_tot, i * H)
                    pool.tensor_copy(st[:], S["hyp32"][:, bass.ds(i * SB, SB)]).then_inc(s_st, 1)
                    hold(pool, S["passed"], s_st, i + 1)

                    def gather(h):
                        for k in (2 * h, 2 * h + 1):
                            pool.indirect_dma_start(out=g[:, k, 0:D], out_offset=None, in_=table,
                                                    in_offset=bass.IndirectOffsetOnAxis(ap=st[:, k:k + 1], axis=0),
                                                    bounds_check=table.shape[0] - 1, oob_is_err=False).then_inc(s_g[h], 16)

                    for h in range(AHEAD):
                        gather(h)
                    for h in range(H):
                        if h + AHEAD < H:
                            gather(h + AHEAD)
                        hold(pool, S["passed"], s_cp, i * H + h + 1)
                        if not (first and h == 0):
                            hold(pool, S["passed"], s_add, (i * H + h) * 32)
                        for k in range(2):
                            pool.indirect_dma_start(out=sums, out_offset=bass.IndirectOffsetOnAxis(ap=idx[h % 2][:, k:k + 1], axis=0),
                                                    in_=tot[h % 2][:, k, :], in_offset=None, bounds_check=sums.shape[0] - 1,
                                                    compute_op=ALU.add).then_inc(s_add, 16)

                body(0, True)
                with pool.Fori(1, bodies) as i:
                    body(i, False)
                pool.wait_ge(s_add, 16 * C)

            @block.vector
            def _(dve):
                dve.memset(g[:], 1.0)
                dve.drain().then_inc(s_one, 1)

                def body(i, first):
                    if not first:
                        dve.wait_ge(s_pk, i * H)
                    dve.tensor_copy(key[:], S["skey"][:, bass.ds(i * SB, SB)])
                    dve.drain()

                    def diagonals(h):
                        if h >= 2:
                            dve.wait_ge(s_pk, i * H + h - 1)
                        for k in range(2):
                            last = dve.tensor_scalar(dg[h % 2][:, k, :], S["ident"][:], key[:, 2 * h + k:2 * h + k + 1], None, ALU.mult)
                        last.then_inc(s_dg, 1)

                    diagonals(0)
                    for h in range(H):
                        if h + 1 < H:
                            diagonals(h + 1)
                        b = h % 2
                        mine = key[:, 2 * h:2 * h + 2]
                        dve.wait_ge(s_pk, i * H + h + 1)
                        if not (first and h < 2):
                            dve.wait_ge(s_tot, i * H + h - 1)
                            dve.wait_ge(s_add, (i * H + h - 1) * 32)
                        for k, (spread_tile, own) in enumerate(((0, 0), (1, 1), (0, 1))):
                            last = dve.tensor_scalar(eq[b][:, k, :], pk[b][:, spread_tile, :], mine[:, own:own + 1], None, ALU.is_equal)
                        last.then_inc(s_eq, 1)
                        dve.tensor_tensor(dist[b][:], S["dummy"][:], mine, ALU.subtract)
                        dve.drain()
                        for k, mask in enumerate(("lower", "lower", "ones")):
                            dve.tensor_tensor_reduce(junk[:, k, :], eq[b][:, k, :], S[mask][:], 1.0, 0.0, ALU.mult, ALU.add,
                                                     cnt[b][:, k:k + 1])
                        dve.drain()
                        dve.tensor_tensor(cnt[b][:, 1:2], cnt[b][:, 1:2], cnt[b][:, 2:3], ALU.add)
                        dve.drain()
                        dve.scalar_tensor_tensor(dist[b][:], cnt[b][:, 0:2], 1.0, dist[b][:], ALU.min, ALU.mult)
                        dve.drain()
                        dve.tensor_tensor(dist[b][:], dist[b][:], mine, ALU.add)
                        dve.drain()
                        dve.tensor_copy(idx[b][:], dist[b][:]).then_inc(s_key, 1)

                body(0, True)
                with dve.Fori(1, bodies) as i:
                    body(i, False)

            @block.tensor
            def _(pe):
                def body(i, first):
                    def keys(h):
                        pe.wait_ge(s_dg, i * H + h + 1)
                        if not (first and h < 2):
                            pe.wait_ge(s_eq, i * H + h - 1)
                        pe.matmul(pk[h % 2][:].rearrange("p k n -> p (k n)"), S["ones"][:],
                                  dg[h % 2][:].rearrange("p k n -> p (k n)"), start=True, stop=True).then_inc(s_pk, 1)

                    keys(0)
                    for h in range(H):
                        if h + 1 < H:
                            keys(h + 1)
                        b = h % 2
                        pe.wait_ge(s_eq, i * H + h + 1)
                        pe.wait_ge(s_g[h], (i + 1) * 32)
                        if not (first and h < 2):
                            pe.wait_ge(s_cp, i * H + h - 1)
                        pe.matmul(pt[b][:, 0, 0:SW], eq[b][:, 0, :], g[:, 2 * h, :], start=True, stop=False)
                        pe.matmul(pt[b][:, 0, 0:SW], eq[b][:, 2, :], g[:, 2 * h + 1, :], start=False, stop=True)
                        pe.matmul(pt[b][:, 1, 0:SW], eq[b][:, 1, :], g[:, 2 * h + 1, :], start=True, stop=True).then_inc(s_tot, 1)

                body(0, True)
                with pe.Fori(1, bodies) as i:
                    body(i, False)

            @block.scalar
            def _(act):
                def body(i, first):
                    for h in range(H):
                        act.wait_ge(s_tot, i * H + h + 1)
                        if not (first and h < 2):
                            act.wait_ge(s_add, (i * H + h - 1) * 32)
                        act.wait_ge(s_key, i * H + h + 1)
                        act.activation(tot[h % 2][:], pt[h % 2][:, :, 0:SW], ACT.Copy).then_inc(s_cp, 1)

                body(0, True)
                with act.Fori(1, bodies) as i:
                    body(i, False)


def node_phase(nc, S, tag, kind, rows, rw, extra=None, ew=D, gather=None, gw=0, heads=0, bias=None, elu="",
               loops=False, norm=False, relu=None, save=None, sw=D, weight=None, oheads=0, out=None, ad=None,
               out_bias=None, final=False):
    gcn, bn, gat, total = kind == "gcn", kind == "bn", kind == "gat", kind == "sum"
    turned = elu == "turned"
    U = (6 if loops or turned else 5) if gat else 4
    hw = D // heads if heads else D
    b_lag = 3 if gat else 0
    c_lag = {"gat": b_lag + (2 if elu else 1), "bn": 2, "sum": 1}.get(kind, 0)
    z_lag = c_lag + 1 if norm else b_lag
    m_lag = c_lag if turned else z_lag + 1
    o_lag = m_lag + 1 if turned else m_lag
    r_lag = max(c_lag - 1, 0)
    act_norm = norm and not bn and relu is None
    with Scope(nc, tag) as s:
        bufs = lambda name, shape, dt=F32: [s.sb(f"{name}{b}", shape, dt) for b in range(U)]
        sems = lambda name: [s.sem(f"{name}{b}") for b in range(U)]
        a = bufs("a", [P, J, rw])
        s_in = sems("rows_loaded")
        s_used = s.sem("rows_used")
        s_rin = sems("residual_loaded")
        s_rused = s.sem("residual_used")
        s_z = s.sem("z_ready")
        s_zs = sems("z_stored")
        s_t = s.sem("z_turned")
        s_zt = s.sem("zt_ready")
        s_m = s.sem("product_ready")
        s_o = s.sem("out_copied")
        s_os = sems("out_stored")
        s_ex = s.sem("exponents_ready")
        s_wt = s.sem("weights_ready")
        s_nw = s.sem("weights_normalized")
        s_v = s.sem("self_part_ready")
        s_st = s.sem("indices_staged")
        s_clr = s.sem("gathered_cleared")
        s_g = [s.pool_sem(S, f"runs_gathered{b}") for b in range(U)]
        s_var = s.sem("variance_ready")
        s_rs = s.sem("rstd_ready")
        s_nb = s.sem("norm_shift_ready")
        s_y = s.sem("bn_ready")
        s_yt = s.sem("bn_turned")
        s_bs = s.sem("turned_read")
        s_en = s.sem("elu_input_ready")
        s_ee = s.sem("elu_exp_done")
        s_a, s_n, s_b, s_c = s.sem("logit_steps"), s.sem("weight_steps"), s.sem("sum_steps"), s.sem("c_steps")
        nin = 2 if bn else 1
        if extra is not None:
            r = bufs("r", [P, J, ew])
        if gather is not None:
            g = bufs("g", [P, J, gw])
            st = bufs("st", [P, J], I32)
        if gat:
            e = s.sb("e", [P, J, heads])
            mm = s.sb("mm", [P, J, heads])
            den = s.sb("den", [P, J, heads])
            ex = bufs("ex", [P, 2, J, heads])
            wt = bufs("wt", [P, 2, J, heads])
            if loops:
                lp = bufs("lp", [P, J])
        u = bufs("u", [P, J, D]) if norm or elu else None
        if elu:
            ee = bufs("ee", [P, J * D])
        if norm:
            bs = s.sb("bs", [P, J, 6])
            mv = bufs("mv", [P, J, 2])
            ve = bufs("ve", [P, J])
            rs = bufs("rs", [P, J])
            if act_norm:
                nm = bufs("nm", [P, J])
                nb = bufs("nb", [P, J])
        if norm or gcn:
            z = bufs("z", [P, J, sw])
        else:
            z = u
        if total or gcn:
            scs = bufs("sc", [P, 2, J])
        if weight is not None:
            zts = [s.sb(f"zt{b}", [P, KC, J, P]) for b in range(2)]
            TURNS = 1 if bn else 2
            pts = [s.ps(f"pt{b}", [P, KC, J, P]) for b in range(TURNS)]
            if gcn:
                o = bufs("o", [P, KC, J * P])
                pm = s.ps("pm", [P, KC, J * P])
                stats = s.sb("stats", [P, KC, NB, 6])
                bmv = s.sb("bmv", [P, KC, 2])
                bt = s.sb("bt", [P, KC, 2])
                s_fin = s.sem("batch_variance")
                s_frs = s.sem("batch_rstd")
            else:
                o = bufs("o", [P, J, RW])
                ao = bufs("ao", [P, J, oheads])
                pm = s.ps("pm", [P, J, 512])
                wc = D + 2 * oheads
        if bn:
            yt = bufs("yt", [P, KC, J * P])
            yr = bufs("yr", [P, KC, J, P])
            py = s.ps("py", [P, J, KC, P])
        per_o = 1 if gcn else 2
        padded = rows.shape[0] == NPAD
        tailrows = lambda t: t[TAIL0:N, :].rearrange("(p j) w -> p j w", j=J)
        blockof = lambda t, n: t[bass.ds(n * BLK, BLK), :].rearrange("(p j) w -> p j w", j=J)
        by_head = lambda x: x[:, :, 0:D].rearrange("p j (h c) -> p j h c", h=heads)
        is_tail = lambda t: t.fixed and t.n == TAILN
        is_padding = lambda t: t.fixed and t.n > TAILN

        with s.block() as block:

            @block.sync
            def _(sp):
                sp.wait_ge(s_clr, 1)

                def load(t):
                    if not t.before(U):
                        hold(sp, S["passed"], s_used, t.n - U + 1)
                    if is_tail(t) and not padded:
                        sp.dma_start(a[t.slot][0:TAILP, :, :], tailrows(rows)).then_inc(s_in[t.slot], 16)
                    elif is_padding(t) and not padded:
                        sp.dma_start(a[t.slot][0:TAILP, :, :], tailrows(rows)).then_inc(s_in[t.slot], 16)
                    else:
                        sp.dma_start(a[t.slot][:], blockof(rows, t.n)).then_inc(s_in[t.slot], 16)
                    if bn:
                        sp.dma_start(yt[t.slot][:], S["AGG"][:, :, bass.ds(t.n * BLK, BLK)]).then_inc(s_in[t.slot], 16)

                def load_residual(t):
                    if not t.before(U):
                        hold(sp, S["passed"], s_rused, t.n - U + 1)
                    sp.dma_start(r[t.slot][:], blockof(extra, t.n)).then_inc(s_rin[t.slot], 16)

                def store_z(t):
                    hold(sp, S["passed"], s_z, t.n + 1)
                    if final and is_tail(t):
                        sp.dma_start(tailrows(save), z[t.slot][0:TAILP, :, :]).then_inc(s_zs[t.slot], 16)
                    elif not (final and is_padding(t)):
                        sp.dma_start(blockof(save, t.n), z[t.slot][:]).then_inc(s_zs[t.slot], 16)

                def store_out(t):
                    hold(sp, S["passed"], s_o, t.n + 1)
                    if gcn:
                        sp.dma_start(S["AGG"][:, :, bass.ds(t.n * BLK, BLK)], o[t.slot][:]).then_inc(s_os[t.slot], 16)
                    else:
                        sp.dma_start(blockof(out, t.n), o[t.slot][:]).then_inc(s_os[t.slot], 16)
                        sp.dma_start(blockof(ad, t.n), ao[t.slot][:]).then_inc(s_os[t.slot], 16)

                def step(t):
                    if t.real(0):
                        load(t)
                    if extra is not None and t.real(r_lag):
                        load_residual(t.back(r_lag))
                    if save is not None and t.real(z_lag + 1):
                        store_z(t.back(z_lag + 1))
                    if weight is not None and t.real(o_lag + 1):
                        store_out(t.back(o_lag + 1))

                over_blocks(sp, step, NB, (o_lag if weight is not None else z_lag) + 1, u=U)
                for b in range(U):
                    if save is not None:
                        sp.wait_ge(s_zs[b], 16 * len(range(b, NREAL if final else NB, U)))
                    if weight is not None:
                        sp.wait_ge(s_os[b], 16 * per_o * len(range(b, NB, U)))

            @block.gpsimd
            def _(pool):
                def gathers(t):
                    hold(pool, S["passed"], s_clr, t.n + 1)
                    pool.tensor_copy(st[t.slot][:], S["last32"][:, bass.ds(t.n * J, J)]).then_inc(s_st, 1)
                    hold(pool, S["passed"], s_st, t.n + 1)
                    for j in range(J):
                        pool.indirect_dma_start(out=g[t.slot][:, j, :], out_offset=None, in_=gather,
                                                in_offset=bass.IndirectOffsetOnAxis(ap=st[t.slot][:, j:j + 1], axis=0),
                                                bounds_check=P * C - 1, oob_is_err=False).then_inc(s_g[t.slot], 16)

                def rstd(t):
                    hold(pool, S["passed"], s_var, t.n + 1)
                    pool.tensor_tensor(rs[t.slot][:], ve[t.slot][:], S["minus_half"][:, 0:J], ALU.pow).then_inc(s_rs, 1)
                    if act_norm:
                        hold(pool, S["passed"], s_rs, t.n + 1)
                        pool.tensor_tensor(nb[t.slot][:], nm[t.slot][:], rs[t.slot][:], ALU.mult).then_inc(s_nb, 1)

                def step(t):
                    if gather is not None and t.real(0):
                        gathers(t)
                    if norm and t.real(rs_lag):
                        rstd(t.back(rs_lag))

                rs_lag = z_lag + 1 if gather is not None else z_lag
                if gather is not None or norm:
                    over_blocks(pool, step, NB, rs_lag if norm else 0, u=U)
                if gcn:
                    pool.wait_ge(s_fin, 1)
                    pool.tensor_tensor(bt[:, :, 0], bmv[:, :, 1], S["minus_half"][:, 0:KC], ALU.pow).then_inc(s_frs, 1)

            @block.tensor
            def _(pe):
                def turn_bn(t):
                    pe.wait_ge(s_y, t.n + 1)
                    if not t.before(1):
                        pe.wait_ge(s_bs, t.n)
                    for j in range(J):
                        for k in range(KC):
                            last = pe.transpose(py[:, j, k, :], yr[t.slot][:, k, j, :], S["ident"][:])
                    last.then_inc(s_yt, 1)

                def turn(t):
                    pt = pts[t.slot % TURNS]
                    pe.wait_ge(s_z, t.n + 1)
                    if not t.before(TURNS):
                        pe.wait_ge(s_zt, t.n - TURNS + 1)
                    for k in range(KC):
                        for j in range(J):
                            last = pe.transpose(pt[:, k, j, :], z[t.slot][:, j, k * P:(k + 1) * P], S["ident"][:])
                    last.then_inc(s_t, 1)

                def product(t):
                    zt = zts[t.slot % 2]
                    pe.wait_ge(s_zt, t.n + 1)
                    if not t.before(1):
                        pe.wait_ge(s_o, t.n)
                    if gcn:
                        for m in range(KC):
                            for k in range(KC):
                                last = pe.matmul(pm[:, m, :], weight[:, k, m * P:(m + 1) * P],
                                                 zt[:, k].rearrange("p j n -> p (j n)"), start=k == 0, stop=k == KC - 1)
                    else:
                        for j in range(J):
                            for k in range(KC):
                                last = pe.matmul(pm[:, j, 0:wc], zt[:, k, j, :], weight[:, k, 0:wc],
                                                 start=k == 0, stop=k == KC - 1)
                    last.then_inc(s_m, 1)

                def step(t):
                    if bn and t.real(1):
                        turn_bn(t.back(1))
                    if turned and t.real(z_lag):
                        turn(t.back(z_lag))
                    if t.real(m_lag):
                        product(t.back(m_lag))
                    if not turned and t.real(z_lag):
                        turn(t.back(z_lag))

                if weight is not None:
                    over_blocks(pe, step, NB, m_lag, u=U)

            @block.scalar
            def _(act):
                def normalize_bn(t):
                    act.wait_ge(s_in[t.slot], (t.turn + 1) * 16 * nin)
                    if not t.before(U):
                        act.wait_ge(s_yt, t.n - U + 1)
                    for k in range(KC):
                        last = act.activation(yr[t.slot][:, k].rearrange("p j n -> p (j n)"), yt[t.slot][:, k, :],
                                              ACT.Relu, bias=S["bnshift"][:, k:k + 1], scale=S["bnscale"][:, k:k + 1])
                    last.then_inc(s_y, 1)

                def exp_weights(t):
                    act.wait_ge(s_ex, t.n + 1)
                    act.activation(wt[t.slot][:], ex[t.slot][:], ACT.Exp).then_inc(s_wt, 1)

                def self_part(t):
                    act.wait_ge(s_nw, t.n + 1)
                    for j in range(J):
                        for h in range(heads):
                            f = slice(h * hw, (h + 1) * hw)
                            last = act.activation(a[t.slot][:, j, f], a[t.slot][:, j, f], ACT.Copy,
                                                  scale=wt[t.slot][:, 0, j, h:h + 1])
                    last.then_inc(s_v, 1)

                def exp_elu(t):
                    if turned:
                        act.wait_ge(s_t, t.n + 1)
                        pt = pts[t.slot % TURNS]
                        for k in range(KC):
                            last = act.activation(ee[t.slot][:, k * J * P:(k + 1) * J * P],
                                                  pt[:, k].rearrange("p j n -> p (j n)"), ACT.Exp, bias=bias[:, k:k + 1])
                    else:
                        act.wait_ge(s_en, t.n + 1)
                        last = act.activation(ee[t.slot][:], u[t.slot][:].rearrange("p j d -> p (j d)"), ACT.Exp,
                                              bias=S["minus_one"][:])
                    last.then_inc(s_ee, 1)

                def copy_turned(t):
                    pt, zt = pts[t.slot % TURNS], zts[t.slot % 2]
                    act.wait_ge(s_t, t.n + 1)
                    if not t.before(2):
                        act.wait_ge(s_m, t.n - 1)
                    if relu is None:
                        last = act.activation(zt[:], pt[:], ACT.Copy)
                    else:
                        for k in range(KC):
                            last = act.activation(zt[:, k], pt[:, k], ACT.Relu, bias=relu[1][:, k:k + 1],
                                                  scale=relu[0][:, k:k + 1])
                    last.then_inc(s_zt, 1)

                def copy_out(t):
                    act.wait_ge(s_m, t.n + 1)
                    if not t.before(U):
                        act.wait_ge(s_os[t.slot], t.turn * 16 * per_o)
                    if gcn:
                        if not t.before(U):
                            act.wait_ge(s_bs, t.n - U + 1)
                        for m in range(KC):
                            last = act.activation(o[t.slot][:, m, :], pm[:, m, :], ACT.Identity, bias=S["c_L2_gnn_b"][:, m:m + 1])
                    else:
                        act.activation(o[t.slot][:, :, 0:wc], pm[:, :, 0:wc], ACT.Copy)
                        last = act.activation(ao[t.slot][:], pm[:, :, D + oheads:D + 2 * oheads], ACT.Copy)
                    last.then_inc(s_o, 1)

                def normalize(t):
                    act.wait_ge(s_nb, t.n + 1)
                    if not t.before(U):
                        if save is not None:
                            act.wait_ge(s_zs[t.slot], t.turn * 16)
                        if weight is not None:
                            act.wait_ge(s_t, t.n - U + 1)
                    if sw > D:
                        act.activation(z[t.slot][:, :, D], S["dinv"][:, bass.ds(t.n * J, J)], ACT.Copy)
                    for j in range(J):
                        last = act.activation(z[t.slot][:, j, 0:D], u[t.slot][:, j, :], ACT.Identity,
                                              bias=nb[t.slot][:, j:j + 1], scale=rs[t.slot][:, j:j + 1])
                    last.then_inc(s_z, 1)

                def step(t):
                    if weight is not None and not turned and t.real(m_lag):
                        copy_turned(t.back(m_lag))
                    if elu and t.real(b_lag + 1):
                        exp_elu(t.back(b_lag + 1))
                    if bn and t.real(0):
                        normalize_bn(t)
                    if gat and t.real(0):
                        exp_weights(t)
                    if act_norm and t.real(z_lag):
                        normalize(t.back(z_lag))
                    if gat and t.real(1):
                        self_part(t.back(1))
                    if weight is not None and out_bias is None and t.real(o_lag):
                        copy_out(t.back(o_lag))

                act.wait_ge(s_clr, 1)
                over_blocks(act, step, NB, o_lag if weight is not None else max(c_lag, z_lag), u=U)

            @block.vector
            def _(dve):
                for b in range(U):
                    if weight is not None and not gcn and wc < RW:
                        dve.memset(o[b][:], 0.0)
                    if not padded:
                        dve.memset(a[b][:], 0.0)
                    if sw > D:
                        dve.memset(z[b][:], 0.0)
                    if gather is not None:
                        dve.memset(g[b][:], 0.0)
                dve.drain()

                def clear(b):
                    if gat:
                        dve.memset(g[b][:, :, D + heads:D + 2 * heads], -BIG).then_inc(s_clr, 1)
                    else:
                        dve.sem_inc(s_clr, 1)

                for b in range(U):
                    clear(b)
                logit = Chain(dve, s_a, 5 if loops else 3)
                share = Chain(dve, s_n, 3)
                summed = Chain(dve, s_b, {"sum": 3, "gcn": 2 + J}.get(kind, J if heads == 1 else 1 if turned or bias is None else 2))
                third = Chain(dve, s_c, 1 if turned else 2 * J + (2 if elu else 1 if bn or (gat and extra is not None) else 0))

                def logits(t):
                    at, gt = a[t.slot], g[t.slot]
                    gm = gt[:, :, D + heads:D + 2 * heads]
                    dve.wait_ge(s_in[t.slot], (t.turn + 1) * 16 * nin)
                    logit.start(t)
                    if loops:
                        logit.link(dve.tensor_copy(lp[t.slot][:], S["loopcut"][:, bass.ds(t.n * J, J)]))
                    logit.link(dve.tensor_tensor(e[:], at[:, :, D:D + heads], at[:, :, D + heads:D + 2 * heads], ALU.add))
                    yield
                    logit.settle()
                    logit.link(dve.scalar_tensor_tensor(e[:], e[:], SLOPE, e[:], ALU.mult, ALU.max))
                    yield
                    logit.settle()
                    if loops:
                        logit.link(dve.tensor_tensor(e[:], e[:], spread(lp[t.slot][:], heads), ALU.add))
                        yield
                        logit.settle()
                    dve.wait_ge(s_g[t.slot], (t.turn + 1) * 16 * J)
                    logit.link(dve.scalar_tensor_tensor(mm[:], e[:], -BIG / 2, gm, ALU.max, ALU.max))
                    yield
                    logit.settle()
                    dve.tensor_tensor(ex[t.slot][:, 0], e[:], mm[:], ALU.subtract)
                    dve.tensor_tensor(ex[t.slot][:, 1], gm, mm[:], ALU.subtract).then_inc(s_ex, 1)
                    logit.stop()

                def shares(t):
                    w = wt[t.slot]
                    dve.wait_ge(s_wt, t.n + 1)
                    share.start(t)
                    share.link(dve.tensor_tensor(den[:], g[t.slot][:, :, D:D + heads], w[:, 1], ALU.mult))
                    yield
                    share.settle()
                    share.link(dve.scalar_tensor_tensor(den[:], den[:], 1e-30, w[:, 0], ALU.max, ALU.add))
                    yield
                    share.settle()
                    share.link(dve.reciprocal(den[:], den[:]))
                    yield
                    share.settle()
                    dve.tensor_tensor(w[:, 0], w[:, 0], den[:], ALU.mult)
                    dve.tensor_tensor(w[:, 1], w[:, 1], den[:], ALU.mult).then_inc(s_nw, 1)
                    share.stop()

                def sum_up(t):
                    at = a[t.slot]
                    if not gat:
                        dve.wait_ge(s_in[t.slot], (t.turn + 1) * 16 * nin)
                    summed.start(t)
                    if gat:
                        ut, gt = u[t.slot], g[t.slot]
                        if turned and not t.before(U):
                            dve.wait_ge(s_t, t.n - U + 1)
                        if act_norm and not t.before(U):
                            dve.wait_ge(s_z, t.n - U + 1)
                        dve.wait_ge(s_nw, t.n + 1)
                        if heads == 1:
                            dve.wait_ge(s_v, t.n + 1)
                            for j in range(J):
                                summed.link(dve.scalar_tensor_tensor(ut[:, j, :], gt[:, j, 0:D], wt[t.slot][:, 1, j, 0:1],
                                                                     a[t.slot][:, j, 0:D], ALU.mult, ALU.add))
                        else:
                            summed.link(dve.tensor_tensor(by_head(ut), by_head(gt), spread(wt[t.slot][:, 1], hw), ALU.mult))
                            dve.wait_ge(s_v, t.n + 1)
                            yield
                            summed.settle()
                        if turned or bias is None:
                            dve.tensor_tensor(ut[:], ut[:], at[:, :, 0:D], ALU.add).then_inc(s_z if turned else s_en, 1)
                        else:
                            if heads > 1:
                                summed.link(dve.tensor_tensor(ut[:], ut[:], at[:, :, 0:D], ALU.add))
                            yield
                            summed.settle()
                            dve.tensor_tensor(ut[:], ut[:], bias[:].unsqueeze(1).to_broadcast([P, J, D]), ALU.add).then_inc(s_en, 1)
                        dve.memset(gt[:, :, D + heads:D + 2 * heads], -BIG).then_inc(s_clr, 1)
                        dve.wait_ge(s_clr, t.n + U + 1)
                        dve.sem_inc(s_used, 1)
                    elif total:
                        rt, ut, sc = r[t.slot], u[t.slot], scs[t.slot]
                        if not t.before(U):
                            dve.wait_ge(s_z, t.n - U + 1)
                        dve.wait_ge(s_rin[t.slot], (t.turn + 1) * 16)
                        summed.link(dve.tensor_scalar(sc[:, 0, :], rt[:, :, D], 1.0, None, ALU.max))
                        yield
                        summed.settle()
                        summed.link(dve.reciprocal(sc[:, 0, :], sc[:, 0, :]))
                        yield
                        summed.settle()
                        summed.link(dve.tensor_tensor(ut[:], rt[:, :, 0:D], spread(sc[:, 0, :], D), ALU.mult))
                        yield
                        summed.settle()
                        dve.tensor_tensor(ut[:], ut[:], at[:, :, 0:D], ALU.add).then_inc(s_en, 1)
                        dve.wait_ge(s_en, t.n + 1)
                        dve.sem_inc(s_used, 1)
                        dve.sem_inc(s_rused, 1)
                    elif gcn:
                        zz, sc = z[t.slot], scs[t.slot]
                        dve.wait_ge(s_g[t.slot], (t.turn + 1) * 16 * J)
                        if not t.before(U):
                            dve.wait_ge(s_t, t.n - U + 1)
                        dve.tensor_copy(sc[:, 0, :], S["dinv"][:, bass.ds(t.n * J, J)])
                        summed.link(dve.tensor_copy(sc[:, 1, :], S["has"][:, bass.ds(t.n * J, J)]))
                        yield
                        summed.settle()
                        summed.link(dve.tensor_tensor(zz[:], at[:, :, 0:D], spread(sc[:, 0, :], D), ALU.mult))
                        yield
                        summed.settle()
                        for j in range(J):
                            summed.link(dve.scalar_tensor_tensor(zz[:, j, :], g[t.slot][:, j, :], sc[:, 1, j:j + 1],
                                                                 zz[:, j, :], ALU.mult, ALU.add))
                        yield
                        summed.settle()
                        dve.tensor_tensor(zz[:], zz[:], spread(sc[:, 0, :], D), ALU.mult).then_inc(s_z, 1)
                        dve.sem_inc(s_used, 1)
                        dve.sem_inc(s_clr, 1)
                    summed.stop()

                def stage_c(t):
                    third.start(t)
                    if turned:
                        dve.wait_ge(s_ee, t.n + 1)
                        pt, zt = pts[t.slot % TURNS], zts[t.slot % 2]
                        if not t.before(2):
                            dve.wait_ge(s_m, t.n - 1)
                        third.link(dve.tensor_scalar(ee[t.slot][:], ee[t.slot][:], 1.0, -1.0, ALU.min, ALU.add))
                        yield
                        third.settle()
                        for k in range(KC):
                            last = dve.scalar_tensor_tensor(zt[:, k].rearrange("p j n -> p (j n)"),
                                                            pt[:, k].rearrange("p j n -> p (j n)"), bias[:, k:k + 1],
                                                            ee[t.slot][:, k * J * P:(k + 1) * J * P], ALU.add, ALU.max)
                        last.then_inc(s_zt, 1)
                        third.stop()
                        return
                    ut = u[t.slot]
                    if elu:
                        dve.wait_ge(s_ee, t.n + 1)
                        third.link(dve.scalar_tensor_tensor(ut[:].rearrange("p j d -> p (j d)"), ee[t.slot][:], 1.0,
                                                            ut[:].rearrange("p j d -> p (j d)"), ALU.min, ALU.max))
                        yield
                        third.settle()
                        dve.wait_ge(s_rin[t.slot], (t.turn + 1) * 16)
                        third.link(dve.scalar_tensor_tensor(ut[:], ut[:], -1.0, r[t.slot][:], ALU.add, ALU.add))
                    elif bn:
                        dve.wait_ge(s_yt, t.n + 1)
                        third.link(dve.tensor_tensor(ut[:], a[t.slot][:, :, 0:D], py[:].rearrange("p j k n -> p j (k n)"), ALU.add))
                        yield
                        third.settle()
                        dve.sem_inc(s_bs, 1)
                        dve.sem_inc(s_used, 1)
                    elif gat and extra is not None:
                        dve.wait_ge(s_rin[t.slot], (t.turn + 1) * 16)
                        dve.wait_ge(s_en, t.n + 1)
                        third.link(dve.tensor_tensor(ut[:], ut[:], r[t.slot][:], ALU.add))
                    else:
                        dve.wait_ge(s_en, t.n + 1)
                    yield
                    third.settle()
                    if extra is not None and gat:
                        dve.sem_inc(s_rused, 1)
                    for j in range(J):
                        third.link(dve.bn_stats(bs[:, j, :], ut[:, j, :]))
                    yield
                    third.settle()
                    dve.sem_inc(S["passed"], 1)
                    for j in range(J):
                        third.link(dve.bn_aggr(mv[t.slot][:, j, :], bs[:, j, :]))
                    yield
                    third.settle()
                    if act_norm:
                        dve.tensor_scalar(nm[t.slot][:], mv[t.slot][:, :, 0], -1.0, None, ALU.mult)
                    last = dve.tensor_scalar(ve[t.slot][:], mv[t.slot][:, :, 1], EPS, None, ALU.add)
                    last.then_inc(s_var, 1)
                    third.stop()

                def normalize(t):
                    ut, zz = u[t.slot], z[t.slot]
                    dve.wait_ge(s_rs, t.n + 1)
                    if not t.before(U):
                        if save is not None:
                            dve.wait_ge(s_zs[t.slot], t.turn * 16)
                        if weight is not None:
                            dve.wait_ge(s_t, t.n - U + 1)
                    if sw > D:
                        dve.tensor_copy(zz[:, :, D], S["dinv"][:, bass.ds(t.n * J, J)])
                    for j in range(J):
                        last = dve.tensor_scalar(zz[:, j, 0:D], ut[:, j, :], mv[t.slot][:, j, 0:1], rs[t.slot][:, j:j + 1],
                                                 ALU.subtract, ALU.mult)
                    last.then_inc(s_z, 1)
                    yield

                def copy_out(t):
                    dve.wait_ge(s_m, t.n + 1)
                    if not t.before(U):
                        dve.wait_ge(s_os[t.slot], t.turn * 16 * per_o)
                    dve.tensor_tensor(o[t.slot][:, :, 0:D], pm[:, :, 0:D], out_bias[:].unsqueeze(1).to_broadcast([P, J, D]), ALU.add)
                    dve.tensor_copy(o[t.slot][:, :, D:wc], pm[:, :, D:wc])
                    dve.tensor_copy(ao[t.slot][:], pm[:, :, D + oheads:D + 2 * oheads]).then_inc(s_o, 1)
                    yield

                def batch_stats(t):
                    dve.wait_ge(s_o, t.n + 1)
                    for m in range(KC):
                        if is_padding(t):
                            continue
                        if is_tail(t):
                            last = dve.bn_stats(stats[:, m, t.n, :], o[t.slot][:, m, :].rearrange("p (j n) -> p j n", n=P)[:, :, 0:TAILP])
                        else:
                            last = dve.bn_stats(stats[:, m, bass.ds(t.n, 1), :].rearrange("p n s -> p (n s)"), o[t.slot][:, m, :])
                    last = dve.drain() if is_padding(t) else last
                    last.then_inc(s_bs, 1)
                    yield

                def step(t):
                    parts = []
                    if not gcn and t.real(c_lag):
                        parts.append(stage_c(t.back(c_lag)))
                    if not bn and t.real(b_lag):
                        parts.append(sum_up(t.back(b_lag)))
                    if gat and t.real(1):
                        parts.append(shares(t.back(1)))
                    if gat and t.real(0):
                        parts.append(logits(t))
                    if norm and not act_norm and t.real(z_lag):
                        parts.append(normalize(t.back(z_lag)))
                    take_turns(*parts)
                    if out_bias is not None and t.real(o_lag):
                        take_turns(copy_out(t.back(o_lag)))
                    if gcn and t.real(m_lag + 1):
                        take_turns(batch_stats(t.back(m_lag + 1)))

                over_blocks(dve, step, NB, max(z_lag, c_lag, m_lag + 1 if gcn else 0, o_lag if out_bias is not None else 0), u=U)
                if gcn:
                    dve.drain()
                    for m in range(KC):
                        dve.bn_aggr(bmv[:, m, :], stats[:, m, 0:NREAL].rearrange("p n s -> p (n s)"))
                    dve.drain()
                    dve.tensor_scalar(bmv[:, :, 1], bmv[:, :, 1], EPS, None, ALU.add).then_inc(s_fin, 1)
                    dve.wait_ge(s_frs, 1)
                    dve.tensor_tensor(S["bnscale"][:], bt[:, :, 0], S["c_L2_gnn_gamma"][:], ALU.mult)
                    dve.drain()
                    dve.tensor_tensor(bt[:, :, 1], bmv[:, :, 0], S["bnscale"][:], ALU.mult)
                    dve.drain()
                    dve.tensor_tensor(S["bnshift"][:], S["c_L2_gnn_beta"][:], bt[:, :, 1], ALU.subtract)


def gnn_kernel(nc, A, out):
    T = {
        "META": nc.dram_tensor("META", (NPAD, 2), I32).ap(),
        "NS0": nc.dram_tensor("NS0", (NPAD, SW), F32).ap(),
        "NS1": nc.dram_tensor("NS1", (NPAD, SW), F32).ap(),
        "HYP": nc.dram_tensor("HYP", (HB * BLK, D), F32).ap(),
        "SUMS": nc.dram_tensor("SUMS", (P * C, D), F32).ap(),
        "GSUMS": nc.dram_tensor("GSUMS", (P * C, RW), F32).ap(),
        "X1": nc.dram_tensor("X1", (NPAD, D), F32).ap(),
        "X2": nc.dram_tensor("X2", (NPAD, SW), F32).ap(),
        "X3": nc.dram_tensor("X3", (NPAD, D), F32).ap(),
        "HA": nc.dram_tensor("HA", (NPAD, RW), F32).ap(),
        "HBT": nc.dram_tensor("HBT", (NPAD, RW), F32).ap(),
        "AD": nc.dram_tensor("AD", (NPAD, 4), F32).ap(),
        "AD1": nc.dram_tensor("AD1", (NPAD, 1), F32).ap(),
        "AGG": nc.dram_tensor("AGG", (P, KC, NPAD), F32).ap(),
    }
    with Scope(nc, "k") as s:
        S = {"AGG": T["AGG"], "passed": s.sem("passed"),
             "scope": s}
        for name, shape, dt in (
            ("src32", [P, C], I32), ("dst32", [P, C], I32), ("hyp32", [P, C], I32), ("skey", [P, C], F32),
            ("same", [P, C], F32), ("cut", [P, C], F32), ("repair32", [P, 1], I32), ("dummy32", [P, 2], I32),
            ("dummy", [P, 2], F32), ("last32", [P, NB * J], I32), ("deg", [P, NB * J], F32), ("dinv", [P, NB * J], F32),
            ("einv", [P, HB * J], F32), ("has", [P, NB * J], F32), ("minus_one", [P, 1], F32), ("r1_L1_gnn_b2", [P, D], F32), ("loop", [P, NB * J], F32), ("loopcut", [P, NB * J], F32),
            ("ident", [P, P], F32), ("ones", [P, P], F32), ("upper", [P, P], F32), ("lower", [P, P], F32),
            ("join", [P, P], F32), ("joinT", [P, P], F32), ("joincut", [P, P], F32), ("minus_half", [P, 64], F32),
            ("tail", [P, RW], F32), ("bnscale", [P, KC], F32), ("bnshift", [P, KC], F32), ("w_L2", [P, KC, D], F32),
        ):
            S[name] = s.sb(name, shape, dt)
        S["weights"] = {"n2e0": A["L0_gnn_W0_n2e"], "e2n0": A["L0_gnn_W0_e2n"], "n2e1": A["L0_gnn_W1_n2e"],
                        "e2n1": A["L0_gnn_W1_e2n"], "L1a": A["L1_gnn_W1"], "L1b": A["L1_gnn_W2"],
                        "L3a": A["L3_gnn_W1"], "L3b": A["L3_gnn_W2"]}
        for name in S["weights"]:
            S["w_" + name] = s.sb("w_" + name, [P, KC, RW])
        for name in ROWS:
            S["r_" + name] = s.sb("r_" + name, [P, D])
        for name in COLS:
            S["c_" + name] = s.sb("c_" + name, [P, KC])

        setup_phase(nc, S, A, T)
        last_weight_phase(nc, S, A)
        edge_phase(nc, S, "e0", A["x"], D, T["SUMS"], D)
        repair_phase(nc, S, "f0", T["SUMS"], D)
        hyper_phase(nc, S, "h0", T["SUMS"], S["w_n2e0"], S["w_e2n0"], T["HYP"], clear=T["NS1"])
        source_sum_phase(nc, S, "s0", T["HYP"], T["NS0"])
        edge_phase(nc, S, "e1", T["NS0"], SW, T["SUMS"], D, scale="inverse")
        repair_phase(nc, S, "f1", T["SUMS"], D)
        hyper_phase(nc, S, "h1", T["SUMS"], S["w_n2e1"], S["w_e2n1"], T["HYP"])
        source_sum_phase(nc, S, "s1", T["HYP"], T["NS1"])
        node_phase(nc, S, "n0", "sum", A["x"], D, extra=T["NS1"], ew=SW, norm=True, save=T["X1"],
                   weight=S["w_L1a"], oheads=4, out=T["HA"], ad=T["AD"])
        edge_phase(nc, S, "e2", T["HA"], RW, T["GSUMS"], RW, heads=4, ad=T["AD"])
        repair_phase(nc, S, "f2", T["GSUMS"], RW, heads=4)
        node_phase(nc, S, "n1", "gat", T["HA"], RW, gather=T["GSUMS"], gw=RW, heads=4, bias=S["c_L1_gnn_b1"],
                   elu="turned", weight=S["w_L1b"], oheads=4, out=T["HBT"], ad=T["AD"], out_bias=S["r1_L1_gnn_b2"])
        edge_phase(nc, S, "e3", T["HBT"], RW, T["GSUMS"], RW, heads=4, ad=T["AD"])
        repair_phase(nc, S, "f3", T["GSUMS"], RW, heads=4)
        node_phase(nc, S, "n2", "gat", T["HBT"], RW, extra=T["X1"], gather=T["GSUMS"], gw=RW, heads=4,
                   elu="rows", norm=True, save=T["X2"], sw=SW)
        edge_phase(nc, S, "e4", T["X2"], SW, T["SUMS"], D, scale="plain")
        repair_phase(nc, S, "f4", T["SUMS"], D)
        node_phase(nc, S, "n3", "gcn", T["X2"], SW, gather=T["SUMS"], gw=D, weight=S["w_L2"])
        node_phase(nc, S, "n4", "bn", T["X2"], SW, norm=True, save=T["X3"], weight=S["w_L3a"], oheads=4,
                   out=T["HA"], ad=T["AD"])
        edge_phase(nc, S, "e5", T["HA"], RW, T["GSUMS"], RW, heads=4, ad=T["AD"])
        repair_phase(nc, S, "f5", T["GSUMS"], RW, heads=4)
        node_phase(nc, S, "n5", "gat", T["HA"], RW, gather=T["GSUMS"], gw=RW, heads=4, bias=S["r_L3_gnn_b1"],
                   loops=True, norm=True, relu=(S["c_L3_gnn_ln_g"], S["c_L3_gnn_ln_b"]), weight=S["w_L3b"],
                   oheads=1, out=T["HBT"], ad=T["AD1"])
        edge_phase(nc, S, "e6", T["HBT"], RW, T["GSUMS"], RW, heads=1, ad=T["AD1"])
        repair_phase(nc, S, "f6", T["GSUMS"], RW, heads=1)
        node_phase(nc, S, "n6", "gat", T["HBT"], RW, extra=T["X3"], gather=T["GSUMS"], gw=RW, heads=1,
                   bias=S["r_L3_gnn_b2"], loops=True, norm=True, save=out, final=True)


_INS = ["x", "src", "dst", "L0_gnn_W0_n2e", "L0_gnn_W0_e2n", "L0_gnn_W1_n2e", "L0_gnn_W1_e2n", "L1_gnn_W1",
        "L1_gnn_att_src1", "L1_gnn_att_dst1", "L1_gnn_b1", "L1_gnn_W2", "L1_gnn_att_src2", "L1_gnn_att_dst2",
        "L1_gnn_b2", "L2_gnn_W", "L2_gnn_b", "L2_gnn_gamma", "L2_gnn_beta", "L3_gnn_W1", "L3_gnn_a1_src",
        "L3_gnn_a1_dst", "L3_gnn_b1", "L3_gnn_ln_g", "L3_gnn_ln_b", "L3_gnn_W2", "L3_gnn_a2_src", "L3_gnn_a2_dst",
        "L3_gnn_b2"]


def kernel(**inputs):
    import numpy as _np
    import concourse.bacc as _bacc
    from concourse import mybir as _mybir
    from concourse.bass_utils import run_bass_kernel_spmd as _run

    nc = _bacc.Bacc("TRN2", target_bir_lowering=False, num_devices=1)
    arrays, aps = {}, {}
    for name in _INS:
        a = _np.ascontiguousarray(inputs[name])
        arrays[f"in_{name}_dram"] = a
        aps[name] = nc.dram_tensor(f"in_{name}_dram", a.shape, _mybir.dt.from_np(a.dtype), kind="ExternalInput").ap()
    out = nc.dram_tensor("out_0_dram", (N, D), _mybir.dt.from_np(_np.dtype("float32")), kind="ExternalOutput").ap()
    gnn_kernel(nc, aps, out)
    r = _run(nc, [arrays], core_ids=[0])
    return r.results[0]["out_0_dram"]
```
